# Optimizing a Trainium2 kernel written in Bass

```python
import numpy as np
import jax
import jax.numpy as jnp

def _softmax(x, axis=-1):
    return jax.nn.softmax(x, axis=axis)

def _gelu(x):
    return jax.nn.gelu(x, approximate=True)

def _silu(x):
    return jax.nn.silu(x)

def _sigmoid(x):
    return jax.nn.sigmoid(x)

def _layernorm(x, axis=-1, eps=1e-05):
    m = jnp.mean(x, axis=axis, keepdims=True)
    v = jnp.var(x, axis=axis, keepdims=True)
    return (x - m) / jnp.sqrt(v + eps)

def _scatter_add(tgt, idx, src, axis=0):
    return tgt.at[idx].add(src)

def _segment_sum(src, seg, n):
    return jax.ops.segment_sum(src, seg, n)
kernel_name = 'mk_flamingo_gated_d4_seqx_r4_33885d'

def setup_inputs(seed: int=0):
    np.random.seed(seed)
    _w = jnp.asarray

    def _rec_inputs():
        import jax
        import jax.numpy as jnp
        _rk = jax.random.key(seed)
        x = -0.0002928 + 1 * jax.random.normal(jax.random.fold_in(_rk, 1), (2, 1024, 256), jnp.float32)
        _lenS = 1024 - jax.random.randint(jax.random.fold_in(_rk, 7), (2,), 0, max(1, 1024 // 4) + 1, jnp.int32)
        _lenS2 = 154 - jax.random.randint(jax.random.fold_in(_rk, 8), (2,), 0, max(1, 154 // 4) + 1, jnp.int32)
        _ctx_1024P = jax.random.normal(jax.random.fold_in(_rk, 11), (2, 16, 256), jnp.float32)
        _ctx_1024c = jax.random.dirichlet(jax.random.fold_in(_rk, 511), 0.3 * jnp.ones((16,), jnp.float32), (2, 154))
        _ctx_1024t = jnp.einsum('bsk,bkd->bsd', _ctx_1024c, _ctx_1024P)
        _ctx_1024t = _ctx_1024t * jax.lax.rsqrt(jnp.mean(jnp.square(_ctx_1024t)) + 1e-12) * 0.953939
        ctx_1024 = -1.39393e-06 + 0.999914 * (_ctx_1024t + 0.3 * jax.random.normal(jax.random.fold_in(_rk, 611), (2, 154, 256), jnp.float32))
        _validS = jnp.arange(1024)[None, :] < _lenS[:, None]
        _validS2 = jnp.arange(154)[None, :] < _lenS2[:, None]
        _causal = jnp.tril(jnp.ones((1024, 1024), dtype=bool))
        mask_BxS2_bf1 = jnp.ones((2, 154), dtype=bool)
        _g = jax.random.normal(jax.random.fold_in(_rk, 9001), (2, 4), jnp.float32)
        _g = jnp.sign(_g) * jnp.maximum(jnp.abs(_g), 1.0) + (_g == 0) * 1.0
        g_xattn = _g[0]
        g_ffn = _g[1]
        return (x, ctx_1024, mask_BxS2_bf1, g_xattn, g_ffn)
    x, ctx_1024, mask_BxS2_bf1, g_xattn, g_ffn = _rec_inputs()

    def _L0_xattn_setup():
        import jax, jax.numpy as jnp
        import numpy as np
        DIM = 256
        H = 16
        D = DIM // H
        SCALE = D ** (-0.5)
        LN_EPS = 1e-05

        def _layernorm(t, gamma, beta):
            mu = jnp.mean(t, axis=-1, keepdims=True)
            var = jnp.var(t, axis=-1, keepdims=True)
            return (t - mu) * jax.lax.rsqrt(var + LN_EPS) * gamma + beta
        key = jax.random.key(seed)
        ks = jax.random.split(key, 8)
        s = DIM ** (-0.5)
        return {'x': jax.random.normal(ks[0], (2, 512, DIM), dtype=jnp.float32), 'y': jax.random.normal(ks[1], (2, 512, DIM), dtype=jnp.float32), 'Wq': jax.random.normal(ks[2], (DIM, DIM), dtype=jnp.float32) * s, 'bq': jnp.zeros((DIM,), dtype=jnp.float32), 'Wkv': jax.random.normal(ks[3], (2 * DIM, DIM), dtype=jnp.float32) * s, 'bkv': jnp.zeros((2 * DIM,), dtype=jnp.float32), 'q_gamma': jnp.ones((D,), dtype=jnp.float32), 'q_beta': jnp.zeros((D,), dtype=jnp.float32), 'k_gamma': jnp.ones((D,), dtype=jnp.float32), 'k_beta': jnp.zeros((D,), dtype=jnp.float32), 'Wproj': jax.random.normal(ks[4], (DIM, DIM), dtype=jnp.float32) * s, 'bproj': jnp.zeros((DIM,), dtype=jnp.float32)}
    _L0_xattn_all = _L0_xattn_setup()
    _L0_xattn_in = {k: v for k, v in _L0_xattn_all.items() if k in ('Wq', 'bq', 'Wkv', 'bkv', 'q_gamma', 'q_beta', 'k_gamma', 'k_beta', 'Wproj', 'bproj')}
    del _L0_xattn_all

    def _L0_ffn_setup():
        import jax, jax.numpy as jnp
        import numpy as np
        HIDDEN = 256
        N_ROUTED = 16
        N_SHARED = 2
        TOP_K = 2
        MID_R = HIDDEN // 4
        MID_S = HIDDEN // 2
        key = jax.random.key(seed)
        ks = jax.random.split(key, 8)
        s = 0.02
        return {'x': jax.random.normal(ks[0], (2, 256, HIDDEN), dtype=jnp.float32), 'router_w': jax.random.normal(ks[1], (HIDDEN, N_ROUTED), dtype=jnp.float32) * s, 'wg_r': jax.random.normal(ks[2], (N_ROUTED, HIDDEN, MID_R), dtype=jnp.float32) * s, 'wu_r': jax.random.normal(ks[3], (N_ROUTED, HIDDEN, MID_R), dtype=jnp.float32) * s, 'wd_r': jax.random.normal(ks[4], (N_ROUTED, MID_R, HIDDEN), dtype=jnp.float32) * s, 'wg_s': jax.random.normal(ks[5], (N_SHARED, HIDDEN, MID_S), dtype=jnp.float32) * s, 'wu_s': jax.random.normal(ks[6], (N_SHARED, HIDDEN, MID_S), dtype=jnp.float32) * s, 'wd_s': jax.random.normal(ks[7], (N_SHARED, MID_S, HIDDEN), dtype=jnp.float32) * s}
    _L0_ffn_all = _L0_ffn_setup()
    _L0_ffn_in = {k: v for k, v in _L0_ffn_all.items() if k in ('router_w', 'wg_r', 'wu_r', 'wd_r', 'wg_s', 'wu_s', 'wd_s')}
    del _L0_ffn_all

    def _L1_xattn_setup():
        import jax, jax.numpy as jnp
        import numpy as np
        D = 256
        NUM_ITERS = 3
        EPS = 1e-06
        SCALE = D ** (-0.5)

        def rmsnorm(x, w, eps=EPS):
            return x * jax.lax.rsqrt(jnp.mean(x * x, axis=-1, keepdims=True) + eps) * w

        def gru_cell(x, h, wih, whh, bih, bhh):
            gx = x @ wih.T + bih
            gh = h @ whh.T + bhh
            xr, xz, xn = jnp.split(gx, 3, axis=-1)
            hr, hz, hn = jnp.split(gh, 3, axis=-1)
            r = jax.nn.sigmoid(xr + hr)
            z = jax.nn.sigmoid(xz + hz)
            n = jnp.tanh(xn + r * hn)
            return (1.0 - z) * n + z * h
        key = jax.random.key(seed)
        ks = jax.random.split(key, 8)
        B, K, M, d = (8, 64, 1024, D)
        w_std = d ** (-0.5)
        return {'slots': jax.random.normal(ks[0], (B, K, d), jnp.float32), 'P': jax.random.normal(ks[1], (B, M, d), jnp.float32), 'Wq': jax.random.normal(ks[2], (d, d), jnp.float32) * w_std, 'Wk': jax.random.normal(ks[3], (d, d), jnp.float32) * w_std, 'Wv': jax.random.normal(ks[4], (d, d), jnp.float32) * w_std, 'gru_wih': jax.random.normal(ks[5], (3 * d, d), jnp.float32) * w_std, 'gru_whh': jax.random.normal(ks[6], (3 * d, d), jnp.float32) * w_std, 'gru_bih': jnp.zeros((3 * d,), jnp.float32), 'gru_bhh': jnp.zeros((3 * d,), jnp.float32), 'slot_norm_w': jnp.ones((d,), jnp.float32), 'input_norm_w': jnp.ones((d,), jnp.float32)}
    _L1_xattn_all = _L1_xattn_setup()
    _L1_xattn_in = {k: v for k, v in _L1_xattn_all.items() if k in ('Wq', 'Wk', 'Wv', 'gru_wih', 'gru_whh', 'gru_bih', 'gru_bhh', 'slot_norm_w', 'input_norm_w')}
    del _L1_xattn_all

    def _L1_ffn_setup():
        import jax, jax.numpy as jnp
        import numpy as np
        HIDDEN = 256
        INTER = 1024
        NUM_EXPERTS = 8
        TOP_K = 2
        EPS = 1e-05

        def _layer_norm(x, g, b):
            m = jnp.mean(x, axis=-1, keepdims=True)
            v = jnp.mean(jnp.square(x - m), axis=-1, keepdims=True)
            return (x - m) * jax.lax.rsqrt(v + EPS) * g + b
        key = jax.random.key(seed)
        ks = jax.random.split(key, 8)
        s = 0.02
        return {'x': jax.random.normal(ks[0], (4, 512, HIDDEN), dtype=jnp.float32), 'ln1_g': jnp.ones((HIDDEN,), jnp.float32), 'ln1_b': jnp.zeros((HIDDEN,), jnp.float32), 'attn_w': jax.random.normal(ks[1], (HIDDEN, HIDDEN), jnp.float32) * s, 'ln2_g': jnp.ones((HIDDEN,), jnp.float32), 'ln2_b': jnp.zeros((HIDDEN,), jnp.float32), 'gate_w': jax.random.normal(ks[2], (NUM_EXPERTS, HIDDEN), jnp.float32) * s, 'gate_proj': jax.random.normal(ks[3], (NUM_EXPERTS, INTER, HIDDEN), jnp.float32) * s, 'up_proj': jax.random.normal(ks[4], (NUM_EXPERTS, INTER, HIDDEN), jnp.float32) * s, 'down_proj': jax.random.normal(ks[5], (NUM_EXPERTS, HIDDEN, INTER), jnp.float32) * s}
    _L1_ffn_all = _L1_ffn_setup()
    _L1_ffn_in = {k: v for k, v in _L1_ffn_all.items() if k in ('ln1_g', 'ln1_b', 'attn_w', 'ln2_g', 'ln2_b', 'gate_w', 'gate_proj', 'up_proj', 'down_proj')}
    del _L1_ffn_all

    def _L2_xattn_setup():
        import jax, jax.numpy as jnp
        import numpy as np
        HEADS = 16
        DIM_HEAD = 64
        SCALE = DIM_HEAD ** (-0.5)
        key = jax.random.key(seed)
        ks = jax.random.split(key, 6)
        B, Nq, Nkv, D = (4, 512, 256, 256)
        inner = HEADS * DIM_HEAD
        return {'x': jax.random.normal(ks[0], (B, Nq, D), dtype=jnp.float32), 'context': jax.random.normal(ks[1], (B, Nkv, D), dtype=jnp.float32), 'mask': jnp.ones((B, Nkv), dtype=bool), 'Wq': jax.random.normal(ks[2], (inner, D), dtype=jnp.float32) * D ** (-0.5), 'Wkv': jax.random.normal(ks[3], (2 * inner, D), dtype=jnp.float32) * D ** (-0.5), 'Wout': jax.random.normal(ks[4], (D, inner), dtype=jnp.float32) * inner ** (-0.5), 'b_out': jnp.zeros((D,), dtype=jnp.float32)}
    _L2_xattn_all = _L2_xattn_setup()
    _L2_xattn_in = {k: v for k, v in _L2_xattn_all.items() if k in ('Wq', 'Wkv', 'Wout', 'b_out')}
    del _L2_xattn_all

    def _L2_ffn_setup():
        import jax, jax.numpy as jnp
        import numpy as np
        NQ, NK, H, DH = (256, 128, 8, 64)
        key = jax.random.key(seed)
        ks = jax.random.split(key, 8)
        b, n, d, g = (4, 1024, 256, 4)
        di = H * DH
        s = lambda fan: 1.0 / np.sqrt(fan)
        return {'x': jax.random.normal(ks[0], (b, n, d), jnp.float32), 'w_qr': jax.random.normal(ks[1], (g, d), jnp.float32) * s(d), 'w_kvr': jax.random.normal(ks[2], (g, d), jnp.float32) * s(d), 'w_q': jax.random.normal(ks[3], (g, di, d), jnp.float32) * s(d), 'w_kv': jax.random.normal(ks[4], (g, 2 * di, d), jnp.float32) * s(d), 'w_out': jax.random.normal(ks[5], (g, d, di), jnp.float32) * s(di), 'null_kv': jax.random.normal(ks[6], (2, g, H, 1, DH), jnp.float32), 'null_token': jax.random.normal(ks[7], (1, 1, d), jnp.float32)}
    _L2_ffn_all = _L2_ffn_setup()
    _L2_ffn_in = {k: v for k, v in _L2_ffn_all.items() if k in ('w_qr', 'w_kvr', 'w_q', 'w_kv', 'w_out', 'null_kv', 'null_token')}
    del _L2_ffn_all

    def _L3_xattn_setup():
        import jax, jax.numpy as jnp
        import numpy as np
        D_MODEL = 256
        B, S = (4, 1024)
        key = jax.random.key(seed)
        kq, kk, kv = jax.random.split(key, 3)
        query = jax.random.normal(kq, (B, S, D_MODEL), dtype=jnp.float32)
        key_t = jax.random.normal(kk, (B, S, D_MODEL), dtype=jnp.float32)
        value = jax.random.normal(kv, (B, S, D_MODEL), dtype=jnp.float32)
        return {'query': query, 'key': key_t, 'value': value}
    _L3_xattn_all = _L3_xattn_setup()
    _L3_xattn_in = {k: v for k, v in _L3_xattn_all.items() if k in ()}
    del _L3_xattn_all

    def _L3_ffn_setup():
        import jax, jax.numpy as jnp
        import numpy as np
        QMAX = 127.0

        def _ste_round(v):
            return v + jax.lax.stop_gradient(jnp.round(v) - v)

        def _act_fake_quant(x, clip_factor):
            scale = jax.nn.sigmoid(clip_factor) * jnp.max(jnp.abs(x)) / QMAX
            return jnp.clip(_ste_round(x / scale), -QMAX - 1.0, QMAX) * scale

        def _weight_fake_quant(w):
            scale = jnp.max(jnp.abs(w), axis=1, keepdims=True) / QMAX
            return jnp.clip(_ste_round(w / scale), -QMAX - 1.0, QMAX) * scale
        key = jax.random.key(seed)
        k1, k2, k3, k4 = jax.random.split(key, 4)
        B, S, H, I = (8, 2048, 256, 704)
        return {'x': jax.random.normal(k1, (B, S, H), dtype=jnp.float32), 'clip_x': jnp.full((1,), 4.0, dtype=jnp.float32), 'clip_down': jnp.full((1,), 4.0, dtype=jnp.float32), 'w_gate': jax.random.normal(k2, (I, H), dtype=jnp.float32) * 0.02, 'w_up': jax.random.normal(k3, (I, H), dtype=jnp.float32) * 0.02, 'w_down': jax.random.normal(k4, (H, I), dtype=jnp.float32) * 0.02}
    _L3_ffn_all = _L3_ffn_setup()
    _L3_ffn_in = {k: v for k, v in _L3_ffn_all.items() if k in ('clip_x', 'clip_down', 'w_gate', 'w_up', 'w_down')}
    del _L3_ffn_all
    return {'x': x, 'ctx_1024': ctx_1024, 'mask_BxS2_bf1': mask_BxS2_bf1, 'g_xattn': g_xattn, 'g_ffn': g_ffn, 'L0_xattn_Wq': _L0_xattn_in['Wq'], 'L0_xattn_bq': _L0_xattn_in['bq'], 'L0_xattn_Wkv': _L0_xattn_in['Wkv'], 'L0_xattn_bkv': _L0_xattn_in['bkv'], 'L0_xattn_q_gamma': _L0_xattn_in['q_gamma'], 'L0_xattn_q_beta': _L0_xattn_in['q_beta'], 'L0_xattn_k_gamma': _L0_xattn_in['k_gamma'], 'L0_xattn_k_beta': _L0_xattn_in['k_beta'], 'L0_xattn_Wproj': _L0_xattn_in['Wproj'], 'L0_xattn_bproj': _L0_xattn_in['bproj'], 'L0_ffn_router_w': _L0_ffn_in['router_w'], 'L0_ffn_wg_r': _L0_ffn_in['wg_r'], 'L0_ffn_wu_r': _L0_ffn_in['wu_r'], 'L0_ffn_wd_r': _L0_ffn_in['wd_r'], 'L0_ffn_wg_s': _L0_ffn_in['wg_s'], 'L0_ffn_wu_s': _L0_ffn_in['wu_s'], 'L0_ffn_wd_s': _L0_ffn_in['wd_s'], 'L1_xattn_Wq': _L1_xattn_in['Wq'], 'L1_xattn_Wk': _L1_xattn_in['Wk'], 'L1_xattn_Wv': _L1_xattn_in['Wv'], 'L1_xattn_gru_wih': _L1_xattn_in['gru_wih'], 'L1_xattn_gru_whh': _L1_xattn_in['gru_whh'], 'L1_xattn_gru_bih': _L1_xattn_in['gru_bih'], 'L1_xattn_gru_bhh': _L1_xattn_in['gru_bhh'], 'L1_xattn_slot_norm_w': _L1_xattn_in['slot_norm_w'], 'L1_xattn_input_norm_w': _L1_xattn_in['input_norm_w'], 'L1_ffn_ln1_g': _L1_ffn_in['ln1_g'], 'L1_ffn_ln1_b': _L1_ffn_in['ln1_b'], 'L1_ffn_attn_w': _L1_ffn_in['attn_w'], 'L1_ffn_ln2_g': _L1_ffn_in['ln2_g'], 'L1_ffn_ln2_b': _L1_ffn_in['ln2_b'], 'L1_ffn_gate_w': _L1_ffn_in['gate_w'], 'L1_ffn_gate_proj': _L1_ffn_in['gate_proj'], 'L1_ffn_up_proj': _L1_ffn_in['up_proj'], 'L1_ffn_down_proj': _L1_ffn_in['down_proj'], 'L2_xattn_Wq': _L2_xattn_in['Wq'], 'L2_xattn_Wkv': _L2_xattn_in['Wkv'], 'L2_xattn_Wout': _L2_xattn_in['Wout'], 'L2_xattn_b_out': _L2_xattn_in['b_out'], 'L2_ffn_w_qr': _L2_ffn_in['w_qr'], 'L2_ffn_w_kvr': _L2_ffn_in['w_kvr'], 'L2_ffn_w_q': _L2_ffn_in['w_q'], 'L2_ffn_w_kv': _L2_ffn_in['w_kv'], 'L2_ffn_w_out': _L2_ffn_in['w_out'], 'L2_ffn_null_kv': _L2_ffn_in['null_kv'], 'L2_ffn_null_token': _L2_ffn_in['null_token'], 'L3_ffn_clip_x': _L3_ffn_in['clip_x'], 'L3_ffn_clip_down': _L3_ffn_in['clip_down'], 'L3_ffn_w_gate': _L3_ffn_in['w_gate'], 'L3_ffn_w_up': _L3_ffn_in['w_up'], 'L3_ffn_w_down': _L3_ffn_in['w_down']}

def reference(x, ctx_1024, mask_BxS2_bf1, g_xattn, g_ffn, L0_xattn_Wq, L0_xattn_bq, L0_xattn_Wkv, L0_xattn_bkv, L0_xattn_q_gamma, L0_xattn_q_beta, L0_xattn_k_gamma, L0_xattn_k_beta, L0_xattn_Wproj, L0_xattn_bproj, L0_ffn_router_w, L0_ffn_wg_r, L0_ffn_wu_r, L0_ffn_wd_r, L0_ffn_wg_s, L0_ffn_wu_s, L0_ffn_wd_s, L1_xattn_Wq, L1_xattn_Wk, L1_xattn_Wv, L1_xattn_gru_wih, L1_xattn_gru_whh, L1_xattn_gru_bih, L1_xattn_gru_bhh, L1_xattn_slot_norm_w, L1_xattn_input_norm_w, L1_ffn_ln1_g, L1_ffn_ln1_b, L1_ffn_attn_w, L1_ffn_ln2_g, L1_ffn_ln2_b, L1_ffn_gate_w, L1_ffn_gate_proj, L1_ffn_up_proj, L1_ffn_down_proj, L2_xattn_Wq, L2_xattn_Wkv, L2_xattn_Wout, L2_xattn_b_out, L2_ffn_w_qr, L2_ffn_w_kvr, L2_ffn_w_q, L2_ffn_w_kv, L2_ffn_w_out, L2_ffn_null_kv, L2_ffn_null_token, L3_ffn_clip_x, L3_ffn_clip_down, L3_ffn_w_gate, L3_ffn_w_up, L3_ffn_w_down):
    import jax
    import jax.numpy as jnp

    def _L0_xattn_ref(x, y, Wq, bq, Wkv, bkv, q_gamma, q_beta, k_gamma, k_beta, Wproj, bproj):
        import jax, jax.numpy as jnp
        import numpy as np
        DIM = 256
        H = 16
        D = DIM // H
        SCALE = D ** (-0.5)
        LN_EPS = 1e-05

        def _layernorm(t, gamma, beta):
            mu = jnp.mean(t, axis=-1, keepdims=True)
            var = jnp.var(t, axis=-1, keepdims=True)
            return (t - mu) * jax.lax.rsqrt(var + LN_EPS) * gamma + beta
        B, N, C = x.shape
        M = y.shape[1]
        q = (x @ Wq.T + bq).reshape(B, N, H, D).transpose(0, 2, 1, 3)
        kv = (y @ Wkv.T + bkv).reshape(B, M, 2, H, D).transpose(2, 0, 3, 1, 4)
        k, v = (kv[0], kv[1])
        q = _layernorm(q, q_gamma, q_beta) * SCALE
        k = _layernorm(k, k_gamma, k_beta)
        attn = jax.nn.softmax(jnp.einsum('bhnd,bhmd->bhnm', q, k), axis=-1)
        out = jnp.einsum('bhnm,bhmd->bhnd', attn, v)
        out = out.transpose(0, 2, 1, 3).reshape(B, N, C)
        return out @ Wproj.T + bproj

    def _L0_ffn_ref(x, router_w, wg_r, wu_r, wd_r, wg_s, wu_s, wd_s):
        import jax, jax.numpy as jnp
        import numpy as np
        HIDDEN = 256
        N_ROUTED = 16
        N_SHARED = 2
        TOP_K = 2
        MID_R = HIDDEN // 4
        MID_S = HIDDEN // 2
        orig_shape = x.shape
        flat = x.reshape(-1, orig_shape[-1])
        gs = jnp.einsum('td,ndm->tnm', flat, wg_s)
        us = jnp.einsum('td,ndm->tnm', flat, wu_s)
        out = jnp.einsum('tnm,nmd->td', jax.nn.silu(gs) * us, wd_s)
        logits = (flat @ router_w).astype(jnp.float32)
        probs = jax.nn.softmax(logits, axis=-1)
        weights, indices = jax.lax.top_k(probs, TOP_K)
        weights = weights / (weights.sum(axis=-1, keepdims=True) + 1e-09)
        weights = weights.astype(x.dtype)
        comb = jnp.sum(jax.nn.one_hot(indices, N_ROUTED, dtype=x.dtype) * weights[..., None], axis=1)
        g = jnp.einsum('td,edm->tem', flat, wg_r)
        u = jnp.einsum('td,edm->tem', flat, wu_r)
        h = jax.nn.silu(g) * u
        h = h * comb[:, :, None]
        out = out + jnp.einsum('tem,emd->td', h, wd_r)
        return out.reshape(orig_shape)

    def _L1_xattn_ref(slots, P, Wq, Wk, Wv, gru_wih, gru_whh, gru_bih, gru_bhh, slot_norm_w, input_norm_w):
        import jax, jax.numpy as jnp
        import numpy as np
        D = 256
        NUM_ITERS = 3
        EPS = 1e-06
        SCALE = D ** (-0.5)

        def rmsnorm(x, w, eps=EPS):
            return x * jax.lax.rsqrt(jnp.mean(x * x, axis=-1, keepdims=True) + eps) * w

        def gru_cell(x, h, wih, whh, bih, bhh):
            gx = x @ wih.T + bih
            gh = h @ whh.T + bhh
            xr, xz, xn = jnp.split(gx, 3, axis=-1)
            hr, hz, hn = jnp.split(gh, 3, axis=-1)
            r = jax.nn.sigmoid(xr + hr)
            z = jax.nn.sigmoid(xz + hz)
            n = jnp.tanh(xn + r * hn)
            return (1.0 - z) * n + z * h
        Pn = rmsnorm(P, input_norm_w)
        k_proj = Pn @ Wk.T
        v_proj = Pn @ Wv.T
        for _ in range(NUM_ITERS):
            sn = rmsnorm(slots, slot_norm_w)
            q_proj = sn @ Wq.T
            scores = jnp.einsum('bkd,bmd->bkm', q_proj, k_proj) * SCALE
            attn = jax.nn.softmax(scores, axis=-2)
            attn = attn / (jnp.sum(attn, axis=-1, keepdims=True) + EPS)
            updates = jnp.einsum('bkm,bmd->bkd', attn, v_proj)
            slots = gru_cell(updates, slots, gru_wih, gru_whh, gru_bih, gru_bhh)
        return slots

    def _L1_ffn_ref(x, ln1_g, ln1_b, attn_w, ln2_g, ln2_b, gate_w, gate_proj, up_proj, down_proj):
        import jax, jax.numpy as jnp
        import numpy as np
        HIDDEN = 256
        INTER = 1024
        NUM_EXPERTS = 8
        TOP_K = 2
        EPS = 1e-05

        def _layer_norm(x, g, b):
            m = jnp.mean(x, axis=-1, keepdims=True)
            v = jnp.mean(jnp.square(x - m), axis=-1, keepdims=True)
            return (x - m) * jax.lax.rsqrt(v + EPS) * g + b
        B, S, H = x.shape
        h = x + jnp.einsum('bsh,oh->bso', _layer_norm(x, ln1_g, ln1_b), attn_w)
        t = _layer_norm(h, ln2_g, ln2_b).reshape(-1, H)
        T = t.shape[0]
        logits = jnp.einsum('th,eh->te', t, gate_w)
        top_vals, top_idx = jax.lax.top_k(logits, TOP_K)
        rw = jax.nn.softmax(top_vals, axis=-1)
        comb = jnp.zeros((T, NUM_EXPERTS), dtype=t.dtype)
        comb = comb.at[jnp.arange(T)[:, None], top_idx].add(rw)
        out = jnp.zeros_like(t)
        for e in range(NUM_EXPERTS):
            g = jnp.einsum('th,ih->ti', t, gate_proj[e])
            u = jnp.einsum('th,ih->ti', t, up_proj[e])
            oe = jnp.einsum('ti,hi->th', jax.nn.silu(g) * u, down_proj[e])
            out = out + comb[:, e:e + 1] * oe
        return h + out.reshape(B, S, H)

    def _L2_xattn_ref(x, context, mask, Wq, Wkv, Wout, b_out):
        import jax, jax.numpy as jnp
        import numpy as np
        HEADS = 16
        DIM_HEAD = 64
        SCALE = DIM_HEAD ** (-0.5)
        B, Nq, _ = x.shape
        Nkv = context.shape[1]
        q = x @ Wq.T
        kv = context @ Wkv.T
        k, v = jnp.split(kv, 2, axis=-1)
        q = q.reshape(B, Nq, HEADS, DIM_HEAD).transpose(0, 2, 1, 3)
        k = k.reshape(B, Nkv, HEADS, DIM_HEAD).transpose(0, 2, 1, 3)
        v = v.reshape(B, Nkv, HEADS, DIM_HEAD).transpose(0, 2, 1, 3)
        sim = jnp.einsum('bhid,bhjd->bhij', q, k) * SCALE
        max_neg = -jnp.finfo(sim.dtype).max
        sim = jnp.where(mask[:, None, None, :], sim, max_neg)
        attn = jax.nn.softmax(sim, axis=-1)
        out = jnp.einsum('bhij,bhjd->bhid', attn, v)
        out = out.transpose(0, 2, 1, 3).reshape(B, Nq, HEADS * DIM_HEAD)
        return out @ Wout.T + b_out

    def _L2_ffn_ref(x, w_qr, w_kvr, w_q, w_kv, w_out, null_kv, null_token):
        import jax, jax.numpy as jnp
        import numpy as np
        NQ, NK, H, DH = (256, 128, 8, 64)
        b, n, d = x.shape
        g = w_qr.shape[0]
        bidx = jnp.arange(b)[:, None, None]
        q_logits = jnp.einsum('bnd,gd->bgn', x, w_qr)
        q_top, q_idx = jax.lax.top_k(q_logits, NQ)
        q_scores = jax.nn.sigmoid(q_top)[..., None]
        queries = x[bidx, q_idx]
        kv_logits = jnp.einsum('bnd,gd->bgn', x, w_kvr)
        kv_top, kv_idx = jax.lax.top_k(kv_logits, NK)
        kv_scores = jax.nn.sigmoid(kv_top)[:, :, None, :, None]
        key_values = x[bidx, kv_idx]
        q = jnp.einsum('bgnd,ged->bgne', queries, w_q)
        kv = jnp.einsum('bgnd,ged->bgne', key_values, w_kv)
        k, v = jnp.split(kv, 2, axis=-1)
        heads = lambda t: t.reshape(b, g, -1, H, DH).transpose(0, 1, 3, 2, 4)
        q, k, v = (heads(q), heads(k), heads(v))
        v = v * kv_scores
        nk = jnp.broadcast_to(null_kv[0][None], (b, g, H, 1, DH))
        nv = jnp.broadcast_to(null_kv[1][None], (b, g, H, 1, DH))
        k = jnp.concatenate([nk, k], axis=-2)
        v = jnp.concatenate([nv, v], axis=-2)
        attn = jax.nn.softmax(jnp.einsum('bghid,bghjd->bghij', q, k) * DH ** (-0.5), axis=-1)
        o = jnp.einsum('bghij,bghjd->bghid', attn, v)
        o = o.transpose(0, 1, 3, 2, 4).reshape(b, g, NQ, H * DH)
        o = jnp.einsum('bgne,gde->bgnd', o, w_out)
        o = o * q_scores
        flat_idx = q_idx.reshape(b, g * NQ)
        flat_o = o.reshape(b, g * NQ, d)
        b2 = jnp.arange(b)[:, None]
        summed = jnp.zeros_like(x).at[b2, flat_idx].add(flat_o)
        counts = jnp.zeros((b, n), x.dtype).at[b2, flat_idx].add(1.0)[..., None]
        meaned = summed / jnp.clip(counts, 1e-05)
        return jnp.where(counts > 0, meaned, null_token)

    def _L3_xattn_ref(query, key, value):
        import jax, jax.numpy as jnp
        import numpy as np
        D_MODEL = 256
        B, S = (4, 1024)
        scale = 1.0 / jnp.sqrt(jnp.asarray(query.shape[-1], query.dtype))
        scores = jnp.einsum('bqd,bkd->bqk', query, key) * scale
        weights = jax.nn.softmax(scores, axis=-1)
        out = jnp.einsum('bqk,bkd->bqd', weights, value)
        return out

    def _L3_ffn_ref(x, clip_x, clip_down, w_gate, w_up, w_down):
        import jax, jax.numpy as jnp
        import numpy as np
        QMAX = 127.0

        def _ste_round(v):
            return v + jax.lax.stop_gradient(jnp.round(v) - v)

        def _act_fake_quant(x, clip_factor):
            scale = jax.nn.sigmoid(clip_factor) * jnp.max(jnp.abs(x)) / QMAX
            return jnp.clip(_ste_round(x / scale), -QMAX - 1.0, QMAX) * scale

        def _weight_fake_quant(w):
            scale = jnp.max(jnp.abs(w), axis=1, keepdims=True) / QMAX
            return jnp.clip(_ste_round(w / scale), -QMAX - 1.0, QMAX) * scale
        xq = _act_fake_quant(x, clip_x[0])
        gate = jnp.einsum('bsh,ih->bsi', xq, _weight_fake_quant(w_gate))
        up = jnp.einsum('bsh,ih->bsi', xq, _weight_fake_quant(w_up))
        h = _act_fake_quant(jax.nn.silu(gate) * up, clip_down[0])
        return jnp.einsum('bsi,hi->bsh', h, _weight_fake_quant(w_down))
    x = x + jnp.tanh(g_xattn[0]) * _L0_xattn_ref(_layernorm(x, axis=-1), ctx_1024, L0_xattn_Wq, L0_xattn_bq, L0_xattn_Wkv, L0_xattn_bkv, L0_xattn_q_gamma, L0_xattn_q_beta, L0_xattn_k_gamma, L0_xattn_k_beta, L0_xattn_Wproj, L0_xattn_bproj)
    x = x + jnp.tanh(g_ffn[0]) * _L0_ffn_ref(_layernorm(x, axis=-1), L0_ffn_router_w, L0_ffn_wg_r, L0_ffn_wu_r, L0_ffn_wd_r, L0_ffn_wg_s, L0_ffn_wu_s, L0_ffn_wd_s)
    x = x + jnp.tanh(g_xattn[1]) * _L1_xattn_ref(_layernorm(x, axis=-1), ctx_1024, L1_xattn_Wq, L1_xattn_Wk, L1_xattn_Wv, L1_xattn_gru_wih, L1_xattn_gru_whh, L1_xattn_gru_bih, L1_xattn_gru_bhh, L1_xattn_slot_norm_w, L1_xattn_input_norm_w)
    x = x + jnp.tanh(g_ffn[1]) * _L1_ffn_ref(_layernorm(x, axis=-1), L1_ffn_ln1_g, L1_ffn_ln1_b, L1_ffn_attn_w, L1_ffn_ln2_g, L1_ffn_ln2_b, L1_ffn_gate_w, L1_ffn_gate_proj, L1_ffn_up_proj, L1_ffn_down_proj)
    x = x + jnp.tanh(g_xattn[2]) * _L2_xattn_ref(_layernorm(x, axis=-1), ctx_1024, mask_BxS2_bf1, L2_xattn_Wq, L2_xattn_Wkv, L2_xattn_Wout, L2_xattn_b_out)
    x = x + jnp.tanh(g_ffn[2]) * _L2_ffn_ref(_layernorm(x, axis=-1), L2_ffn_w_qr, L2_ffn_w_kvr, L2_ffn_w_q, L2_ffn_w_kv, L2_ffn_w_out, L2_ffn_null_kv, L2_ffn_null_token)
    x = x + jnp.tanh(g_xattn[3]) * _L3_xattn_ref(_layernorm(x, axis=-1), ctx_1024, ctx_1024)
    x = x + jnp.tanh(g_ffn[3]) * _L3_ffn_ref(_layernorm(x, axis=-1), L3_ffn_clip_x, L3_ffn_clip_down, L3_ffn_w_gate, L3_ffn_w_up, L3_ffn_w_down)
    return x

_drawn_inputs = setup_inputs


def setup_inputs(seed=0):
    import zlib

    import numpy as np

    out = dict(_drawn_inputs(seed))
    spreads = {'L0_xattn_bq': (0.0, 0.1),
     'L0_xattn_bkv': (0.0, 0.1),
     'L0_xattn_q_gamma': (1.0, 0.2),
     'L0_xattn_q_beta': (0.0, 0.379),
     'L0_xattn_k_gamma': (1.0, 0.2),
     'L0_xattn_k_beta': (0.0, 0.8),
     'L0_xattn_bproj': (0.0, 0.1),
     'L1_xattn_gru_bih': (0.0, 0.1),
     'L1_xattn_gru_bhh': (0.0, 0.1),
     'L1_xattn_slot_norm_w': (1.0, 0.2),
     'L1_xattn_input_norm_w': (1.0, 0.2),
     'L1_ffn_ln1_g': (1.0, 0.2),
     'L1_ffn_ln1_b': (0.0, 0.505),
     'L1_ffn_ln2_g': (1.0, 0.6),
     'L1_ffn_ln2_b': (0.0, 0.371),
     'L2_xattn_b_out': (0.0, 0.1)}
    factors = {'L0_ffn_router_w': 3.145,
     'L0_ffn_wg_r': 2.836,
     'L2_ffn_w_q': 3.738,
     'L2_ffn_null_kv': 8.0,
     'L3_ffn_w_gate': 4.532,
     'L3_ffn_w_up': 4.232,
     'L3_ffn_w_down': 4.188}
    for name, (base, spread) in spreads.items():
        noise = np.random.default_rng([zlib.crc32(name.encode()), seed]).standard_normal(out[name].shape)
        drawn = base * np.exp(spread * noise) if base else spread * noise
        out[name] = jnp.asarray(drawn.astype(out[name].dtype))
    for name, factor in factors.items():
        out[name] = (out[name] * factor).astype(out[name].dtype)
    return out
```

```python
from contextlib import ExitStack

import numpy as np

import concourse.bass as bass
from concourse import mybir

F32 = mybir.dt.float32
BF16 = mybir.dt.bfloat16
U8 = mybir.dt.uint8
ALU = mybir.AluOpType
ACT = mybir.ActivationFunctionType
AX = mybir.AxisListType
RMAX = bass.bass_isa.ReduceOp.max

P = 128
B, S, D = 2, 1024, 256
KD = D // P
T = B * S // P
TB = T // B
CH = 512
NC = B * S // CH
M = 154
ML = M - P
LN_EPS = 1e-5
STOP = 8


def rows(ap, k):
    return ap.rearrange("(k p) n -> p k n", p=P)


class Core:

    def __init__(self, nc, ctx, dram):
        self.nc, self.ctx, self.dram = nc, ctx, dram
        sb = self.sb
        self.x = sb(ctx, "x_tok", [P, T * D])
        self.xn = sb(ctx, "xn_tok", [P, T * D])
        self.xnT = sb(ctx, "xn_feat", [P, KD, B * S])
        self.ident = sb(ctx, "ident", [P, P])
        self.ones = sb(ctx, "ones", [P, P])
        self.small = sb(ctx, "small", [P, 8])
        self.tg = sb(ctx, "tanh_gates", [P, 8])
        self.stats = sb(ctx, "stats", [P, 2, 8])
        self.ctxT = sb(ctx, "ctx_feat", [P, KD, B * M])
        self.wa = sb(ctx, "weights_a", [P, 8192])
        self.wb = sb(ctx, "weights_b", [P, 8192])
        self.eps = self.small[:, 0:1]
        self.neg_half = self.small[:, 1:2]
        self.eps6 = self.small[:, 2:3]
        self.unround = self.small[:, 3:4]
        self.ctxR = sb(ctx, "ctx_last_repeated", [P, KD, B, 4 * ML])
        self.consts = sb(ctx, "consts", [P, dram["consts"].shape[1]])
        self.vrows = sb(ctx, "vrows", [1, dram["vrows"].shape[1]])
        self.banks = [ctx.enter_context(nc.psum_tensor(f"bank{i}", [P, 512], F32)) for i in range(8)]
        self.wa_loaded = ctx.enter_context(nc.semaphore("wa_loaded"))
        self.wb_loaded = ctx.enter_context(nc.semaphore("wb_loaded"))
        self.we_loaded = [ctx.enter_context(nc.semaphore(f"expert_loaded{n}")) for n in range(2)]
        self.wr_loaded = [ctx.enter_context(nc.semaphore(f"gate_loaded{n}")) for n in range(2)]
        self.wa_count = self.wb_count = self.phases = 0

    def sb(self, ctx, name, shape, dt=F32):
        return ctx.enter_context(self.nc.sbuf_tensor(name, shape, dt))

    def const(self, name):
        at, n = self.dram["const_at"][name]
        return self.consts[:, at:at + n]

    def vrow(self, name):
        at, n = self.dram["vrow_at"][name]
        return self.vrows[0:1, at:at + n]

    def load_a(self, sp, to, of):
        sp.dma_start(to, of).then_inc(self.wa_loaded, 16)
        self.wa_count += 16

    def load_b(self, sp, to, of):
        sp.dma_start(to, of).then_inc(self.wb_loaded, 16)
        self.wb_count += 16


class Sems(dict):

    def __init__(self, core, names):
        self.core = core
        core.phases += 1
        for n in names.split():
            self[n] = core.nc.alloc_semaphore(f"{n}_{core.phases}")

    def close(self):
        self.core.nc.clear_and_free_semaphores(list(self.values()))
        self.core.nc.all_engine_barrier()


def held(e, sem, value, gate):
    e.wait_ge(sem, value)
    e.sem_inc(gate, 1)



TAIL = " y_ready y_free stat aggr eps_added rstd centred xn_ready gate_dve gate_pool gate_act gate_pe"


def tok(buf, t):
    return buf[:, t * D:(t + 1) * D] if isinstance(t, int) else buf[:, bass.ds(t * D, D)]


def tail_stats(c, e, s, t, p, first, src=None):
    src = c.x if src is None else src
    if not first:
        held(e, s["xn_ready"], t - 1, s["gate_dve"])
    e.bn_stats(c.stats[:, p, 0:6], tok(src, t)).then_inc(s["stat"], 1)
    held(e, s["stat"], t + 1, s["gate_dve"])
    e.bn_aggr(c.stats[:, p, 6:8], c.stats[:, p, 0:6]).then_inc(s["aggr"], 1)


def tail_dve(c, e, s, t, p, first, y, layer, ready=None, count=None):
    held(e, ready or s["y_ready"], t + 1 if count is None else count, s["gate_dve"])
    xt = tok(c.x, t)
    e.scalar_tensor_tensor(out=xt, in0=y, scalar=c.tg[:, layer:layer + 1], in1=xt,
                           op0=ALU.mult, op1=ALU.add).then_inc(s["y_free"], 1)
    held(e, s["y_free"], t + 1, s["gate_dve"])
    tail_stats(c, e, s, t, p, first)


def tail_pool(c, e, s, t, p, src=None, dst=None):
    src, dst = c.x if src is None else src, c.xn if dst is None else dst
    mean, var = c.stats[:, p, 6:7], c.stats[:, p, 7:8]
    e.wait_ge(s["aggr"], t + 1)
    e.tensor_tensor(var, var, c.eps, ALU.add).then_inc(s["eps_added"], 1)
    e.wait_ge(s["eps_added"], t + 1)
    e.tensor_tensor(var, var, c.neg_half, ALU.pow).then_inc(s["rstd"], 1)
    held(e, s["rstd"], t + 1, s["gate_pool"])
    xt, xn = tok(src, t), tok(dst, t)
    e.tensor_tensor(xn, xt, mean.broadcast_to([P, D]), ALU.subtract).then_inc(s["centred"], 1)
    held(e, s["centred"], t + 1, s["gate_pool"])
    e.tensor_tensor(xn, xn, var.broadcast_to([P, D]), ALU.mult).then_inc(s["xn_ready"], 1)


def tail_pool_all(c, pool, s, src=None, dst=None):
    with pool.Fori(0, T // 2) as i:
        for p in range(2):
            tail_pool(c, pool, s, 2 * i + p, p, src, dst)


def pairs(e, body):
    body(0, True)
    with e.Fori(1, T // 2) as i:
        body(i, False)


def transpose_xn(c, load=None, src=None, scale=None, shift=None):
    src = c.xn if src is None else src
    s = Sems(c, "turned evac_act evac_dve")
    with c.nc.Block() as block:
        @block.sync
        def _(sp):
            if load:
                load(sp)

        @block.tensor
        def _(pe):
            for n in range(KD * T):
                t, k = n // KD, n % KD
                mm = pe.transpose(c.banks[n // 4][:, n % 4 * P:n % 4 * P + P],
                                  src[:, t * D + k * P:t * D + k * P + P], c.ident[:, :])
                if n % 4 == 3:
                    mm.then_inc(s["turned"], 1)

        def evacuate(e, j, sem, copy, affine):
            e.wait_ge(s["turned"], j + 1)
            of = c.banks[j][:, :].rearrange("p (t k n) -> p t k n", t=2, k=KD)
            to = c.xnT[:, :, 2 * j * P:2 * (j + 1) * P].rearrange("p k (t n) -> p t k n", t=2)
            if scale is None:
                copy(to, of).then_inc(sem, 1)
            else:
                for k in range(KD):
                    affine(to[:, :, k, :], of[:, :, k, :], scale[k], shift[k]).then_inc(sem, 1)

        @block.scalar
        def _(act):
            for j in range(0, T // 2, 2):
                evacuate(act, j, s["evac_act"], act.copy,
                         lambda to, of, g, b: act.activation(to, of, ACT.Identity, bias=b, scale=g))

        @block.vector
        def _(dve):
            for j in range(1, T // 2, 2):
                evacuate(dve, j, s["evac_dve"], dve.tensor_copy,
                         lambda to, of, g, b: dve.tensor_scalar(to, of, g, b, ALU.mult, ALU.add))
    s.close()


def phase_setup(c):
    d = c.dram
    s = Sems(c, "loaded set tanhs" + TAIL)
    with c.nc.Block() as block:
        @block.sync
        def _(sp):
            sp.dma_start(c.x[:, :].rearrange("p (t d) -> p t d", d=D),
                         d["x"].rearrange("(t p) d -> p t d", p=P)).then_inc(s["loaded"], 16)
            sp.dma_start(c.ident[:, :], d["ident"]).then_inc(s["loaded"], 16)
            sp.dma_start(c.tg[:, :], d["gates"]).then_inc(s["loaded"], 16)
            sp.dma_start(c.ctxT[:, :, :], rows(d["ctxT"], KD)).then_inc(s["loaded"], 16)
            sp.dma_start(c.consts[:, :], d["consts"]).then_inc(s["loaded"], 16)
            sp.dma_start(c.vrows[:, :], d["vrows"]).then_inc(s["loaded"], 16)

        @block.gpsimd
        def _(pool):
            pool.memset(c.ones[:, :], 1.0)
            pool.memset(c.eps, LN_EPS)
            pool.memset(c.eps6, 1e-6)
            pool.memset(c.unround, -ROUND)
            pool.memset(c.neg_half, -0.5).then_inc(s["set"], 1)
            pool.wait_ge(s["set"], 1)
            pool.wait_ge(s["loaded"], 96)
            for k in range(KD):
                for b in range(B):
                    pool.tensor_copy(c.ctxR[:, k, b, :].rearrange("p (r m) -> p r m", r=4),
                                     c.ctxT[:, k, b * M + P:(b + 1) * M].unsqueeze(1).broadcast_to([P, 4, ML]))
            tail_pool_all(c, pool, s)

        @block.scalar
        def _(act):
            act.wait_ge(s["loaded"], 96)
            act.activation(c.tg[:, :], c.tg[:, :], ACT.Tanh).then_inc(s["tanhs"], 1)

        @block.vector
        def _(dve):
            dve.wait_ge(s["loaded"], 96)

            def pair(i, first):
                for p in range(2):
                    tail_stats(c, dve, s, 2 * i + p, p, first)
            pairs(dve, pair)
    s.close()



class Heads:

    def __init__(self, H, DH, NK, HG, QB, masked=False):
        self.H, self.DH, self.NK, self.HG, self.QB, self.masked = H, DH, NK, HG, QB, masked
        self.NL = NK - P
        self.GL = H // HG
        self.C = H * DH
        self.CT = self.C // P
        self.groups = [list(range(h, min(h + 3, H))) for h in range(0, H, 3)]
        self.G = len(self.groups)
        self.R = 3 if self.G % 3 == 0 else 2
        turned = list(range(H + self.GL))
        self.batches = [turned[i:i + 4] for i in range(0, len(turned), 4)]
        self.NB = len(self.batches)

    def rows_of(self, n):
        return P if n < self.H else self.HG * self.NL

    def q_of(self, h):
        return list(range(KD)) if self.H == 1 else [h * self.DH // P]


ATT = " last_ready q_ready q_evac scores_ready masked_ max_ready exped turned p_evac o_ready recips osb_ready o_turned ot_evac"
TURN, YB, OB = (3, 4), 5, (6, 7)


class AttentionMemory:

    def __init__(self, c, ctx, a, tag, borrowed=()):
        had = dict(borrowed)

        def of(name, shape):
            return had[name] if name in had else c.sb(ctx, name + tag, shape)

        self.q = of("q", [P, 2, a.QB, P])
        self.p = of("p", [P, 2, a.H, a.NK])
        self.pt = of("pt", [P, a.H + a.GL, P])
        self.pl = of("pl", [P, 2, a.H * a.NL])
        self.nmax = of("nmax", [P, 2, a.H])
        self.sum = of("sum", [P, 2, a.H])
        self.rsum = of("rsum", [P, 2, a.H])
        self.osb = of("osb", [P, a.C])
        self.ot = of("ot", [P, a.CT, P])


class Parts:

    def __init__(self, keys, values, left, mask, stage, q_pe, q_act, project, finish_dve, finish_pool):
        self.keys, self.values, self.left, self.mask = keys, values, left, mask
        self.stage, self.q_pe, self.q_act = stage, q_pe, q_act
        self.project, self.finish_dve, self.finish_pool = project, finish_dve, finish_pool


def att_scores(c, pe, s, a, m, i, t, p, first, keys):
    for g, hs in enumerate(a.groups):
        n = a.G * t + g
        slot = p * a.G + g
        if g == 0:
            held(pe, s["q_ready"], t + 1, s["gate_pe"])
        if not (first and slot < a.R):
            held(pe, s["masked_"] if a.masked else s["exped"], n + 1 - a.R, s["gate_pe"])
        for j, h in enumerate(hs):
            ks = a.q_of(h)
            for kk, k in enumerate(ks):
                mm = pe.matmul(c.banks[slot % a.R][:, j * a.NK:(j + 1) * a.NK], m.q[:, p, k, :], keys(i, h, kk),
                               start=(kk == 0), stop=(kk == len(ks) - 1))
        mm.then_inc(s["scores_ready"], 1)


def att_max(c, dve, s, a, m, i, t, p, mask):
    for g, hs in enumerate(a.groups):
        n = a.G * t + g
        bank = c.banks[(p * a.G + g) % a.R]
        sc = bank[:, 0:len(hs) * a.NK].rearrange("p (h k) -> p h k", k=a.NK)
        held(dve, s["scores_ready"], n + 1, s["gate_dve"])
        if a.masked:
            to = m.p[:, p, hs[0]:hs[-1] + 1, :]
            dve.tensor_tensor(to, sc, mask(i).unsqueeze(1).broadcast_to([P, len(hs), a.NK]),
                              ALU.add).then_inc(s["masked_"], 1)
            dve.wait_ge(s["masked_"], n + 1)
            sc = to
        dve.tensor_reduce(m.nmax[:, p, hs[0]:hs[-1] + 1], sc, AX.X, ALU.max, negate=True).then_inc(s["max_ready"], 1)


def att_exp(c, act, s, a, m, t, p):
    for g, hs in enumerate(a.groups):
        n = a.G * t + g
        bank = c.banks[(p * a.G + g) % a.R]
        act.wait_ge(s["max_ready"], n + 1)
        for j, h in enumerate(hs):
            src = m.p[:, p, h, :] if a.masked else bank[:, j * a.NK:(j + 1) * a.NK]
            ins = act.activation(m.p[:, p, h, :], src, ACT.Exp, bias=m.nmax[:, p, h:h + 1],
                                 accum_out=m.sum[:, p, h:h + 1])
        ins.then_inc(s["exped"], 1)


def att_turn(c, pe, s, a, m, t, p):
    for j, batch in enumerate(a.batches):
        if j == 0:
            held(pe, s["exped"], a.G * (t + 1), s["gate_pe"])
        if j >= 2:
            held(pe, s["p_evac"], a.NB * t + j - 1, s["gate_pe"])
        for q, u in enumerate(batch):
            g = u - a.H
            if u == a.H:
                held(pe, s["last_ready"], t + 1, s["gate_pe"])
            w = a.HG * a.NL
            src = m.p[:, p, u, 0:P] if u < a.H else m.pl[:, p, g * w:(g + 1) * w]
            mm = pe.transpose(c.banks[TURN[j % 2]][0:a.rows_of(u), q * P:(q + 1) * P], src, c.ident[:, :])
        mm.then_inc(s["turned"], 1)


def att_evacuate(c, act, s, a, m, t, p):
    for j, batch in enumerate(a.batches):
        bank = c.banks[TURN[j % 2]]
        act.wait_ge(s["turned"], a.NB * t + j + 1)
        full = [u for u in batch if u < a.H]
        part = [u for u in batch if u >= a.H]
        if full:
            ins = act.activation(m.pt[:, full[0]:full[-1] + 1, :], bank[:, 0:len(full) * P], ACT.Copy)
        if part:
            r = a.rows_of(part[0])
            ins = act.activation(m.pt[0:r, part[0]:part[-1] + 1, :], bank[0:r, len(full) * P:len(batch) * P], ACT.Copy)
        ins.then_inc(s["p_evac"], 1)


def att_values(c, pe, s, a, m, i, t, p, vals, left):
    held(pe, s["p_evac"], a.NB * (t + 1), s["gate_pe"])
    w = a.HG * a.DH
    started = set()
    for g in range(a.GL):
        b = g * w // 512
        pe.matmul(c.banks[OB[b]][:, g * w % 512:g * w % 512 + w], m.pt[0:a.HG * a.NL, a.H + g, :], left(i, g),
                  start=(b not in started), stop=False, skip_group_check=True)
        started.add(b)
    for h in range(a.H):
        o = h * a.DH
        mm = pe.matmul(c.banks[OB[o // 512]][:, o % 512:o % 512 + a.DH], m.pt[:, h, :], vals(i, h),
                       start=False, stop=True, skip_group_check=True)
    mm.then_inc(s["o_ready"], 1)


def att_normalise(c, dve, s, a, m, t, p):
    dve.wait_ge(s["exped"], a.G * (t + 1))
    dve.reciprocal(m.rsum[:, p, :], m.sum[:, p, :]).then_inc(s["recips"], 1)
    held(dve, s["recips"], t + 1, s["gate_dve"])
    held(dve, s["o_ready"], t + 1, s["gate_dve"])
    nb = -(-a.C // 512)
    hb, w = a.H // nb, a.C // nb
    for b in range(nb):
        ins = dve.tensor_tensor(m.osb[:, b * w:(b + 1) * w].rearrange("p (h d) -> p h d", d=a.DH),
                                c.banks[OB[b]][:, 0:w].rearrange("p (h d) -> p h d", d=a.DH),
                                m.rsum[:, p, b * hb:(b + 1) * hb].unsqueeze(2).broadcast_to([P, hb, a.DH]),
                                ALU.mult)
    ins.then_inc(s["osb_ready"], 1)


def att_finish_pe(c, pe, s, a, m, i, t, w_out, b_out):
    held(pe, s["osb_ready"], t + 1, s["gate_pe"])
    for k in range(a.CT):
        mm = pe.transpose(c.banks[OB[k // 4]][:, k % 4 * P:(k % 4 + 1) * P], m.osb[:, k * P:(k + 1) * P], c.ident[:, :])
    mm.then_inc(s["o_turned"], 1)
    held(pe, s["ot_evac"], t + 1, s["gate_pe"])
    for k in range(a.CT):
        mm = pe.matmul(c.banks[YB][:, 0:D], m.ot[:, k, :], w_out(i, k), start=(k == 0),
                       stop=(k == a.CT - 1 and b_out is None))
    if b_out is not None:
        mm = pe.matmul(c.banks[YB][:, 0:D], c.ones[0:1, :], b_out, start=False, stop=True)
    mm.then_inc(s["y_ready"], 1)


def att_finish_act(c, act, s, a, m, t):
    act.wait_ge(s["o_turned"], t + 1)
    for b in range(-(-a.CT // 4)):
        n = min(4, a.CT - 4 * b)
        ins = act.activation(m.ot[:, 4 * b:4 * b + n, :], c.banks[OB[b]][:, 0:n * P], ACT.Copy)
    ins.then_inc(s["ot_evac"], 1)


def attention(c, block, s, a, m, h):
    @block.tensor
    def _(pe):
        if h.q_pe:
            h.q_pe(pe, 0, 0, 0, True)

        def pair(i, first):
            for p in range(2):
                t = 2 * i + p
                att_scores(c, pe, s, a, m, i, t, p, first, h.keys)
                if not (first and p == 0) and h.project:
                    att_finish_pe(c, pe, s, a, m, i, t - 1, *h.project)
                att_turn(c, pe, s, a, m, t, p)
                if not (first and p == 0) and not h.project:
                    held(pe, s["osb_ready"], t, s["gate_pe"])
                att_values(c, pe, s, a, m, i, t, p, h.values, h.left)
                if h.q_pe:
                    h.q_pe(pe, i if p == 0 else i + 1, t + 1, 1 - p, False)
        pairs(pe, pair)
        if h.project:
            att_finish_pe(c, pe, s, a, m, T // 2 - 1, T - 1, *h.project)

    @block.scalar
    def _(act):
        if h.q_act:
            h.q_act(act, 0, 0)

        def pair(i, first):
            for p in range(2):
                t = 2 * i + p
                att_exp(c, act, s, a, m, t, p)
                if not (first and p == 0) and h.project:
                    att_finish_act(c, act, s, a, m, t - 1)
                att_evacuate(c, act, s, a, m, t, p)
                if h.q_act:
                    h.q_act(act, t + 1, 1 - p)
        pairs(act, pair)
        if h.project:
            att_finish_act(c, act, s, a, m, T - 1)

    @block.vector
    def _(dve):
        def pair(i, first):
            for p in range(2):
                t = 2 * i + p
                att_max(c, dve, s, a, m, i, t, p, h.mask)
                if not (first and p == 0):
                    h.finish_dve(dve, t - 1, 1 - p, first)
                att_normalise(c, dve, s, a, m, t, p)
        pairs(dve, pair)
        h.finish_dve(dve, T - 1, 1, False)

    @block.gpsimd
    def _(pool):
        def pair(i, first):
            if h.stage:
                for p in range(2):
                    h.stage(pool, 2 * i + p, p, first)
            for p in range(2):
                t = 2 * i + p
                held(pool, s["exped"], a.G * (t + 1), s["gate_pool"])
                pool.tensor_copy(m.pl[:, p, :].rearrange("p (h k) -> p h k", k=a.NL),
                                 m.p[:, p, :, P:a.NK]).then_inc(s["last_ready"], 1)
                if not (first and p == 0):
                    h.finish_pool(pool, t - 1, 1 - p)
        pairs(pool, pair)
        h.finish_pool(pool, T - 1, 1)


def stage_tile(c, s, a, m, src):
    def stage(pool, t, p, first):
        if not first:
            held(pool, s["scores_ready"], a.G * (t - 1), s["gate_pool"])
        sl = src[:, :, t * P:(t + 1) * P] if isinstance(t, int) else src[:, :, bass.ds(t * P, P)]
        pool.tensor_copy(m.q[:, p, :, :], sl).then_inc(s["q_ready"], 1)
    return stage



L0X = Heads(H=16, DH=16, NK=M, HG=4, QB=KD)


def load_l0x(c, sp):
    d, w = c.dram, c.wa
    c.load_a(sp, w[:, 0:512].rearrange("p (k n) -> p k n", k=KD), rows(d["L0_xattn_Wq"], KD))
    c.load_a(sp, w[:, 512:1536].rearrange("p (k n) -> p k n", k=2 * KD), rows(d["L0_xattn_Wkv"], 2 * KD))
    c.load_a(sp, w[:, 1536:2048].rearrange("p (k n) -> p k n", k=KD), rows(d["L0_WvT"], KD))
    c.load_a(sp, w[:, 2048:2560].rearrange("p (k n) -> p k n", k=KD), rows(d["L0_WprojT"], KD))


def layer0_attention(c, load_next):
    with ExitStack() as ctx:
        a = L0X
        w = c.wa
        w_nat = [w[:, 0:512].rearrange("p (m n) -> p m n", m=KD), w[:, 512:1024].rearrange("p (m n) -> p m n", m=KD)]
        wv = w[:, 1536:2048].rearrange("p (k n) -> p k n", k=KD)
        wo = w[:, 2048:2560].rearrange("p (k n) -> p k n", k=KD)
        kb = c.sb(ctx, "l0_keys", [P, B * 16 * M])
        vm = c.sb(ctx, "l0_values", [P, B * D])
        vl = c.sb(ctx, "l0_values_last", [P, B * 4 * 64])
        with ExitStack() as prep:
            layer0_prepare(c, prep, w_nat, wv, kb, vm, vl)
        m = AttentionMemory(c, ctx, a, "_l0")
        s = Sems(c, ATT + TAIL)
        with c.nc.Block() as block:
            @block.sync
            def _(sp):
                load_next(c, sp)

            def keys(i, h, kk):
                o = h * M
                return kb[:, o:o + M] if isinstance(i, int) else kb[:, bass.ds(i // (T // 4) * (16 * M) + o, M)]

            def values(i, h):
                return vm[:, h * 16:h * 16 + 16] if isinstance(i, int) else vm[:, bass.ds(i // (T // 4) * D + h * 16, 16)]

            def left(i, g):
                return (vl[0:104, g * 64:g * 64 + 64] if isinstance(i, int)
                        else vl[0:104, bass.ds(i // (T // 4) * 256 + g * 64, 64)])

            def finish(dve, t, p, first):
                tail_dve(c, dve, s, t, p, first, c.banks[YB][:, 0:D], 0)

            attention(c, block, s, a, m, Parts(
                q_pe=None, q_act=None, keys=keys, values=values, left=left, mask=None, stage=stage_tile(c, s, a, m, c.xnT),
                project=(lambda i, k: wo[:, k, :], c.vrow("L0_xattn_bproj")), finish_dve=finish,
                finish_pool=lambda pool, t, p: tail_pool(c, pool, s, t, p)))
        s.close()


def layer0_prepare(c, ctx, w_nat, wv, kb, vm, vl):
    wc = c.sb(ctx, "centred_weights", [P, 2, KD, D])
    bc = c.sb(ctx, "centred_biases", [P, 4])
    qc = c.sb(ctx, "centred_q", [P, 2, KD, CH])
    sq = c.sb(ctx, "squares", [P, 2, KD, CH])
    kn = c.sb(ctx, "normed_k", [P, KD, B * M])
    s = Sems(c, "weights_ready job evac squared inverted scaled normed blocks values_done")
    chunks = [(1, c.ctxT[:, :, :], B * M, kn[:, :, :])]
    chunks += [(0, c.xnT[:, :, n * CH:(n + 1) * CH], CH, c.xnT[:, :, n * CH:(n + 1) * CH]) for n in range(NC)]
    jobs = [("centre", 0), ("centre", 1), ("bias", 0)]
    for n in range(len(chunks) + 1):
        if n < len(chunks):
            jobs += [("project", n, 0), ("project", n, 1)]
        if n >= 1:
            jobs += [("average", n - 1, 0), ("average", n - 1, 1)]
    jobs += [("values", 0), ("values", 1), ("last", 0), ("last", 1)]
    at = {j: n for n, j in enumerate(jobs)}
    bank = {j: c.banks[n % 8] for n, j in enumerate(jobs)}
    with c.nc.Block() as block:
        @block.tensor
        def _(pe):
            pe.wait_ge(c.wa_loaded, c.wa_count)
            for n, job in enumerate(jobs):
                if n >= 8:
                    pe.wait_ge(s["evac"], n - 7)
                out = bank[job]
                if job[0] == "centre":
                    for cb in range(KD):
                        for mb in range(KD):
                            mm = pe.matmul(out[:, cb * D + mb * P:cb * D + (mb + 1) * P],
                                           w_nat[job[1]][:, mb, cb * P:(cb + 1) * P], c.const("centre16"),
                                           start=True, stop=True)
                elif job[0] == "bias":
                    for j, name in enumerate(("bq0", "bq1", "bk0", "bk1")):
                        mm = pe.matmul(out[:, j:j + 1], c.const("centre16"), c.const(name), start=True, stop=True)
                elif job[0] == "project":
                    kind, src, width, _dst = chunks[job[1]]
                    if job[2] == 0 and job[1] == 0:
                        pe.wait_ge(s["evac"], 3)
                    for k in range(KD):
                        mm = pe.matmul(out[:, 0:width], wc[:, kind, k, job[2] * P:(job[2] + 1) * P], src[:, k, :],
                                       start=(k == 0), stop=(k == KD - 1))
                elif job[0] == "average":
                    width = chunks[job[1]][2]
                    pe.wait_ge(s["squared"], job[1] + 1)
                    mm = pe.matmul(out[:, 0:width], c.const("average16"), sq[:, job[1] % 2, job[2], 0:width],
                                   start=True, stop=True)
                else:
                    b = job[1]
                    r = P if job[0] == "values" else 104
                    for k in range(KD):
                        lhs = c.ctxT[:, k, b * M:b * M + P] if r == P else c.ctxR[:, k, b, :]
                        pe.matmul(out[0:r, 0:D], lhs, wv[:, k, :], start=(k == 0), stop=False)
                    mm = pe.matmul(out[0:r, 0:D], c.ones[0:1, 0:r], c.vrow("bv"), start=False, stop=True)
                mm.then_inc(s["job"], 1)

        @block.scalar
        def _(act):
            for n, job in enumerate(jobs):
                act.wait_ge(s["job"], n + 1)
                src = bank[job]
                if job[0] == "centre":
                    act.activation(wc[:, job[1], :, :], src[:, :], ACT.Copy).then_inc(s["evac"], 1)
                elif job[0] == "bias":
                    act.activation(bc[:, :], src[:, 0:4], ACT.Copy).then_inc(s["evac"], 1)
                    act.wait_ge(s["evac"], n + 1)
                elif job[0] == "project":
                    kind, _src, width, _dst = chunks[job[1]]
                    if job[2] == 0 and job[1] >= 2:
                        act.wait_ge(s["scaled"], job[1] - 1)
                    act.activation(qc[:, job[1] % 2, job[2], 0:width], src[:, 0:width], ACT.Identity,
                                   bias=bc[:, 2 * kind + job[2]:2 * kind + job[2] + 1]).then_inc(s["evac"], 1)
                elif job[0] == "average":
                    width = chunks[job[1]][2]
                    act.activation(sq[:, job[1] % 2, job[2], 0:width], src[:, 0:width], ACT.Sqrt,
                                   bias=c.eps).then_inc(s["evac"], 1)
                elif job[0] == "values":
                    b = job[1]
                    act.activation(vm[:, b * D:(b + 1) * D], src[:, 0:D], ACT.Copy).then_inc(s["evac"], 1)
                else:
                    b = job[1]
                    act.activation(vl[0:104, b * D:(b + 1) * D], src[0:104, 0:D], ACT.Copy).then_inc(s["evac"], 1)

        @block.vector
        def _(dve):
            def squares(n):
                width = chunks[n][2]
                dve.wait_ge(s["evac"], at[("project", n, 1)] + 1)
                if n >= 2:
                    dve.wait_ge(s["scaled"], n - 1)
                v = qc[:, n % 2, :, 0:width]
                dve.tensor_tensor(sq[:, n % 2, :, 0:width], v, v, ALU.mult).then_inc(s["squared"], 1)

            def norm(n):
                kind, _src, width, dst = chunks[n]
                gamma, beta = (("kgam", "kbet") if kind else ("qgam", "qbet"))
                dve.wait_ge(s["evac"], at[("average", n, 1)] + 1)
                v, r = qc[:, n % 2, :, 0:width], sq[:, n % 2, :, 0:width]
                dve.reciprocal(r, r).then_inc(s["inverted"], 1)
                dve.wait_ge(s["inverted"], n + 1)
                dve.scalar_tensor_tensor(out=v, in0=v, scalar=c.const(gamma), in1=sq[:, n % 2, :, 0:width],
                                         op0=ALU.mult, op1=ALU.mult).then_inc(s["normed"], 1)
                dve.wait_ge(s["normed"], n + 1)
                dve.tensor_scalar(dst, v, c.const(beta), None, ALU.add).then_inc(s["scaled"], 1)

            for n in range(len(chunks) + 1):
                if n < len(chunks):
                    squares(n)
                if n >= 1:
                    norm(n - 1)
            dve.wait_ge(s["scaled"], len(chunks))
            kbv = kb[:, :].rearrange("p (b h k) -> p b h k", b=B, h=16)
            for h in range(16):
                dve.tensor_scalar(kbv[:, :, h, :], kn[:, h // 8, :].rearrange("p (b k) -> p b k", b=B),
                                  c.const("heads16")[:, h % 8:h % 8 + 1], None, ALU.mult).then_inc(s["blocks"], 1)
            for b in range(B):
                dve.wait_ge(s["evac"], at[("last", b)] + 1)
                v = vl[0:104, b * D:(b + 1) * D].rearrange("p (g n) -> p g n", g=4)
                dve.tensor_tensor(v, v, c.const("left16")[0:104, :].unsqueeze(1).broadcast_to([104, 4, 64]),
                                  ALU.mult).then_inc(s["values_done"], 1)
    s.close()



def route(c, block, s, logits, n_experts, comb, work, floor):
    E = n_experts
    shape = [P, T, E]

    def view(n):
        return work[:, n * T * E:(n + 1) * T * E].rearrange("p (t e) -> p t e", e=E)

    def each(n):
        return work[:, 5 * T * E + n * T:5 * T * E + (n + 1) * T]

    def spread(v):
        return v.unsqueeze(2).broadcast_to(shape)

    L, first, second, score, ex = (view(n) for n in range(5))
    best, most, den, rest = (each(n) for n in range(4))
    order = c.const("falling")[:, 0:E].unsqueeze(1).broadcast_to(shape)
    cb = comb[:, 0:T * E].rearrange("p (t e) -> p t e", e=E)

    def on_vector(dve):
        steps = [0]

        def step(ins):
            steps[0] += 1
            ins.then_inc(s["routed"], 1)
            dve.wait_ge(s["routed"], steps[0])

        step(dve.tensor_copy(L, logits))
        for chosen in (first, second):
            step(dve.tensor_reduce(most, L, AX.X, ALU.max))
            if chosen is first:
                step(dve.tensor_copy(best, most))
                step(dve.tensor_tensor(ex, L, spread(best), ALU.subtract))
            step(dve.tensor_tensor(score, L, spread(most), ALU.is_equal))
            step(dve.tensor_tensor(score, score, order, ALU.mult))
            step(dve.tensor_reduce(most, score, AX.X, ALU.max))
            step(dve.tensor_tensor(chosen, score, spread(most), ALU.is_equal))
            if chosen is first:
                step(dve.scalar_tensor_tensor(out=L, in0=first, scalar=-3e38, in1=L, op0=ALU.mult, op1=ALU.add))
        step(dve.tensor_tensor(first, first, second, ALU.add))
        dve.sem_inc(s["shifted"], 1)
        dve.wait_ge(s["exponentials"], 1)
        if floor:
            step(dve.tensor_reduce(rest, ex, AX.X, ALU.add))
        step(dve.tensor_tensor(first, first, ex, ALU.mult))
        step(dve.tensor_reduce(den, first, AX.X, ALU.add))
        if floor:
            step(dve.scalar_tensor_tensor(out=den, in0=rest, scalar=1e-9, in1=den, op0=ALU.mult, op1=ALU.add))
        step(dve.reciprocal(den, den))
        step(dve.tensor_tensor(cb, first, spread(den), ALU.mult))
        dve.sem_inc(s["comb_ready"], 1)

    def on_scalar(act):
        act.wait_ge(s["shifted"], 1)
        act.activation(ex, ex, ACT.Exp).then_inc(s["exponentials"], 1)

    return on_vector, on_scalar


ROUTE = " logits_ready routed shifted exponentials comb_ready"


def router_logits(c, pe, s, weights, E, bank):
    for t in range(T):
        for k in range(KD):
            mm = pe.matmul(bank[:, t * E:(t + 1) * E], c.xnT[:, k, t * P:(t + 1) * P], weights[:, k, :],
                           start=(k == 0), stop=(k == KD - 1), skip_group_check=True)
    mm.then_inc(s["logits_ready"], 1)


MLP = " gate_pe gate_act gate_dve gate_up_ready silu_done product h_ready downed y_read"
GATE, UP, WEIGH, DOWN = (0, 1), (2, 3), (4, 5), (6, 7)


def mlp_gate_pe(c, pe, s, n, p, rhs, gate, up, weigh=None):
    held(pe, s["h_ready"], n + 1, s["gate_pe"])
    for w, bank in ((gate, GATE), (up, UP)):
        for k in range(KD):
            mm = pe.matmul(c.banks[bank[p]][:, :], w(k), rhs(k), start=(k == 0), stop=(k == KD - 1))
    if weigh:
        mm = pe.matmul(c.banks[WEIGH[p]][:, :], *weigh, start=True, stop=True)
    mm.then_inc(s["gate_up_ready"], 1)


def mlp_down_pe(c, pe, s, n, hT, wd, banks, first, last):
    held(pe, s["h_ready"], n + 3, s["gate_pe"])
    for tt in range(CH // P):
        mm = pe.matmul(c.banks[banks[tt // 2]][:, tt % 2 * D:(tt % 2 + 1) * D], hT[:, tt * P:(tt + 1) * P], wd,
                       start=first and tt % 2 == 0, stop=last, skip_group_check=True)
    mm.then_inc(s["downed"], 1)


def mlp_act(c, act, s, n, p, sg):
    held(act, s["h_ready"], n + 1, s["gate_act"])
    act.wait_ge(s["gate_up_ready"], n + 1)
    act.activation(sg[:, p, :], c.banks[GATE[p]][:, :], ACT.Silu).then_inc(s["silu_done"], 1)


def mlp_dve(c, dve, s, n, p, sg, hT, weighed):
    held(dve, s["downed"], n + 1, s["gate_dve"])
    dve.wait_ge(s["silu_done"], n + 1)
    ins = dve.tensor_tensor(hT[:, p, :], sg[:, p, :], c.banks[UP[p]][:, :], ALU.mult)
    if weighed is not None:
        ins.then_inc(s["product"], 1)
        dve.wait_ge(s["product"], weighed + 1)
        ins = dve.tensor_tensor(hT[:, p, :], hT[:, p, :], c.banks[WEIGH[p]][:, :], ALU.mult)
    ins.then_inc(s["h_ready"], 1)


def chunks(e, body):
    with e.Fori(0, NC) as i:
        body(i)


N_R, MID_R, N_S, MID_S = 16, 64, 2, 128
L0F_BLOCKS = (N_R * MID_R + N_S * MID_S) // P
L0F_ROUTED = N_R * MID_R // P


def load_l0f(c, sp):
    d, w, n = c.dram, c.wb, L0F_BLOCKS * P
    c.load_b(sp, w[:, 0:2 * n].rearrange("p (k n) -> p k n", k=KD), rows(d["L0_gates"], KD))
    c.load_b(sp, w[:, 2 * n:4 * n].rearrange("p (k n) -> p k n", k=KD), rows(d["L0_ups"], KD))
    c.load_b(sp, w[:, 4 * n:6 * n].rearrange("p (k n) -> p k n", k=L0F_BLOCKS), rows(d["L0_downs"], L0F_BLOCKS))
    c.load_b(sp, w[:, 6 * n:6 * n + 2 * N_R].rearrange("p (k n) -> p k n", k=KD), rows(d["L0_ffn_router_w"], KD))


def layer0_experts(c, load_next):
    n = L0F_BLOCKS * P
    wg = c.wb[:, 0:2 * n].rearrange("p (k n) -> p k n", k=KD)
    wu = c.wb[:, 2 * n:4 * n].rearrange("p (k n) -> p k n", k=KD)
    wd = c.wb[:, 4 * n:6 * n].rearrange("p (k n) -> p k n", k=L0F_BLOCKS)
    wr = c.wb[:, 6 * n:6 * n + 2 * N_R].rearrange("p (k n) -> p k n", k=KD)
    with ExitStack() as ctx:
        comb = c.sb(ctx, "comb0", [P, T * N_R])
        combT = c.sb(ctx, "comb0_feat", [N_R, B * S])
        work = c.sb(ctx, "route0_work", [P, 5 * T * N_R + 4 * T])
        sg = c.sb(ctx, "silu0", [P, 2, CH])
        hT = c.sb(ctx, "hidden0", [P, 2, CH])
        s = Sems(c, "comb_turned" + ROUTE)
        with c.nc.Block() as block:
            on_vector, on_scalar = route(c, block, s, c.banks[0][:, 0:T * N_R].rearrange("p (t e) -> p t e", e=N_R),
                                         N_R, comb, work, True)

            @block.tensor
            def _(pe):
                pe.wait_ge(c.wb_loaded, c.wb_count)
                router_logits(c, pe, s, wr, N_R, c.banks[0])
                pe.wait_ge(s["comb_ready"], 1)
                for t in range(T):
                    mm = pe.transpose(c.banks[1 + t // 4][0:N_R, t % 4 * P:(t % 4 + 1) * P],
                                      comb[:, t * N_R:(t + 1) * N_R], c.ident[:, :])
                mm.then_inc(s["comb_turned"], 1)

            @block.vector
            def _(dve):
                dve.wait_ge(s["logits_ready"], 1)
                on_vector(dve)
                dve.wait_ge(s["comb_turned"], 1)
                for n4 in range(4):
                    dve.tensor_copy(combT[:, n4 * CH:(n4 + 1) * CH], c.banks[1 + n4][0:N_R, :])

            @block.scalar
            def _(act):
                on_scalar(act)
        s.close()

        s = Sems(c, MLP + TAIL.replace(' gate_pe', '').replace(' gate_act', '').replace(' gate_dve', ''))
        NB = L0F_BLOCKS
        with c.nc.Block() as block:
            @block.sync
            def _(sp):
                load_next(c, sp)

            @block.tensor
            def _(pe):
                pe.sem_inc(s["downed"], 2)

                def chunk(i):
                    for m in range(NB):
                        mlp_gate_pe(c, pe, s, i * NB + m, m % 2, lambda k: c.xnT[:, k, bass.ds(i * CH, CH)],
                                    lambda k: wg[:, k, m * P:(m + 1) * P], lambda k: wu[:, k, m * P:(m + 1) * P],
                                    (c.const("pairs16")[0:N_R, m * P:(m + 1) * P], combT[:, bass.ds(i * CH, CH)])
                                    if m < L0F_ROUTED else None)
                        if m == 1:
                            held(pe, s["y_read"], i * 4 + 1, s["gate_pe"])
                        if m >= 1:
                            mlp_down_pe(c, pe, s, i * NB + m - 1, hT[:, (m - 1) % 2, :], wd[:, m - 1, :], DOWN,
                                        m == 1, False)
                    mlp_down_pe(c, pe, s, i * NB + NB - 1, hT[:, (NB - 1) % 2, :], wd[:, NB - 1, :], DOWN, False, True)
                chunks(pe, chunk)

            @block.scalar
            def _(act):
                def chunk(i):
                    for m in range(NB):
                        mlp_act(c, act, s, i * NB + m, m % 2, sg)
                chunks(act, chunk)

            @block.vector
            def _(dve):
                dve.sem_inc(s["h_ready"], 2)
                dve.sem_inc(s["y_read"], 1)
                def chunk(i):
                    for m in range(NB):
                        mlp_dve(c, dve, s, i * NB + m, m % 2, sg, hT, i * L0F_ROUTED + m if m < L0F_ROUTED else None)
                    held(dve, s["downed"], (i + 1) * NB + 2, s["gate_dve"])
                    for tt in range(4):
                        t = 4 * i + tt
                        y = c.banks[DOWN[tt // 2]][:, tt % 2 * D:(tt % 2 + 1) * D]
                        xt = tok(c.x, t)
                        dve.scalar_tensor_tensor(out=xt, in0=y, scalar=c.tg[:, 1:2], in1=xt,
                                                 op0=ALU.mult, op1=ALU.add).then_inc(s["y_read"], 1)
                    for tt in range(4):
                        t = 4 * i + tt
                        held(dve, s["y_read"], 4 * (i + 1) + 1, s["gate_dve"])
                        held(dve, s["xn_ready"], t + 1, s["gate_dve"])
                        dve.bn_stats(c.stats[:, tt % 2, 0:6], tok(c.x, t)).then_inc(s["stat"], 1)
                        held(dve, s["stat"], t + 1, s["gate_dve"])
                        dve.bn_aggr(c.stats[:, tt % 2, 6:8], c.stats[:, tt % 2, 0:6]).then_inc(s["aggr"], 1)
                chunks(dve, chunk)

            @block.gpsimd
            def _(pool):
                pool.sem_inc(s["xn_ready"], 2)
                tail_pool_all(c, pool, s)
        s.close()



ITERS = 3
GRU = 3 * D


def load_l1x(c, sp):
    d, w = c.dram, c.wa
    at = 0
    for src, n in ((d["L1_xattn_Wq"], D), (d["L1_WkT"], D), (d["L1_WvT"], D), (d["L1_wihT"], GRU), (d["L1_whhT"], GRU)):
        c.load_a(sp, w[:, at:at + KD * n].rearrange("p (k n) -> p k n", k=KD), rows(src, KD))
        at += KD * n


def layer1_slots(c, load_next):
    def part(at, n):
        return c.wa[:, at:at + KD * n].rearrange("p (k n) -> p k n", k=KD)

    wq, wk, wv, wih, whh = part(0, D), part(512, D), part(1024, D), part(1536, GRU), part(3072, GRU)
    with ExitStack() as ctx:
        mq = c.sb(ctx, "slot_keys", [P, KD, B * M])
        vw = c.sb(ctx, "slot_values", [P, B, 2, GRU])
        gb = c.sb(ctx, "gate_biases", [P, 6])
        with ExitStack() as prep:
            layer1_prepare(c, prep, wq, wk, wv, wih, mq, vw, gb)
        sq = c.xn[:, :].rearrange("p (c k n) -> p c k n", c=NC, k=KD)
        rbc = c.sb(ctx, "slot_rstd", [P, NC, CH])
        ex = c.sb(ctx, "slot_scores", [P, 2, B * S])
        nm = c.sb(ctx, "slot_max", [P, B, 2])
        sm = c.sb(ctx, "slot_sum", [P, B, 2])
        rs = c.sb(ctx, "slot_rsum", [P, B, 2])
        rsb = c.sb(ctx, "slot_rsum_wide", [P, B, 2, P])
        rd = c.sb(ctx, "slot_rden", [P, 2, CH])
        at = c.sb(ctx, "slot_attn", [P, 2, 2, CH])
        r_sb = c.sb(ctx, "gate_r", [P, KD, CH])
        z_sb = c.sb(ctx, "gate_z", [P, KD, CH])
        n_in = c.sb(ctx, "gate_n_in", [P, KD, CH])
        n_sb = c.sb(ctx, "gate_n", [P, KD, CH])
        slots = c.xnT
        s = Sems(c, "sq_ready ms_ready root_done inverted scores_done e_done max_done exp_done rsum_done wide_done "
                    "d_ready d_read rd_done attn_ready r_ready hn_ready z_ready xin_ready r_done z_done hn_read "
                    "xin_read n_done diff scaled_diff slots_done gate_pe gate_act gate_dve")
        SC, MS, DN = (4, 5), 6, 7
        rows_of = (P, ML)
        with c.nc.Block() as block:
            @block.sync
            def _(sp):
                load_next(c, sp)

            @block.tensor
            def _(pe):
                def sl(k, ch):
                    return slots[:, k, ch * CH:(ch + 1) * CH]

                def colsum(it, ch):
                    b, n = ch // 2, it * NC + ch
                    held(pe, s["wide_done"], (it * B + b + 1) * 2, s["gate_pe"])
                    held(pe, s["d_read"], n + 1, s["gate_pe"])
                    for j, r in enumerate(rows_of):
                        mm = pe.matmul(c.banks[DN][:, :], rsb[0:r, b, j, :], ex[0:r, j, ch * CH:(ch + 1) * CH],
                                       start=(j == 0), stop=(j == 1))
                    mm.then_inc(s["d_ready"], 1)

                def gates(it, ch):
                    b, n = ch // 2, it * NC + ch
                    held(pe, s["attn_ready"], 2 * n + 2, s["gate_pe"])
                    for m in range(KD):
                        g = 2 * n + m
                        for bank, at_col, from_attn, from_slots, free, ready in (
                                (0, 0, 1, 1, s["r_done"], s["r_ready"]), (1, 2, 0, 1, s["hn_read"], s["hn_ready"]),
                                (2, 1, 1, 1, s["z_done"], s["z_ready"]), (3, 2, 1, 0, s["xin_read"], s["xin_ready"])):
                            held(pe, free, g + 1, s["gate_pe"])
                            cols = slice(at_col * D + m * P, at_col * D + (m + 1) * P)
                            ops = [(whh[:, k, cols], sl(k, ch)) for k in range(KD)] if from_slots else []
                            if from_attn:
                                ops += [(vw[0:r, b, j, cols], at[0:r, ch % 2, j, :]) for j, r in enumerate(rows_of)]
                            for q, (lhs, rhs) in enumerate(ops):
                                mm = pe.matmul(c.banks[bank][:, :], lhs, rhs, start=(q == 0), stop=(q == len(ops) - 1))
                            mm.then_inc(ready, 1)

                with pe.Fori(0, ITERS) as it:
                    for ch in range(NC):
                        b, n = ch // 2, it * NC + ch
                        held(pe, s["sq_ready"], n + 1, s["gate_pe"])
                        held(pe, s["root_done"], n + 1, s["gate_pe"])
                        for k in range(KD):
                            mm = pe.matmul(c.banks[MS][:, :], c.const("mean256"), sq[:, ch, k, :], start=(k == 0), stop=(k == KD - 1))
                        mm.then_inc(s["ms_ready"], 1)
                        held(pe, s["e_done"], 2 * n + 2, s["gate_pe"])
                        for j, r in enumerate(rows_of):
                            for k in range(KD):
                                mm = pe.matmul(c.banks[SC[j]][0:r, :], mq[:, k, b * M + j * P:b * M + j * P + r], sl(k, ch),
                                               start=(k == 0), stop=(k == KD - 1))
                        mm.then_inc(s["scores_done"], 1)
                    colsum(it, 0)
                    for ch in range(NC):
                        if ch + 1 < NC:
                            colsum(it, ch + 1)
                        gates(it, ch)

            @block.scalar
            def _(act):
                act.sem_inc(s["root_done"], 1)
                act.sem_inc(s["r_done"], 1)
                act.sem_inc(s["z_done"], 1)
                with act.Fori(0, ITERS) as it:
                    for ch in range(NC):
                        n = it * NC + ch
                        act.wait_ge(s["ms_ready"], n + 1)
                        act.activation(rbc[:, ch, :], c.banks[MS][:, :], ACT.Sqrt, bias=c.eps6).then_inc(s["root_done"], 1)
                    for b in range(B):
                        act.wait_ge(s["max_done"], 2 * (it * B + b) + 2)
                        for j, r in enumerate(rows_of):
                            v = ex[0:r, j, b * S:(b + 1) * S]
                            ins = act.activation(v, v, ACT.Exp, bias=nm[0:r, b, j:j + 1], accum_out=sm[0:r, b, j:j + 1])
                        ins.then_inc(s["exp_done"], 1)
                    for ch in range(NC):
                        for m in range(KD):
                            g = 2 * (it * NC + ch) + m
                            act.wait_ge(s["r_ready"], g + 1)
                            act.activation(r_sb[:, m, :], c.banks[0][:, :], ACT.Sigmoid, bias=gb[:, m:m + 1]).then_inc(s["r_done"], 1)
                            held(act, s["scaled_diff"], g + 1, s["gate_act"])
                            act.wait_ge(s["z_ready"], g + 1)
                            act.activation(z_sb[:, m, :], c.banks[2][:, :], ACT.Sigmoid, bias=gb[:, 2 + m:3 + m]).then_inc(s["z_done"], 1)
                            act.wait_ge(s["xin_read"], g + 2)
                            act.activation(n_sb[:, m, :], n_in[:, m, :], ACT.Tanh, bias=c.const("bih")[:, 4 + m:5 + m]).then_inc(s["n_done"], 1)

            @block.vector
            def _(dve):
                dve.sem_inc(s["e_done"], 2)
                dve.sem_inc(s["d_read"], 1)
                dve.sem_inc(s["hn_read"], 1)
                dve.sem_inc(s["xin_read"], 1)
                dve.sem_inc(s["slots_done"], 1)
                dve.sem_inc(s["scaled_diff"], 2)

                def attn(it, ch):
                    b, n = ch // 2, it * NC + ch
                    held(dve, s["d_ready"], n + 1, s["gate_dve"])
                    v = rd[:, ch % 2, :]
                    dve.tensor_scalar(v, c.banks[DN][:, :], c.eps6, None, ALU.add).then_inc(s["d_read"], 1)
                    dve.wait_ge(s["d_read"], n + 2)
                    dve.reciprocal(v, v).then_inc(s["rd_done"], 1)
                    dve.wait_ge(s["rd_done"], n + 1)
                    for j, r in enumerate(rows_of):
                        dve.scalar_tensor_tensor(out=at[0:r, ch % 2, j, :], in0=ex[0:r, j, ch * CH:(ch + 1) * CH],
                                                 scalar=rs[0:r, b, j:j + 1], in1=rd[0:r, ch % 2, :],
                                                 op0=ALU.mult, op1=ALU.mult).then_inc(s["attn_ready"], 1)

                def gru(it, ch):
                    n = it * NC + ch
                    for m in range(KD):
                        g = 2 * n + m
                        held(dve, s["r_done"], g + 2, s["gate_dve"])
                        held(dve, s["hn_ready"], g + 1, s["gate_dve"])
                        v = n_in[:, m, :]
                        dve.scalar_tensor_tensor(out=v, in0=c.banks[1][:, :], scalar=c.const("bhh")[:, 4 + m:5 + m],
                                                 in1=r_sb[:, m, :], op0=ALU.add, op1=ALU.mult).then_inc(s["hn_read"], 1)
                        held(dve, s["hn_read"], g + 2, s["gate_dve"])
                        held(dve, s["xin_ready"], g + 1, s["gate_dve"])
                        dve.tensor_tensor(v, v, c.banks[3][:, :], ALU.add).then_inc(s["xin_read"], 1)
                    for m in range(KD):
                        g = 2 * n + m
                        h, v = slots[:, m, ch * CH:(ch + 1) * CH], n_in[:, m, :]
                        held(dve, s["n_done"], g + 1, s["gate_dve"])
                        dve.tensor_tensor(v, h, n_sb[:, m, :], ALU.subtract).then_inc(s["diff"], 1)
                        held(dve, s["diff"], g + 1, s["gate_dve"])
                        dve.tensor_tensor(v, v, z_sb[:, m, :], ALU.mult).then_inc(s["scaled_diff"], 1)
                        dve.wait_ge(s["scaled_diff"], g + 3)
                        dve.tensor_tensor(h, v, n_sb[:, m, :], ALU.add).then_inc(s["slots_done"], 1)

                with dve.Fori(0, ITERS) as it:
                    held(dve, s["slots_done"], it * (NC * KD) + 1, s["gate_dve"])
                    for ch in range(NC):
                        v = slots[:, :, ch * CH:(ch + 1) * CH]
                        dve.tensor_tensor(sq[:, ch, :, :], v, v, ALU.mult).then_inc(s["sq_ready"], 1)
                    for ch in range(NC):
                        n = it * NC + ch
                        held(dve, s["root_done"], n + 2, s["gate_dve"])
                        dve.reciprocal(rbc[:, ch, :], rbc[:, ch, :]).then_inc(s["inverted"], 1)
                        held(dve, s["inverted"], n + 1, s["gate_dve"])
                        held(dve, s["scores_done"], n + 1, s["gate_dve"])
                        for j, r in enumerate(rows_of):
                            dve.tensor_tensor(ex[0:r, j, ch * CH:(ch + 1) * CH], c.banks[SC[j]][0:r, :], rbc[0:r, ch, :],
                                              ALU.mult).then_inc(s["e_done"], 1)
                        if ch % 2:
                            b = ch // 2
                            held(dve, s["e_done"], 2 * n + 4, s["gate_dve"])
                            for j, r in enumerate(rows_of):
                                dve.tensor_reduce(nm[0:r, b, j:j + 1], ex[0:r, j, b * S:(b + 1) * S], AX.X, ALU.max,
                                                  negate=True).then_inc(s["max_done"], 1)
                    for b in range(B):
                        held(dve, s["exp_done"], it * B + b + 1, s["gate_dve"])
                        for j, r in enumerate(rows_of):
                            dve.reciprocal(rs[0:r, b, j:j + 1], sm[0:r, b, j:j + 1]).then_inc(s["rsum_done"], 1)
                        held(dve, s["rsum_done"], 2 * (it * B + b) + 2, s["gate_dve"])
                        for j, r in enumerate(rows_of):
                            dve.tensor_scalar(rsb[0:r, b, j, :], c.ones[0:r, :], rs[0:r, b, j:j + 1], None,
                                              ALU.mult).then_inc(s["wide_done"], 1)
                    attn(it, 0)
                    for ch in range(NC):
                        if ch + 1 < NC:
                            attn(it, ch + 1)
                        gru(it, ch)
        s.close()

    s = Sems(c, TAIL)
    with c.nc.Block() as block:
        @block.tensor
        def _(pe):
            for t in range(T):
                if t >= 8:
                    pe.wait_ge(s["y_free"], t - 7)
                for k in range(KD):
                    mm = pe.transpose(c.banks[t % 8][:, k * P:(k + 1) * P], slots[:, k, t * P:(t + 1) * P], c.ident[:, :])
                mm.then_inc(s["y_ready"], 1)

        @block.vector
        def _(dve):
            for t in range(T):
                tail_dve(c, dve, s, t, t % 2, t < 2, c.banks[t % 8][:, 0:D], 2)

        @block.gpsimd
        def _(pool):
            tail_pool_all(c, pool, s)
    s.close()


def layer1_prepare(c, ctx, wq, wk, wv, wih, mq, vw, gb):
    W = B * M
    sq = c.sb(ctx, "ctx_squares", [P, KD, W])
    r = c.sb(ctx, "ctx_rstd", [P, W])
    pn = c.sb(ctx, "ctx_normed", [P, KD, W])
    kT = c.sb(ctx, "slot_k", [P, KD, W])
    vT = c.sb(ctx, "slot_v", [P, KD, W])
    w16 = c.sb(ctx, "slot_w_sixteenth", [P, KD])
    s = Sems(c, "step job evac rooted")
    with c.nc.Block() as block:
        @block.tensor
        def _(pe):
            pe.wait_ge(c.wa_loaded, c.wa_count)
            pe.wait_ge(s["step"], 1)
            for k in range(KD):
                mm = pe.matmul(c.banks[0][:, 0:W], c.const("mean256"), sq[:, k, :], start=(k == 0), stop=(k == KD - 1))
            mm.then_inc(s["job"], 1)
            pe.wait_ge(s["step"], 4)
            for n, w in enumerate((wk, wk, wv, wv)):
                for k in range(KD):
                    mm = pe.matmul(c.banks[1 + n][:, 0:W], w[:, k, n % 2 * P:(n % 2 + 1) * P], pn[:, k, :],
                                   start=(k == 0), stop=(k == KD - 1))
                mm.then_inc(s["job"], 1)
            pe.wait_ge(s["evac"], 2)
            for m in range(KD):
                for k in range(KD):
                    mm = pe.matmul(c.banks[5 + m][:, 0:W], wq[:, k, m * P:(m + 1) * P], kT[:, k, :],
                                   start=(k == 0), stop=(k == KD - 1))
                mm.then_inc(s["job"], 1)
            pe.wait_ge(s["evac"], 6)
            for n in range(8):
                b, j, half = n // 4, n // 2 % 2, n % 2
                rr = (P, ML)[j]
                if n >= 6:
                    pe.wait_ge(s["evac"], n + 1)
                for k in range(KD):
                    mm = pe.matmul(c.banks[n % 6][0:rr, 0:384], vT[:, k, b * M + j * P:b * M + j * P + rr],
                                   wih[:, k, half * 384:(half + 1) * 384], start=(k == 0), stop=(k == KD - 1))
                mm.then_inc(s["job"], 1)

        @block.scalar
        def _(act):
            act.wait_ge(s["job"], 1)
            act.activation(r[:, :], c.banks[0][:, 0:W], ACT.Sqrt, bias=c.eps6).then_inc(s["rooted"], 1)
            for n in range(4):
                act.wait_ge(s["job"], 2 + n)
                act.activation((kT if n < 2 else vT)[:, n % 2, :], c.banks[1 + n][:, 0:W], ACT.Copy).then_inc(s["evac"], 1)
            for m in range(KD):
                act.wait_ge(s["job"], 6 + m)
                act.activation(mq[:, m, :], c.banks[5 + m][:, 0:W], ACT.Copy, scale=w16[:, m:m + 1]).then_inc(s["evac"], 1)
            for n in range(8):
                b, j, half = n // 4, n // 2 % 2, n % 2
                rr = (P, ML)[j]
                act.wait_ge(s["job"], 8 + n)
                act.activation(vw[0:rr, b, j, half * 384:(half + 1) * 384], c.banks[n % 6][0:rr, 0:384], ACT.Copy).then_inc(s["evac"], 1)

        @block.vector
        def _(dve):
            dve.tensor_scalar(w16[:, :], c.const("slotw"), float(D) ** -0.5, None, ALU.mult)
            dve.tensor_tensor(sq[:, :, :], c.ctxT[:, :, :], c.ctxT[:, :, :], ALU.mult).then_inc(s["step"], 1)
            dve.wait_ge(s["rooted"], 1)
            dve.reciprocal(r[:, :], r[:, :]).then_inc(s["step"], 1)
            dve.wait_ge(s["step"], 2)
            for k in range(KD):
                dve.scalar_tensor_tensor(out=pn[:, k, :], in0=c.ctxT[:, k, :], scalar=c.const("inw")[:, k:k + 1], in1=r[:, :],
                                         op0=ALU.mult, op1=ALU.mult).then_inc(s["step"], 1)
            dve.tensor_tensor(gb[:, :], c.const("bih"), c.const("bhh"), ALU.add)
    s.close()



N_E, INTER = 8, 1024
EB = INTER // P
EXPERT = 2 * KD * INTER + EB * D


def load_l1f(c, sp):
    d, w = c.dram, c.wb
    c.load_b(sp, w[:, 0:512].rearrange("p (k n) -> p k n", k=KD), rows(d["L1_attnT"], KD))
    c.load_b(sp, w[:, 512:512 + KD * N_E].rearrange("p (k n) -> p k n", k=KD), rows(d["L1_gateT"], KD))


def layer1_experts(c, load_next):
    wa = c.wb[:, 0:512].rearrange("p (k n) -> p k n", k=KD)
    wr = c.wb[:, 512:512 + KD * N_E].rearrange("p (k n) -> p k n", k=KD)
    with ExitStack() as ctx:
        t_tok = c.sb(ctx, "normed_again", [P, T * D])
        wexp = c.sb(ctx, "expert_weights", [P, 2, EXPERT])
        comb = c.sb(ctx, "comb1", [P, T * N_E])
        work = c.sb(ctx, "route1_work", [P, 5 * T * N_E + 4 * T])
        sg = c.sb(ctx, "silu1", [P, 2, CH])
        hT = c.sb(ctx, "hidden1", [P, 2, CH])

        s = Sems(c, TAIL)
        with c.nc.Block() as block:
            @block.sync
            def _(sp):
                for e in range(2):
                    sp.dma_start(wexp[:, e, :], c.dram["L1_experts"][e, :, :]).then_inc(c.we_loaded[e], 16)

            @block.vector
            def _(dve):
                def pair(i, first):
                    for p in range(2):
                        tail_stats(c, dve, s, 2 * i + p, p, first, c.xn)
                pairs(dve, pair)

            @block.gpsimd
            def _(pool):
                tail_pool_all(c, pool, s, c.xn, t_tok)
        s.close()
        transpose_xn(c, None, t_tok, [c.const("ln1g")[:, k:k + 1] for k in range(KD)],
                     [c.const("ln1b")[:, k:k + 1] for k in range(KD)])

        s = Sems(c, TAIL)
        with c.nc.Block() as block:
            @block.tensor
            def _(pe):
                pe.wait_ge(c.wb_loaded, c.wb_count)
                for t in range(T):
                    if t >= 8:
                        pe.wait_ge(s["y_free"], t - 7)
                    for k in range(KD):
                        mm = pe.matmul(c.banks[t % 8][:, 0:D], c.xnT[:, k, t * P:(t + 1) * P], wa[:, k, :],
                                       start=(k == 0), stop=(k == KD - 1))
                    mm.then_inc(s["y_ready"], 1)

            @block.vector
            def _(dve):
                for t in range(T):
                    dve.wait_ge(s["y_ready"], t + 1)
                    dve.tensor_tensor(tok(c.xn, t), tok(c.xn, t), c.banks[t % 8][:, 0:D], ALU.add).then_inc(s["y_free"], 1)
                    dve.wait_ge(s["y_free"], t + 1)
                    tail_stats(c, dve, s, t, t % 2, t < 2, c.xn)

            @block.gpsimd
            def _(pool):
                tail_pool_all(c, pool, s, c.xn, t_tok)
        s.close()
        transpose_xn(c, None, t_tok, [c.const("ln2g")[:, k:k + 1] for k in range(KD)],
                     [c.const("ln2b")[:, k:k + 1] for k in range(KD)])

        s = Sems(c, ROUTE)
        with c.nc.Block() as block:
            on_vector, on_scalar = route(c, block, s, c.banks[0][:, 0:T * N_E].rearrange("p (t e) -> p t e", e=N_E),
                                         N_E, comb, work, False)

            @block.tensor
            def _(pe):
                router_logits(c, pe, s, wr, N_E, c.banks[0])

            @block.vector
            def _(dve):
                dve.wait_ge(s["logits_ready"], 1)
                on_vector(dve)

            @block.scalar
            def _(act):
                on_scalar(act)
        s.close()

        s = Sems(c, MLP)
        outs = ((4, 5), (6, 7))
        with c.nc.Block() as block:
            @block.sync
            def _(sp):
                load_next(c, sp)
                with sp.Fori(1, N_E // 2) as ep:
                    for eb in range(2):
                        e = 2 * ep + eb
                        sp.wait_ge(s["downed"], (e - 1) * NC * EB + 2)
                        sp.dma_start(wexp[:, eb, :], c.dram["L1_experts"][bass.ds(e, 1), :, :].rearrange("e p n -> (e p) n")).then_inc(c.we_loaded[eb], 16)

            @block.tensor
            def _(pe):
                pe.sem_inc(s["downed"], 2)
                with pe.Fori(0, N_E // 2) as ep:
                    for eb in range(2):
                        e = 2 * ep + eb
                        w = wexp[:, eb, :]
                        held(pe, c.we_loaded[eb], (ep + 1) * 16, s["gate_pe"])
                        with pe.Fori(0, NC // 2) as cp:
                            for par in range(2):
                                ch = 2 * cp + par
                                q = e * NC + ch
                                for m in range(EB + 1):
                                    if m < EB:
                                        mlp_gate_pe(c, pe, s, q * EB + m, m % 2, lambda k: c.xnT[:, k, bass.ds(ch * CH, CH)],
                                                    lambda k: w[:, k * INTER + m * P:k * INTER + (m + 1) * P],
                                                    lambda k: w[:, (KD + k) * INTER + m * P:(KD + k) * INTER + (m + 1) * P])
                                    if m == 1:
                                        held(pe, s["y_read"], 4 * (q + 1), s["gate_pe"])
                                    if m >= 1:
                                        at = 2 * KD * INTER + (m - 1) * D
                                        mlp_down_pe(c, pe, s, q * EB + m - 1, hT[:, (m - 1) % 2, :], w[:, at:at + D],
                                                    outs[par], m == 1, m == EB)

            def every_chunk(eng, body):
                with eng.Fori(0, N_E) as e:
                    with eng.Fori(0, NC // 2) as cp:
                        for par in range(2):
                            body(e, 2 * cp + par, par)

            @block.scalar
            def _(act):
                def body(e, ch, par):
                    for m in range(EB):
                        mlp_act(c, act, s, (e * NC + ch) * EB + m, m % 2, sg)
                every_chunk(act, body)

            @block.vector
            def _(dve):
                dve.sem_inc(s["h_ready"], 2)
                dve.sem_inc(s["y_read"], 8)

                def body(e, ch, par):
                    q = e * NC + ch
                    for m in range(EB):
                        mlp_dve(c, dve, s, q * EB + m, m % 2, sg, hT, None)
                    held(dve, s["downed"], (q + 1) * EB + 2, s["gate_dve"])
                    for tt in range(4):
                        t = 4 * ch + tt
                        ht = tok(c.xn, t)
                        dve.scalar_tensor_tensor(out=ht, in0=c.banks[outs[par][tt // 2]][:, tt % 2 * D:(tt % 2 + 1) * D],
                                                 scalar=comb[:, bass.ds(t * N_E + e, 1)], in1=ht,
                                                 op0=ALU.mult, op1=ALU.add).then_inc(s["y_read"], 1)
                every_chunk(dve, body)
        s.close()

        s = Sems(c, TAIL)
        with c.nc.Block() as block:
            @block.vector
            def _(dve):
                dve.sem_inc(s["y_ready"], T)

                def pair(i, first):
                    for p in range(2):
                        t = 2 * i + p
                        tail_dve(c, dve, s, t, p, first, tok(c.xn, t), 3)
                pairs(dve, pair)

            @block.gpsimd
            def _(pool):
                tail_pool_all(c, pool, s)
        s.close()



L2X = Heads(H=16, DH=64, NK=M, HG=4, QB=8, masked=True)
FLT_MAX = 3.4028234663852886e38


def load_l2x(c, sp):
    d, w = c.dram, c.wa
    for n, (src, k) in enumerate(((d["L2_WqT"], KD), (d["L2_WkT"], KD), (d["L2_WvT"], KD), (d["L2_WoutT"], 8))):
        c.load_a(sp, w[:, n * 2048:(n + 1) * 2048].rearrange("p (k n) -> p k n", k=k), rows(src, k))


def layer2_attention(c, load_next):
    a = L2X
    W, C = B * M, 16 * 64
    wq, wk, wv = (c.wa[:, n * 2048:(n + 1) * 2048].rearrange("p (k n) -> p k n", k=KD) for n in range(3))
    wo = c.wa[:, 6144:8192].rearrange("p (k n) -> p k n", k=8)
    with ExitStack() as ctx:
        kb = c.sb(ctx, "l2_keys", [P, B * 16 * M])
        vm = c.sb(ctx, "l2_values", [P, B * C])
        vl = c.sb(ctx, "l2_values_last", [P, B * C])
        mb = c.sb(ctx, "mask_bias", [P, W])
        with ExitStack() as prep:
            m01 = c.sb(prep, "mask_ones", [P, W])
            mu8 = c.sb(prep, "mask_bytes", [P, W], U8)
            ctxm = c.sb(prep, "ctx_masked", [P, KD, W])
            s = Sems(c, "mask_loaded step job k_evac v_evac done")
            with c.nc.Block() as block:
                @block.sync
                def _(sp):
                    sp.dma_start(mu8[:, :], c.dram["mask"]).then_inc(s["mask_loaded"], 16)

                @block.tensor
                def _(pe):
                    pe.wait_ge(c.wa_loaded, c.wa_count)
                    for n in range(8):
                        b, half = n // 2 % 2, n % 2
                        r = P if n < 4 else 104
                        for k in range(KD):
                            lhs = c.ctxT[:, k, b * M:b * M + P] if n < 4 else c.ctxR[:, k, b, :]
                            mm = pe.matmul(c.banks[n][0:r, :], lhs, wv[:, k, half * 512:(half + 1) * 512],
                                           start=(k == 0), stop=(k == KD - 1))
                        mm.then_inc(s["job"], 1)
                    pe.wait_ge(s["step"], 4)
                    for n in range(8):
                        pe.wait_ge(s["v_evac"], n + 1)
                        for k in range(KD):
                            mm = pe.matmul(c.banks[n][:, 0:W], wk[:, k, n * P:(n + 1) * P], ctxm[:, k, :],
                                           start=(k == 0), stop=(k == KD - 1))
                        mm.then_inc(s["job"], 1)

                @block.scalar
                def _(act):
                    for n in range(8):
                        b, half = n // 2 % 2, n % 2
                        r, to = (P, vm) if n < 4 else (104, vl)
                        act.wait_ge(s["job"], n + 1)
                        act.activation(to[0:r, b * C + half * 512:b * C + (half + 1) * 512], c.banks[n][0:r, :],
                                       ACT.Copy).then_inc(s["v_evac"], 1)

                @block.vector
                def _(dve):
                    dve.wait_ge(s["mask_loaded"], 16)
                    dve.tensor_copy(m01[:, :], mu8[:, :]).then_inc(s["step"], 1)
                    dve.wait_ge(s["step"], 1)
                    dve.tensor_scalar(mb[:, :], m01[:, :], -1.0, FLT_MAX, ALU.add, ALU.mult).then_inc(s["step"], 1)
                    for k in range(KD):
                        dve.tensor_tensor(ctxm[:, k, :], c.ctxT[:, k, :], m01[:, :], ALU.mult).then_inc(s["step"], 1)
                    kbv = kb[:, :].rearrange("p (b h k) -> p b h k", b=B, h=16)
                    for h in range(16):
                        dve.wait_ge(s["job"], 8 + h // 2 + 1)
                        dve.tensor_scalar(kbv[:, :, h, :], c.banks[h // 2][:, 0:W].rearrange("p (b k) -> p b k", b=B),
                                          c.const("heads64")[:, h % 2:h % 2 + 1], None, ALU.mult).then_inc(s["k_evac"], 1)
                    dve.wait_ge(s["v_evac"], 8)
                    for b in range(B):
                        v = vl[0:104, b * C:(b + 1) * C].rearrange("p (g n) -> p g n", g=4)
                        dve.tensor_tensor(v, v, c.const("left64")[0:104, :].unsqueeze(1).broadcast_to([104, 4, 256]),
                                          ALU.mult).then_inc(s["done"], 1)
            s.close()

        m = AttentionMemory(c, ctx, a, "_l2", {
            "osb": c.wb[:, 4096:5120], "ot": c.wb[:, 5120:6144].rearrange("p (k n) -> p k n", k=8)})
        s = Sems(c, "q_projected" + ATT + TAIL)
        with c.nc.Block() as block:
            @block.sync
            def _(sp):
                load_next(c, sp)

            def at(i, size, o, n):
                return slice(o, o + n) if isinstance(i, int) else bass.ds(i // (T // 4) * size + o, n)

            def q_pe(pe, i, t, p, first):
                cols = slice(t * P, (t + 1) * P) if isinstance(t, int) else bass.ds(t % T * P, P)
                for n in range(8):
                    for k in range(KD):
                        mm = pe.matmul(c.banks[TURN[n // 4]][:, n % 4 * P:(n % 4 + 1) * P], wq[:, k, n * P:(n + 1) * P],
                                       c.xnT[:, k, cols], start=(k == 0), stop=(k == KD - 1), skip_group_check=True)
                mm.then_inc(s["q_projected"], 1)

            def q_act(act, t, p):
                act.wait_ge(s["q_projected"], t + 1)
                for b in range(2):
                    ins = act.activation(m.q[:, p, 4 * b:4 * b + 4, :], c.banks[TURN[b]][:, :], ACT.Copy)
                ins.then_inc(s["q_ready"], 1)

            attention(c, block, s, a, m, Parts(
                q_pe=q_pe, q_act=q_act, stage=None, mask=lambda i: mb[:, at(i, M, 0, M)],
                keys=lambda i, h, kk: kb[:, at(i, 16 * M, h * M, M)],
                values=lambda i, h: vm[:, at(i, C, h * 64, 64)],
                left=lambda i, g: vl[0:104, at(i, C, g * 256, 256)],
                project=(lambda i, k: wo[:, k, :], c.vrow("L2_xattn_b_out")),
                finish_dve=lambda dve, t, p, first: tail_dve(c, dve, s, t, p, first, c.banks[YB][:, 0:D], 4),
                finish_pool=lambda pool, t, p: tail_pool(c, pool, s, t, p)))
        s.close()



GATES, NQ, NKV, RH, RD = 4, 256, 128, 8, 64
RC = RH * RD
PAIRS = B * GATES
R_W = 2 * RC + 4 * RC + 4 * D
L2F = Heads(H=RH, DH=RD, NK=NKV + 1, HG=RH, QB=RC // P)
PICKED = -3.0e38


def load_l2f(c, sp):
    sp.dma_start(c.wb[:, 0:R_W], c.dram["L2_gates"][0]).then_inc(c.wr_loaded[0], 16)


def layer2_routed(c, load_next):
    a = L2F
    NR, ST_ = 2 * PAIRS, S // P
    with ExitStack() as ctx:
        pos = c.sb(ctx, "place_rows", [NR, S])
        sig = c.sb(ctx, "sigmoid_rows", [NR, S])
        posT = c.sb(ctx, "place_tok", [P, ST_, NR])
        sigT = c.sb(ctx, "sigmoid_tok", [P, ST_, NR])
        wr = c.sb(ctx, "routing_weights", [P, KD, 2, NR])
        with ExitStack() as prep:
            lg = c.sb(prep, "logit_rows", [NR, S])
            early = c.sb(prep, "chosen_128", [NR, S])
            one = c.sb(prep, "row_ones", [NR, S])
            best = c.sb(prep, "best8", [NR, 8])
            s = Sems(c, "w_loaded logits evac best_ready replaced step rows_ready rows_turned turned_evac gate_dve")
            with c.nc.Block() as block:
                @block.sync
                def _(sp):
                    sp.dma_start(wr[:, :, :, :], c.dram["L2_routing"].rearrange("(k p) b n -> p k b n", p=P)).then_inc(s["w_loaded"], 16)

                @block.tensor
                def _(pe):
                    pe.wait_ge(s["w_loaded"], 16)
                    for half in range(2):
                        for n in range(2 * KD):
                            b, k = n // KD, n % KD
                            at = b * S + half * CH
                            mm = pe.matmul(c.banks[half][0:NR, :], wr[:, k, b, :], c.xnT[:, k, at:at + CH],
                                           start=(n == 0), stop=(n == 2 * KD - 1))
                        mm.then_inc(s["logits"], 1)
                    pe.wait_ge(s["rows_ready"], 2)
                    for n, src in enumerate((pos, sig)):
                        for t in range(ST_):
                            mm = pe.transpose(c.banks[2 + n][:, t * NR:(t + 1) * NR], src[:, t * P:(t + 1) * P], c.ident[0:NR, 0:NR])
                        mm.then_inc(s["rows_turned"], 1)

                @block.scalar
                def _(act):
                    for half in range(2):
                        act.wait_ge(s["logits"], half + 1)
                        act.activation(lg[:, half * CH:(half + 1) * CH], c.banks[half][0:NR, :], ACT.Copy).then_inc(s["evac"], 1)
                    act.activation(sig[:, 0:CH], c.banks[0][0:NR, :], ACT.Sigmoid)
                    act.activation(sig[:, CH:S], c.banks[1][0:NR, :], ACT.Sigmoid).then_inc(s["rows_ready"], 1)
                    act.wait_ge(s["rows_turned"], 2)
                    act.activation(posT[:, :, :], c.banks[2][:, 0:ST_ * NR], ACT.Copy)
                    act.activation(sigT[:, :, :], c.banks[3][:, 0:ST_ * NR], ACT.Copy).then_inc(s["turned_evac"], 1)

                @block.vector
                def _(dve):
                    dve.memset(one[:, :], 1.0)
                    dve.wait_ge(s["evac"], 2)
                    for stage in range(2):
                        with dve.Fori(0, NKV // 8) as i:
                            n = stage * (NKV // 8) + i
                            dve.max(best[:, :], lg[:, :]).then_inc(s["best_ready"], 1)
                            held(dve, s["best_ready"], n + 1, s["gate_dve"])
                            dve.match_replace(lg[:, :], best[:, :], lg[:, :], PICKED).then_inc(s["replaced"], 1)
                            held(dve, s["replaced"], n + 1, s["gate_dve"])
                        if stage == 0:
                            dve.tensor_scalar(early[:, :], lg[:, :], PICKED, None, ALU.is_equal).then_inc(s["step"], 1)
                    dve.wait_ge(s["step"], 1)
                    dve.tensor_scalar(lg[:, :], lg[:, :], PICKED, c.const("query_rows")[0:NR, :], ALU.is_equal, ALU.mult).then_inc(s["step"], 1)
                    dve.wait_ge(s["step"], 2)
                    dve.scalar_tensor_tensor(out=lg[:, :], in0=early[:, :], scalar=c.const("key_rows")[0:NR, :], in1=lg[:, :],
                                             op0=ALU.mult, op1=ALU.add).then_inc(s["step"], 1)
                    dve.wait_ge(s["step"], 3)
                    dve.tensor_tensor_scan(early[:, :], one[:, :], lg[:, :], 0.0, ALU.mult, ALU.add).then_inc(s["step"], 1)
                    dve.wait_ge(s["step"], 4)
                    dve.tensor_tensor(early[:, :], early[:, :], lg[:, :], ALU.mult).then_inc(s["step"], 1)
                    dve.wait_ge(s["step"], 5)
                    dve.tensor_scalar(pos[:, :], early[:, :], -1.0, None, ALU.add).then_inc(s["rows_ready"], 1)
            s.close()

        kb = c.sb(ctx, "l3_keys", [P, RH, NKV + 1])
        vm = c.sb(ctx, "l3_values", [P, RC])
        vl = c.sb(ctx, "l3_null_values", [RH, 2, RC])
        nk = c.sb(ctx, "null_keys", [P, PAIRS // B * 4])
        nv = c.sb(ctx, "null_values", [RH, GATES * RC])
        sel = c.wa[:, 0:2 * ST_ * (NQ + NKV)].rearrange("p (i t n) -> p i t n", i=2, t=ST_)
        back = c.sb(ctx, "chosen_back", [P, 2, S])
        posb = c.sb(ctx, "place_wide", [P, S])
        xq = c.sb(ctx, "chosen_queries", [P, KD, NQ])
        xk = c.sb(ctx, "chosen_keys", [P, KD, NKV])
        kvs = c.sb(ctx, "key_scores", [P, 1])
        osc = c.sb(ctx, "gate_out", [P, 2, D])
        pick = c.sb(ctx, "row_pick", [NR, 2, P])
        cnt = c.sb(ctx, "counts", [P, 4 * T])
        msk = c.sb(ctx, "picked_tok", [P, B, ST_, GATES])
        nul = c.sb(ctx, "null_wide", [P, D])
        m = AttentionMemory(c, ctx, a, "_r", {
            "osb": c.wa[:, 6144:6656], "ot": c.wa[:, 6656:7168].rearrange("p (k n) -> p k n", k=4)})
        acc = c.xnT[:, :, :].rearrange("p k n -> p (k n)")
        s = Sems(c, "nulls_loaded sel_ready gathered x_evac qkv_done kv_evac keys_ready wide_ready pos_evac back_ready scattered "
                    "summed finished pick_ready" + ATT + TAIL)

        def weights(i):
            w = c.wb[:, i % 2 * R_W:(i % 2 + 1) * R_W]
            return (w[:, 0:2 * RC].rearrange("p (k n) -> p k n", k=KD), w[:, 2 * RC:6 * RC].rearrange("p (k n) -> p k n", k=KD),
                    w[:, 6 * RC:6 * RC + 4 * D].rearrange("p (k n) -> p k n", k=4))

        def row(i):
            return i // GATES * 2 * GATES + i % GATES

        with c.nc.Block() as block:
            @block.sync
            def _(sp):
                sp.dma_start(nk[:, :], c.dram["L2_null_k"]).then_inc(s["nulls_loaded"], 16)
                sp.dma_start(nv[:, :], c.dram["L2_null_v"]).then_inc(s["nulls_loaded"], 16)
                sp.dma_start(nul[:, :], c.dram["L2_null_token"]).then_inc(s["nulls_loaded"], 16)
                for i in range(1, PAIRS):
                    if i >= 2:
                        sp.wait_ge(s["y_ready"], 2 * (i - 1))
                    sp.dma_start(c.wb[:, i % 2 * R_W:(i % 2 + 1) * R_W], c.dram["L2_gates"][i % GATES]).then_inc(c.wr_loaded[i % 2], 16)
                load_next(c, sp)

            @block.tensor
            def _(pe):
                def gather(i):
                    r, b = row(i), i // GATES
                    pe.wait_ge(s["sel_ready"], i + 1)
                    for kd in range(KD):
                        for n, w, at in ((0, NQ, 0), (1, NKV, NQ)):
                            for t in range(ST_):
                                src = c.xn[:, (b * ST_ + t) * D + kd * P:(b * ST_ + t) * D + (kd + 1) * P]
                                mm = pe.matmul(c.banks[TURN[n]][:, kd * w:(kd + 1) * w], src, sel[:, i % 2, t, at:at + w],
                                               start=(t == 0), stop=(t == ST_ - 1), skip_group_check=True)
                    for t in range(ST_):
                        mm = pe.matmul(c.banks[TURN[1]][:, 2 * NKV:2 * NKV + 1], sel[:, i % 2, t, NQ:NQ + NKV],
                                       sigT[:, t, r + GATES:r + GATES + 1], start=(t == 0), stop=(t == ST_ - 1), skip_group_check=True)
                    mm.then_inc(s["gathered"], 1)

                def qkv(i):
                    wq, wkv, _ = weights(i)
                    pe.wait_ge(c.wr_loaded[i % 2], 16 * (i // 2 + 1))
                    pe.wait_ge(s["x_evac"], i + 1)
                    if i:
                        pe.wait_ge(s["exped"], a.G * 2 * i)
                    for n in range(4):
                        for k in range(KD):
                            pe.matmul(c.banks[0][:, n * P:(n + 1) * P], wkv[:, k, n * P:(n + 1) * P], xk[:, k, :],
                                      start=(k == 0), stop=(k == KD - 1), skip_group_check=True)
                    for k in range(KD):
                        mm = pe.matmul(c.banks[1][:, :], xk[:, k, :], wkv[:, k, RC:2 * RC], start=(k == 0), stop=(k == KD - 1))
                    mm.then_inc(s["qkv_done"], 1)
                    for n in range(4):
                        for k in range(KD):
                            mm = pe.matmul(c.banks[TURN[n // 2]][:, n % 2 * NQ:(n % 2 + 1) * NQ], wq[:, k, n * P:(n + 1) * P],
                                           xq[:, k, :], start=(k == 0), stop=(k == KD - 1), skip_group_check=True)
                    mm.then_inc(s["qkv_done"], 1)

                def scatter(i):
                    pe.wait_ge(s["pick_ready"], i + 1)
                    pe.wait_ge(s["q_ready"], min(2 * (i + 2), 2 * PAIRS))
                    pe.wait_ge(s["finished"], 2 * i + 2)
                    for half in range(2):
                        for src, bank in ((pos, (3, 5)[half]), (sig, (4, 6)[half])):
                            mm = pe.matmul(c.banks[bank][:, :], pick[:, i % 2, :], src[:, half * CH:(half + 1) * CH], start=True, stop=True)
                    mm.then_inc(s["wide_ready"], 1)
                    pe.wait_ge(s["back_ready"], i + 1)
                    for f in range(ST_ // 2):
                        if f >= 2:
                            pe.wait_ge(s["summed"], 4 * i + f - 1)
                        for u in range(2):
                            t = 2 * f + u
                            for j in range(2):
                                mm = pe.matmul(c.banks[OB[1 - f % 2]][:, u * D:(u + 1) * D], back[:, j, t * P:(t + 1) * P], osc[:, j, :],
                                               start=(j == 0), stop=(j == 1), skip_group_check=True)
                        mm.then_inc(s["scattered"], 1)

                def finish(t):
                    att_finish_pe(c, pe, s, a, m, t // 2, t, lambda i, k: weights(i)[2][:, k, :], None)

                pe.wait_ge(s["nulls_loaded"], 48)
                for i in range(PAIRS):
                    gather(i)
                    if i:
                        finish(2 * i - 1)
                    qkv(i)
                    pe.wait_ge(s["keys_ready"], i + 1)
                    pe.wait_ge(s["kv_evac"], i + 1)
                    for p in range(2):
                        t = 2 * i + p
                        att_scores(c, pe, s, a, m, i, t, p, i == 0, lambda i, h, kk: kb[:, h, :])
                        if p == 0 and i:
                            scatter(i - 1)
                            pe.wait_ge(s["summed"], 4 * i)
                        if p == 1:
                            finish(t - 1)
                        att_turn(c, pe, s, a, m, t, p)
                        att_values(c, pe, s, a, m, i, t, p, lambda i, h: vm[:, h * RD:(h + 1) * RD], lambda i, g: vl[:, i % 2, :])
                finish(T - 1)
                scatter(PAIRS - 1)

            @block.scalar
            def _(act):
                def places(i):
                    act.wait_ge(s["wide_ready"], i + 1)
                    act.activation(posb[:, 0:CH], c.banks[3][:, :], ACT.Copy)
                    act.activation(posb[:, CH:S], c.banks[5][:, :], ACT.Copy).then_inc(s["pos_evac"], 1)

                for i in range(PAIRS):
                    act.wait_ge(s["gathered"], i + 1)
                    act.activation(xq[:, :, :], c.banks[TURN[0]][:, :], ACT.Copy)
                    act.activation(kvs[:, :], c.banks[TURN[1]][:, 2 * NKV:2 * NKV + 1], ACT.Copy)
                    act.activation(xk[:, :, :], c.banks[TURN[1]][:, 0:2 * NKV], ACT.Copy).then_inc(s["x_evac"], 1)
                    if i:
                        att_finish_act(c, act, s, a, m, 2 * i - 1)
                    act.wait_ge(s["qkv_done"], 2 * i + 1)
                    act.wait_ge(s["x_evac"], i + 1)
                    act.activation(vm[:, :], c.banks[1][:, :], ACT.Copy, scale=kvs[:, 0:1]).then_inc(s["kv_evac"], 1)
                    act.wait_ge(s["qkv_done"], 2 * i + 2)
                    for p in range(2):
                        for n in range(2):
                            of = c.banks[TURN[n]][:, :].rearrange("p (n t q) -> p n t q", n=2, t=2)
                            ins = act.activation(m.q[:, p, 2 * n:2 * n + 2, :], of[:, :, p, :], ACT.Copy)
                        ins.then_inc(s["q_ready"], 1)
                    for p in range(2):
                        t = 2 * i + p
                        att_exp(c, act, s, a, m, t, p)
                        if p == 0 and i:
                            places(i - 1)
                        if p == 1:
                            att_finish_act(c, act, s, a, m, t - 1)
                        att_evacuate(c, act, s, a, m, t, p)
                att_finish_act(c, act, s, a, m, T - 1)
                places(PAIRS - 1)

            @block.vector
            def _(dve):
                def choose(i):
                    r = row(i)
                    if i >= 2:
                        dve.wait_ge(s["gathered"], i - 1)
                    dve.tensor_tensor(vl[:, i % 2, :], nv[:, i % GATES * RC:(i % GATES + 1) * RC], c.const("diag8")[0:RH, :], ALU.mult)
                    if i >= 2:
                        dve.wait_ge(s["wide_ready"], i - 1)
                    dve.tensor_scalar(pick[:, i % 2, :], c.ones[0:NR, :], c.ident[0:NR, r:r + 1], None, ALU.mult).then_inc(s["pick_ready"], 1)
                    for t in range(ST_):
                        dve.tensor_scalar(sel[:, i % 2, t, 0:NQ], c.const("counting"), posT[:, t, r:r + 1], None, ALU.is_equal)
                        ins = dve.tensor_scalar(sel[:, i % 2, t, NQ:NQ + NKV], c.const("counting")[:, 0:NKV],
                                                posT[:, t, r + GATES:r + GATES + 1], None, ALU.is_equal)
                    ins.then_inc(s["sel_ready"], 1)

                def keys(i):
                    dve.wait_ge(s["qkv_done"], 2 * i + 1)
                    if i:
                        dve.wait_ge(s["scores_ready"], a.G * 2 * i)
                    for e in range(2):
                        scale = c.const("heads64")[:, e:e + 1]
                        dve.tensor_scalar(kb[:, e::2, 0:NKV], c.banks[0][:, :].rearrange("p (n k) -> p n k", n=4), scale, None, ALU.mult)
                        ins = dve.tensor_scalar(kb[:, e::2, NKV], nk[:, i % GATES * 4:(i % GATES + 1) * 4], scale, None, ALU.mult)
                    ins.then_inc(s["keys_ready"], 1)

                def send_back(i):
                    dve.wait_ge(s["pos_evac"], i + 1)
                    for half in range(2):
                        for j in range(2):
                            ins = dve.scalar_tensor_tensor(out=back[:, j, half * CH:(half + 1) * CH], in0=posb[:, half * CH:(half + 1) * CH],
                                                           scalar=c.const("places")[:, j:j + 1], in1=c.banks[(4, 6)[half]][:, :],
                                                           op0=ALU.is_equal, op1=ALU.mult)
                    ins.then_inc(s["back_ready"], 1)
                    for f in range(ST_ // 2):
                        dve.wait_ge(s["scattered"], 4 * i + f + 1)
                        at = (i // GATES * ST_ + 2 * f) * D
                        to = acc[:, at:at + 2 * D]
                        src = c.banks[OB[1 - f % 2]][:, :]
                        if i % GATES == 0:
                            dve.tensor_copy(to, src).then_inc(s["summed"], 1)
                        else:
                            if f == 0:
                                dve.wait_ge(s["summed"], 4 * i)
                            dve.tensor_tensor(to, to, src, ALU.add).then_inc(s["summed"], 1)

                def finish(t):
                    dve.wait_ge(s["y_ready"], t + 1)
                    if t >= 2:
                        dve.wait_ge(s["scattered"], 4 * (t // 2))
                    dve.tensor_copy(osc[:, t % 2, :], c.banks[YB][:, 0:D]).then_inc(s["finished"], 1)

                dve.wait_ge(s["nulls_loaded"], 48)
                choose(0)
                for i in range(PAIRS):
                    if i:
                        finish(2 * i - 1)
                    keys(i)
                    for p in range(2):
                        t = 2 * i + p
                        att_max(c, dve, s, a, m, i, t, p, None)
                        if p == 0 and i:
                            send_back(i - 1)
                        if p == 1:
                            finish(t - 1)
                            if i + 1 < PAIRS:
                                choose(i + 1)
                        att_normalise(c, dve, s, a, m, t, p)
                finish(T - 1)
                send_back(PAIRS - 1)

            @block.gpsimd
            def _(pool):
                for t in range(T):
                    pool.wait_ge(s["exped"], a.G * (t + 1))
                    pool.tensor_copy(m.pl[:, t % 2, :].rearrange("p (h k) -> p h k", k=a.NL),
                                     m.p[:, t % 2, :, P:a.NK]).then_inc(s["last_ready"], 1)
        s.close()

        s = Sems(c, "step mean_done null_added" + TAIL)
        n_, inv, zero = cnt[:, 0:T], cnt[:, T:2 * T], cnt[:, 2 * T:3 * T]
        with c.nc.Block() as block:
            @block.vector
            def _(dve):
                for b in range(B):
                    dve.tensor_scalar(msk[:, b, :, :], posT[:, :, b * 2 * GATES:b * 2 * GATES + GATES], 0.0, None,
                                      ALU.is_ge).then_inc(s["step"], 1)
                dve.wait_ge(s["step"], 2)
                dve.tensor_reduce(n_, msk[:, :, :, :].rearrange("p b t g -> p (b t) g"), AX.X, ALU.add).then_inc(s["step"], 1)
                dve.wait_ge(s["step"], 3)
                dve.tensor_scalar(inv, n_, 1e-5, None, ALU.max).then_inc(s["step"], 1)
                dve.tensor_scalar(zero, n_, 0.0, None, ALU.is_equal).then_inc(s["step"], 1)
                dve.wait_ge(s["step"], 5)
                dve.reciprocal(inv, inv).then_inc(s["step"], 1)
                dve.wait_ge(s["step"], 6)
                dve.sem_inc(s["y_ready"], T)

                def pair(i, first):
                    for p in range(2):
                        t = 2 * i + p
                        y = tok(acc, t)
                        one_of = (lambda v: v[:, t:t + 1]) if isinstance(t, int) else (lambda v: v[:, bass.ds(t, 1)])
                        dve.tensor_scalar(y, y, one_of(inv), None, ALU.mult).then_inc(s["mean_done"], 1)
                        dve.wait_ge(s["mean_done"], t + 1)
                        dve.scalar_tensor_tensor(out=y, in0=nul[:, :], scalar=one_of(zero), in1=y,
                                                 op0=ALU.mult, op1=ALU.add).then_inc(s["null_added"], 1)
                        dve.wait_ge(s["null_added"], t + 1)
                        tail_dve(c, dve, s, t, p, first, y, 5)
                pairs(dve, pair)

            @block.gpsimd
            def _(pool):
                tail_pool_all(c, pool, s)
        s.close()



L3X = Heads(H=1, DH=D, NK=M, HG=1, QB=KD)


def load_l3x(c, sp):
    v = c.dram["ctx_tok"].rearrange("(b m) d -> m b d", b=B)
    c.load_a(sp, c.wa[:, 7168:7680].rearrange("p (b d) -> p b d", b=B), v[0:P])
    c.load_a(sp, c.wa[0:ML, 7680:8192].rearrange("p (b d) -> p b d", b=B), v[P:M])


def layer3_attention(c, load_next):
    a = L3X
    vm, vl = c.wa[:, 7168:7680], c.wa[:, 7680:8192]
    with ExitStack() as ctx:
        kb = c.sb(ctx, "ctx_sixteenth", [P, KD, B * M])
        m = AttentionMemory(c, ctx, a, "_l3")
        s = Sems(c, "keys_scaled" + ATT + TAIL)
        with c.nc.Block() as block:
            @block.vector
            def _(dve):
                dve.tensor_scalar(kb[:, :, :], c.ctxT[:, :, :], float(D) ** -0.5, None, ALU.mult).then_inc(s["keys_scaled"], 1)

            @block.tensor
            def _(pe):
                pe.wait_ge(s["keys_scaled"], 1)
                pe.wait_ge(c.wa_loaded, c.wa_count)
        s.close()
        s = Sems(c, ATT + TAIL)
        with c.nc.Block() as block:
            @block.sync
            def _(sp):
                load_next(c, sp)

            def at(i, size, o, n):
                return slice(o, o + n) if isinstance(i, int) else bass.ds(i // (T // 4) * size + o, n)

            attention(c, block, s, a, m, Parts(
                q_pe=None, q_act=None, stage=stage_tile(c, s, a, m, c.xnT), mask=None, project=None,
                keys=lambda i, h, kk: kb[:, kk, at(i, M, 0, M)],
                values=lambda i, h: vm[:, at(i, D, 0, D)],
                left=lambda i, g: vl[0:ML, at(i, D, 0, D)],
                finish_dve=lambda dve, t, p, first: tail_dve(c, dve, s, t, p, first, m.osb[:, :], 6, s["osb_ready"]),
                finish_pool=lambda pool, t, p: tail_pool(c, pool, s, t, p)))
        s.close()



INNER = 704
IB = -(-INNER // P)
IL = INNER - (IB - 1) * P
ROUND = 1.5 * 2.0 ** 23
QMAX = 127.0


def block_rows(m):
    return P if m < IB - 1 else IL


def load_l3f(c, sp):
    w, n = c.wb, IB * D
    for j, src in enumerate((c.dram["L3_ffn_w_gate"], c.dram["L3_ffn_w_up"])):
        full = (IB - 1) * P
        c.load_b(sp, w[:, j * n:j * n + (IB - 1) * D].rearrange("p (k n) -> p k n", k=IB - 1), rows(src[0:full], IB - 1))
        c.load_b(sp, w[0:IL, j * n + (IB - 1) * D:(j + 1) * n], src[full:INNER])
    c.load_b(sp, w[:, 2 * n:2 * n + KD * INNER].rearrange("p (k n) -> p k n", k=KD), rows(c.dram["L3_ffn_w_down"], KD))


def layer3_quantised(c, load_next):
    n_g = IB * D
    nat = [c.wb[:, 0:n_g].rearrange("p (k n) -> p k n", k=IB), c.wb[:, n_g:2 * n_g].rearrange("p (k n) -> p k n", k=IB),
           c.wb[:, 2 * n_g:2 * n_g + KD * INNER].rearrange("p (k n) -> p k n", k=KD)]
    hv = c.wa[:, :].rearrange("p (m n) -> p m n", n=B * S)
    hx = c.xn[:, :].rearrange("p (m n) -> p m n", n=B * S)

    def hidden(m, cols):
        return hv[0:block_rows(m), m, cols] if m < 4 else hx[0:block_rows(m), m - 4, cols]

    with ExitStack() as ctx:
        xi = c.sb(ctx, "x_whole", [P, KD, B * S], BF16)
        wgu = c.sb(ctx, "gate_up_whole", [P, 2, KD, INNER], BF16)
        wd = c.sb(ctx, "down_whole", [P, IB, D], BF16)
        most = c.sb(ctx, "row_most", [P, 16])
        ws = c.sb(ctx, "row_scales", [P, 16])
        winv = c.sb(ctx, "row_inverses", [P, 16])
        sc = c.sb(ctx, "scales", [P, 12])
        clip = c.sb(ctx, "clips", [P, 2])
        one = c.sb(ctx, "most_one", [1, 2])
        downs = c.sb(ctx, "down_scales_wide", [P, D])
        sx, ix, sh, ih, sig = sc[:, 0:1], sc[:, 1:2], sc[:, 2:3], sc[:, 3:4], sc[:, 4:6]

        with ExitStack() as prep:
            wi = [c.sb(prep, "gate_whole_rows", [P, IB, D], BF16), c.sb(prep, "up_whole_rows", [P, IB, D], BF16),
                  c.sb(prep, "down_whole_rows", [P, KD, INNER], BF16)]
            ib = c.sb(prep, "ident_whole", [P, P], BF16)
            dg = c.sb(prep, "down_diag", [P, KD, P])
            s = Sems(c, "clips_loaded sig_done zeroed ident_copied reduced scaled column_up row_most column_down x_scaled rounded "
                        "whole turned evac gate_dve diag down_wide")
            parts = [(0, P, 0, IB - 1), (0, IL, IB - 1, 1), (1, P, 0, IB - 1), (1, IL, IB - 1, 1), (2, P, 0, KD)]
            with c.nc.Block() as block:
                @block.sync
                def _(sp):
                    sp.dma_start(clip[:, :], c.dram["L3_clips"]).then_inc(s["clips_loaded"], 16)

                @block.gpsimd
                def _(pool):
                    pool.tensor_copy(ib[:, :], c.ident[:, :]).then_inc(s["ident_copied"], 1)

                @block.tensor
                def _(pe):
                    pe.wait_ge(s["reduced"], 1)
                    pe.transpose(c.banks[7][0:1, 0:P], most[:, 14:15], c.ident[:, :]).then_inc(s["column_up"], 1)
                    pe.wait_ge(s["row_most"], 1)
                    pe.matmul(c.banks[7][:, 256:257], c.ones[0:1, :], one[0:1, 0:1], start=True, stop=True).then_inc(s["column_down"], 1)
                    pe.wait_ge(s["diag"], KD)
                    for k in range(KD):
                        mm = pe.matmul(c.banks[6][:, k * P:(k + 1) * P], c.ones[:, :], dg[:, k, :], start=True, stop=True,
                                       skip_group_check=True)
                    mm.then_inc(s["down_wide"], 1)
                    pe.wait_ge(s["ident_copied"], 1)
                    for n in range(4):
                        j, k = n // KD, n % KD
                        pe.wait_ge(s["whole"], 2 * j + 2)
                        if n >= 2:
                            pe.wait_ge(s["evac"], 2 * (n - 1))
                        for m in range(IB):
                            r = block_rows(m)
                            mm = pe.matmul(c.banks[n % 2 * 2 + m // 4][:, m % 4 * P:m % 4 * P + r], wi[j][0:r, m, k * P:(k + 1) * P],
                                           ib[0:r, 0:r], start=True, stop=True, skip_group_check=True)
                        mm.then_inc(s["turned"], 1)
                    pe.wait_ge(s["whole"], 5)
                    for m in range(IB):
                        if m == 0:
                            pe.wait_ge(s["evac"], 8)
                        r = block_rows(m)
                        for k in range(KD):
                            mm = pe.matmul(c.banks[m // 2][0:r, m % 2 * D + k * P:m % 2 * D + (k + 1) * P], wi[2][:, k, m * P:m * P + r],
                                           ib[:, :], start=True, stop=True, skip_group_check=True)
                    mm.then_inc(s["turned"], 1)

                @block.scalar
                def _(act):
                    act.wait_ge(s["clips_loaded"], 16)
                    act.activation(sig, clip[:, :], ACT.Sigmoid).then_inc(s["sig_done"], 1)
                    for n, (j, r, m, k) in enumerate(parts):
                        act.wait_ge(s["rounded"], 2 * (n + 1))
                        act.activation(wi[j][0:r, m:m + k, :], nat[j][0:r, m:m + k, :], ACT.Identity, bias=c.unround[0:r, :]).then_inc(s["whole"], 1)
                    act.wait_ge(s["rounded"], 2 * len(parts) + 2 * 2)
                    for k in range(KD):
                        act.activation(xi[:, k, :], c.xnT[:, k, :], ACT.Identity, bias=c.unround)
                    for n in range(4):
                        act.wait_ge(s["turned"], n + 1)
                        to = wgu[:, n // KD, n % KD, :]
                        act.activation(to[:, 0:512], c.banks[n % 2 * 2][:, :], ACT.Copy).then_inc(s["evac"], 1)
                        act.activation(to[:, 512:INNER], c.banks[n % 2 * 2 + 1][:, 0:INNER - 512], ACT.Copy).then_inc(s["evac"], 1)
                    act.wait_ge(s["turned"], 5)
                    for m in range(IB):
                        r = block_rows(m)
                        act.activation(wd[0:r, m, :], c.banks[m // 2][0:r, m % 2 * D:(m % 2 + 1) * D], ACT.Copy)

                @block.vector
                def _(dve):
                    dve.memset(most[:, :], 1.0).then_inc(s["zeroed"], 1)
                    dve.wait_ge(s["zeroed"], 1)
                    dve.tensor_reduce(most[:, 14:15], c.xn[:, :], AX.X, ALU.max, apply_absolute_value=True).then_inc(s["reduced"], 1)
                    dve.wait_ge(c.wb_loaded, c.wb_count)
                    for j, r, m, k in parts:
                        ins = dve.tensor_reduce(most[0:r, 6 * j + m:6 * j + m + k], nat[j][0:r, m:m + k, :], AX.X, ALU.max,
                                                apply_absolute_value=True)
                        ins.then_inc(s["reduced"], 1)
                    dve.wait_ge(s["reduced"], 1 + len(parts))
                    dve.tensor_scalar(ws[:, :], most[:, :], 1.0 / QMAX, None, ALU.mult).then_inc(s["scaled"], 1)
                    dve.wait_ge(s["scaled"], 1)
                    dve.reciprocal(winv[:, :], ws[:, :]).then_inc(s["scaled"], 1)
                    for k in range(KD):
                        dve.tensor_scalar(dg[:, k, :], c.ident[:, :], ws[:, 12 + k:13 + k], None, ALU.mult).then_inc(s["diag"], 1)
                    dve.wait_ge(s["column_up"], 1)
                    dve.tensor_reduce(one[0:1, 0:1], c.banks[7][0:1, 0:P], AX.X, ALU.max).then_inc(s["row_most"], 1)
                    dve.wait_ge(s["scaled"], 2)
                    done = 0

                    def whole(v, inv):
                        nonlocal done
                        dve.tensor_scalar(v, v, inv, ROUND, ALU.mult, ALU.add).then_inc(s["rounded"], 1)
                        dve.wait_ge(s["rounded"], done + 1)
                        dve.tensor_scalar(v, v, ROUND + QMAX, ROUND - QMAX - 1.0, ALU.min, ALU.max).then_inc(s["rounded"], 1)
                        done += 2

                    for j, r, m, k in parts:
                        v = nat[j][0:r, m:m + k, :]
                        w = winv[0:r, 6 * j + m:6 * j + m + k].unsqueeze(2).broadcast_to(list(v.shape))
                        dve.tensor_tensor(v, v, w, ALU.mult).then_inc(s["x_scaled"], 1)
                        dve.wait_ge(s["x_scaled"], parts.index((j, r, m, k)) + 1)
                        whole(v, 1.0)
                    dve.wait_ge(s["column_down"], 1)
                    dve.wait_ge(s["sig_done"], 1)
                    n = len(parts)
                    dve.scalar_tensor_tensor(out=sx, in0=c.banks[7][:, 256:257], scalar=1.0 / QMAX, in1=sig[:, 0:1],
                                             op0=ALU.mult, op1=ALU.mult).then_inc(s["x_scaled"], 1)
                    dve.wait_ge(s["x_scaled"], n + 1)
                    dve.reciprocal(ix, sx).then_inc(s["x_scaled"], 1)
                    dve.wait_ge(s["x_scaled"], n + 2)
                    for k in range(KD):
                        whole(c.xnT[:, k, :], ix)
                    dve.tensor_scalar(ws[:, 0:12], ws[:, 0:12], sx, None, ALU.mult)
                    dve.wait_ge(s["down_wide"], 1)
                    dve.tensor_copy(downs[:, :], c.banks[6][:, 0:D])
            s.close()

        sg = c.sb(ctx, "silu3", [P, 3, CH])
        hm = c.sb(ctx, "hidden_most", [P, IB * NC])
        hi = c.sb(ctx, "hidden_whole", [P, 2, IB, CH], BF16)
        yb = c.sb(ctx, "scaled_out", [P, 2, D])
        s = Sems(c, "gate_up_ready silu_done h_ready zeroed most_ready column_up row_most column_down scaled gate_pe gate_act gate_dve")
        with c.nc.Block() as block:
            @block.tensor
            def _(pe):
                with pe.Fori(0, NC) as i:
                    for m in range(IB):
                        r, n = block_rows(m), i * IB + m
                        held(pe, s["h_ready"], n + 1, s["gate_pe"])
                        for j in range(2):
                            for k in range(KD):
                                mm = pe.matmul(c.banks[3 * j + m % 3][0:r, :], wgu[:, j, k, m * P:m * P + r],
                                               xi[:, k, bass.ds(i * CH, CH)], start=(k == 0), stop=(k == KD - 1))
                        mm.then_inc(s["gate_up_ready"], 1)
                pe.wait_ge(s["most_ready"], NC + 1)
                pe.transpose(c.banks[7][0:1, 0:P], most[:, 15:16], c.ident[:, :]).then_inc(s["column_up"], 1)
                pe.wait_ge(s["row_most"], 1)
                pe.matmul(c.banks[7][:, 256:257], c.ones[0:1, :], one[0:1, 1:2], start=True, stop=True).then_inc(s["column_down"], 1)

            @block.scalar
            def _(act):
                with act.Fori(0, NC) as i:
                    for m in range(IB):
                        r, n = block_rows(m), i * IB + m
                        held(act, s["h_ready"], n + 1, s["gate_act"])
                        act.wait_ge(s["gate_up_ready"], n + 1)
                        act.activation(sg[0:r, m % 3, :], c.banks[m % 3][0:r, :], ACT.Silu, scale=ws[0:r, m:m + 1]).then_inc(s["silu_done"], 1)

            @block.vector
            def _(dve):
                dve.memset(hm[:, :], 0.0).then_inc(s["zeroed"], 1)
                dve.wait_ge(s["zeroed"], 1)
                dve.sem_inc(s["h_ready"], 3)
                with dve.Fori(0, NC) as i:
                    for m in range(IB):
                        r, n = block_rows(m), i * IB + m
                        held(dve, s["silu_done"], n + 1, s["gate_dve"])
                        dve.scalar_tensor_tensor(out=hidden(m, bass.ds(i * CH, CH)), in0=c.banks[3 + m % 3][0:r, :],
                                                 scalar=ws[0:r, 6 + m:7 + m], in1=sg[0:r, m % 3, :],
                                                 op0=ALU.mult, op1=ALU.mult).then_inc(s["h_ready"], 1)
                    held(dve, s["h_ready"], (i + 1) * IB + 3, s["gate_dve"])
                    for v, at, r in ((hv[:, :, bass.ds(i * CH, CH)], 0, P), (hx[:, 0:1, bass.ds(i * CH, CH)], 4, P),
                                     (hx[0:IL, 1:2, bass.ds(i * CH, CH)], 5, IL)):
                        n = v.shape[1]
                        ins = dve.tensor_reduce(hm[0:r, bass.ds(i * IB + at, n)], v, AX.X, ALU.max, apply_absolute_value=True)
                    ins.then_inc(s["most_ready"], 1)
                dve.wait_ge(s["most_ready"], NC)
                dve.tensor_reduce(most[:, 15:16], hm[:, :], AX.X, ALU.max).then_inc(s["most_ready"], 1)
                dve.wait_ge(s["column_up"], 1)
                dve.tensor_reduce(one[0:1, 1:2], c.banks[7][0:1, 0:P], AX.X, ALU.max).then_inc(s["row_most"], 1)
                dve.wait_ge(s["column_down"], 1)
                dve.scalar_tensor_tensor(out=sh, in0=c.banks[7][:, 256:257], scalar=1.0 / QMAX, in1=sig[:, 1:2],
                                         op0=ALU.mult, op1=ALU.mult).then_inc(s["scaled"], 1)
                dve.wait_ge(s["scaled"], 1)
                dve.reciprocal(ih, sh).then_inc(s["scaled"], 1)
                dve.tensor_scalar(downs[:, :], downs[:, :], sh, c.tg[:, 7:8], ALU.mult, ALU.mult).then_inc(s["scaled"], 1)
        s.close()

        s = Sems(c, "clipped whole downed scaled_y stored x_done gate_pe gate_act gate_dve")
        with c.nc.Block() as block:
            @block.sync
            def _(sp):
                for i in range(NC):
                    sp.wait_ge(s["x_done"], 4 * (i + 1))
                    sp.dma_start(c.out[:, 4 * i:4 * i + 4, :], c.x[:, 4 * i * D:(4 * i + 4) * D].rearrange("p (t d) -> p t d", d=D)).then_inc(s["stored"], 16)
                sp.wait_ge(s["stored"], 16 * NC)

            def both(i):
                cols = slice(i * CH, (i + 1) * CH)
                return ((hv[:, :, cols], 0, 4), (hx[:, :, cols], 4, 6))

            @block.vector
            def _(dve):
                def whole(i):
                    for q, (v, lo, hi_) in enumerate(both(i)):
                        dve.tensor_scalar(v, v, ih, ROUND, ALU.mult, ALU.add).then_inc(s["clipped"], 1)
                        dve.wait_ge(s["clipped"], 4 * i + 2 * q + 1)
                        dve.tensor_scalar(v, v, ROUND + QMAX, ROUND - QMAX - 1.0, ALU.min, ALU.max).then_inc(s["clipped"], 1)

                whole(0)
                for i in range(NC):
                    if i + 1 < NC:
                        whole(i + 1)
                    for tt in range(4):
                        t = 4 * i + tt
                        dve.wait_ge(s["downed"], t + 1)
                        dve.tensor_tensor(yb[:, t % 2, :], c.banks[t % 8][:, 0:D], downs[:, :], ALU.mult).then_inc(s["scaled_y"], 1)
                        dve.wait_ge(s["scaled_y"], t + 1)
                        dve.tensor_tensor(tok(c.x, t), tok(c.x, t), yb[:, t % 2, :], ALU.add).then_inc(s["x_done"], 1)

            @block.scalar
            def _(act):
                for i in range(NC):
                    act.wait_ge(s["clipped"], 4 * (i + 1))
                    if i >= 2:
                        act.wait_ge(s["downed"], 4 * (i - 1))
                    for v, lo, hi_ in both(i):
                        act.activation(hi[:, i % 2, lo:hi_, :], v, ACT.Identity, bias=c.unround).then_inc(s["whole"], 1)

            @block.tensor
            def _(pe):
                for i in range(NC):
                    pe.wait_ge(s["whole"], 2 * (i + 1))
                    for tt in range(4):
                        t = 4 * i + tt
                        if t >= 8:
                            pe.wait_ge(s["scaled_y"], t - 7)
                        for m in range(IB):
                            r = block_rows(m)
                            mm = pe.matmul(c.banks[t % 8][:, 0:D], hi[0:r, i % 2, m, tt * P:(tt + 1) * P], wd[0:r, m, :],
                                           start=(m == 0), stop=(m == IB - 1))
                        mm.then_inc(s["downed"], 1)
        s.close()



def program(nc, dram, out, layers):
    with ExitStack() as ctx:
        c = Core(nc, ctx, dram)
        c.out = out.rearrange("b (t p) d -> p (b t) d", p=P)
        phase_setup(c)
        steps = [(layer0_attention, load_l0x), (layer0_experts, load_l0f), (layer1_slots, load_l1x), (layer1_experts, load_l1f),
                 (layer2_attention, load_l2x), (layer2_routed, load_l2f), (layer3_attention, load_l3x), (layer3_quantised, load_l3f)]
        todo = steps[:layers]
        for n, (layer, load) in enumerate(todo):
            transpose_xn(c, (lambda sp, load=load: load(c, sp)) if n == 0 else None)
            nxt = todo[n + 1][1] if n + 1 < len(todo) else (lambda c, sp: None)
            layer(c, nxt)
        if layers == len(steps):
            return
        s = Sems(c, "stored")
        with nc.Block() as block:
            @block.sync
            def _(sp):
                sp.dma_start(c.out,
                             c.x[:, :].rearrange("p (t d) -> p t d", d=D)).then_inc(s["stored"], 16)
                sp.wait_ge(s["stored"], 16)


def col(v):
    return np.ascontiguousarray(v.reshape(-1, P).T)


def layouts(i):
    f = np.float32
    p = np.arange(P)
    consts = {
        "centre16": np.eye(P, dtype=f) - (p[:, None] // 16 == p[None, :] // 16).astype(f) / f(16),
        "average16": (p[:, None] // 16 == p[None, :] // 16).astype(f) / f(16),
        "heads16": (p[:, None] // 16 == np.arange(8)[None, :]).astype(f) * f(0.25),
        "heads64": (p[:, None] // 64 == np.arange(2)[None, :]).astype(f) * f(0.125),
        "left16": (p[:, None] // 26 == np.arange(64)[None, :] // 16).astype(f),
        "left64": (p[:, None] // 26 == np.arange(256)[None, :] // 64).astype(f),
        "mean256": np.full((P, P), 1 / 256, f),
        "ln1g": col(i["L1_ffn_ln1_g"]), "ln1b": col(i["L1_ffn_ln1_b"]),
        "ln2g": col(i["L1_ffn_ln2_g"]), "ln2b": col(i["L1_ffn_ln2_b"]),
        "slotw": col(i["L1_xattn_slot_norm_w"]), "inw": col(i["L1_xattn_input_norm_w"]),
        "bih": col(i["L1_xattn_gru_bih"]), "bhh": col(i["L1_xattn_gru_bhh"]),
        "counting": np.broadcast_to(np.arange(NQ, dtype=f), (P, NQ)),
        "places": np.stack([p, p + P], 1),
        "diag8": (p[:, None] == np.arange(RC)[None, :] // RD),
        "query_rows": (p[:, None] % 8 < 4), "key_rows": (p[:, None] % 8 >= 4),
        "falling": np.broadcast_to(32 - np.arange(16, dtype=f), (P, 16)),
        "pairs16": (p[:, None] == np.arange(N_R * MID_R)[None, :] // MID_R).astype(f),
        "bq0": col(i["L0_xattn_bq"])[:, 0:1], "bq1": col(i["L0_xattn_bq"])[:, 1:2],
        "bk0": col(i["L0_xattn_bkv"])[:, 0:1], "bk1": col(i["L0_xattn_bkv"])[:, 1:2],
        "qgam": np.tile(i["L0_xattn_q_gamma"], 8)[:, None], "qbet": np.tile(i["L0_xattn_q_beta"], 8)[:, None],
        "kgam": np.tile(i["L0_xattn_k_gamma"], 8)[:, None], "kbet": np.tile(i["L0_xattn_k_beta"], 8)[:, None],
    }
    vrows = {
        "bv": i["L0_xattn_bkv"][D:], "L0_xattn_bproj": i["L0_xattn_bproj"],
        "L2_xattn_b_out": i["L2_xattn_b_out"],
    }
    a = {
        "x": i["x"].reshape(B * S, D),
        "ctxT": i["ctx_1024"].transpose(2, 0, 1).reshape(D, B * M),
        "ctx_tok": i["ctx_1024"].reshape(B * M, D),
        "L3_ffn_w_gate": i["L3_ffn_w_gate"], "L3_ffn_w_up": i["L3_ffn_w_up"], "L3_ffn_w_down": i["L3_ffn_w_down"],
        "L3_clips": np.broadcast_to(np.stack([i["L3_ffn_clip_x"], i["L3_ffn_clip_down"]], 1), (P, 2)),
        "ident": np.eye(P, dtype=f),
        "gates": np.broadcast_to(np.stack([i["g_xattn"], i["g_ffn"]], 1).reshape(1, 8), (P, 8)),
        "L0_xattn_Wq": i["L0_xattn_Wq"], "L0_xattn_Wkv": i["L0_xattn_Wkv"],
        "L0_WvT": i["L0_xattn_Wkv"][D:].T, "L0_WprojT": i["L0_xattn_Wproj"].T,
    }
    wide = lambda r, sh: np.concatenate([r.transpose(1, 0, 2).reshape(D, -1), sh.transpose(1, 0, 2).reshape(D, -1)], 1)
    a["L0_gates"] = wide(i["L0_ffn_wg_r"], i["L0_ffn_wg_s"])
    a["L0_ups"] = wide(i["L0_ffn_wu_r"], i["L0_ffn_wu_s"])
    a["L0_downs"] = np.concatenate([i["L0_ffn_wd_r"].reshape(-1, D), i["L0_ffn_wd_s"].reshape(-1, D)], 0)
    a["L0_ffn_router_w"] = i["L0_ffn_router_w"]
    a["L1_xattn_Wq"] = i["L1_xattn_Wq"]
    a["L1_WkT"], a["L1_WvT"] = i["L1_xattn_Wk"].T, i["L1_xattn_Wv"].T
    a["L1_wihT"], a["L1_whhT"] = i["L1_xattn_gru_wih"].T, i["L1_xattn_gru_whh"].T
    a["L1_attnT"], a["L1_gateT"] = i["L1_ffn_attn_w"].T, i["L1_ffn_gate_w"].T
    side = lambda w: w.reshape(N_E, -1, P, w.shape[2]).transpose(0, 2, 1, 3).reshape(N_E, P, -1)
    a["L1_experts"] = np.concatenate([side(i["L1_ffn_gate_proj"].transpose(0, 2, 1)), side(i["L1_ffn_up_proj"].transpose(0, 2, 1)),
                                      side(i["L1_ffn_down_proj"].transpose(0, 2, 1))], 2)
    a["mask"] = np.broadcast_to(i["mask_BxS2_bf1"].view(np.uint8).reshape(1, B * M), (P, B * M))
    a["L2_WqT"], a["L2_WkT"], a["L2_WvT"] = i["L2_xattn_Wq"].T, i["L2_xattn_Wkv"][:1024].T, i["L2_xattn_Wkv"][1024:].T
    a["L2_WoutT"] = i["L2_xattn_Wout"].T
    rt = np.concatenate([i["L2_ffn_w_qr"], i["L2_ffn_w_kvr"]], 0).T
    none = np.zeros_like(rt)
    a["L2_routing"] = np.stack([np.concatenate([rt, none], 1), np.concatenate([none, rt], 1)], 1)
    side4 = lambda w: w.reshape(GATES, -1, P, w.shape[2]).transpose(0, 2, 1, 3).reshape(GATES, P, -1)
    a["L2_gates"] = np.concatenate([side4(i["L2_ffn_w_q"].transpose(0, 2, 1)), side4(i["L2_ffn_w_kv"].transpose(0, 2, 1)),
                                    side4(i["L2_ffn_w_out"].transpose(0, 2, 1))], 2)
    a["L2_null_k"] = i["L2_ffn_null_kv"][0].reshape(GATES * 4, P).T
    a["L2_null_v"] = np.broadcast_to(i["L2_ffn_null_kv"][1].reshape(1, GATES * RC), (RH, GATES * RC))
    a["L2_null_token"] = np.broadcast_to(i["L2_ffn_null_token"].reshape(1, D), (P, D))
    const_at, vrow_at, n = {}, {}, 0
    for k, v in consts.items():
        const_at[k] = (n, v.shape[1])
        n += v.shape[1]
    a["consts"] = np.concatenate([v.astype(f) for v in consts.values()], 1)
    n = 0
    for k, v in vrows.items():
        vrow_at[k] = (n, v.size)
        n += v.size
    a["vrows"] = np.concatenate([v.reshape(1, -1) for v in vrows.values()], 1)
    return {k: np.ascontiguousarray(v) for k, v in a.items()}, const_at, vrow_at


def kernel(**inputs):
    import concourse.bacc as bacc
    from concourse.bass_utils import run_bass_kernel_spmd

    arrays, const_at, vrow_at = layouts({k: np.asarray(v) for k, v in inputs.items()})
    nc = bacc.Bacc("TRN2", target_bir_lowering=False, num_devices=1)
    dram = {"const_at": const_at, "vrow_at": vrow_at}
    for name, v in arrays.items():
        dram[name] = nc.dram_tensor(f"in_{name}", v.shape, mybir.dt.from_np(v.dtype), kind="ExternalInput").ap()
    out = nc.dram_tensor("out_x", (B, S, D), F32, kind="ExternalOutput").ap()
    program(nc, dram, out, STOP)
    r = run_bass_kernel_spmd(nc, [{f"in_{k}": v for k, v in arrays.items()}], core_ids=[0])
    return r.results[0]["out_x"]
```

```python
from contextlib import ExitStack

import numpy as np

import concourse.bass as bass
from concourse import mybir

F32 = mybir.dt.float32
BF16 = mybir.dt.bfloat16
F32R = mybir.dt.float32r
U8 = mybir.dt.uint8
U32 = mybir.dt.uint32
ALU = mybir.AluOpType
ACT = mybir.ActivationFunctionType
AX = mybir.AxisListType
RMAX = bass.bass_isa.ReduceOp.max

P = 128
B, S, D = 2, 1024, 256
KD = D // P
T = B * S // P
TB = T // B
CH = 512
NC = B * S // CH
M = 154
ML = M - P
LN_EPS = 1e-5
ROUND = 1.5 * 2.0 ** 23


def rows(ap, k):
    return ap.rearrange("(k p) n -> p k n", p=P)


class Core:

    def __init__(self, nc, ctx, dram):
        self.nc, self.ctx, self.dram = nc, ctx, dram
        sb = self.sb
        self.x = sb(ctx, "x_tok", [P, T * D])
        self.xn = sb(ctx, "xn_tok", [P, T * D])
        self.xnT = sb(ctx, "xn_feat", [P, KD, B * S])
        self.ident = sb(ctx, "ident", [P, P])
        self.ones = sb(ctx, "ones", [P, P])
        self.small = sb(ctx, "small", [P, 8])
        self.tg = sb(ctx, "tanh_gates", [P, 8])
        self.stats = sb(ctx, "stats", [P, T, 8])
        self.ctxT = sb(ctx, "ctx_feat", [P, KD, B * M])
        self.wa = sb(ctx, "weights_a", [P, 8192])
        self.wb = sb(ctx, "weights_b", [P, 8192])
        self.eps = self.small[:, 0:1]
        self.neg_half = self.small[:, 1:2]
        self.eps6 = self.small[:, 2:3]
        self.unround = self.small[:, 3:4]
        self.ctxR = sb(ctx, "ctx_last_repeated", [P, KD, B, 4 * ML])
        self.consts = sb(ctx, "consts", [P, dram["consts"].shape[1]])
        self.vrows = sb(ctx, "vrows", [1, dram["vrows"].shape[1]])
        self.banks = [ctx.enter_context(nc.psum_tensor(f"bank{i}", [P, 512], F32)) for i in range(8)]
        self.wa_loaded = ctx.enter_context(nc.semaphore("wa_loaded"))
        self.wb_loaded = ctx.enter_context(nc.semaphore("wb_loaded"))
        self.we_loaded = [ctx.enter_context(nc.semaphore(f"expert_loaded{n}")) for n in range(2)]
        self.wr_loaded = [ctx.enter_context(nc.semaphore(f"gate_loaded{n}")) for n in range(2)]
        self.zero_stored = ctx.enter_context(nc.semaphore("zero_stored"))
        self.wa_count = self.wb_count = self.phases = 0

    def sb(self, ctx, name, shape, dt=F32):
        return ctx.enter_context(self.nc.sbuf_tensor(name, shape, dt))

    def const(self, name):
        at, n = self.dram["const_at"][name]
        return self.consts[:, at:at + n]

    def vrow(self, name):
        at, n = self.dram["vrow_at"][name]
        return self.vrows[0:1, at:at + n]

    def load_a(self, sp, to, of):
        sp.dma_start(to, of).then_inc(self.wa_loaded, 16)
        self.wa_count += 16

    def load_b(self, sp, to, of):
        sp.dma_start(to, of).then_inc(self.wb_loaded, 16)
        self.wb_count += 16


class Sems(dict):

    def __init__(self, core, names):
        self.core = core
        core.phases += 1
        for n in names.split():
            self[n] = core.nc.alloc_semaphore(f"{n}_{core.phases}")

    def close(self):
        self.core.nc.clear_and_free_semaphores(list(self.values()))
        self.core.nc.all_engine_barrier()


def held(e, sem, value, gate):
    e.wait_ge(sem, value)
    e.sem_inc(gate, 1)



TAIL = " y_ready y_free stat aggr eps_added rstd centred xn_ready gate_dve gate_pool gate_act gate_pe"


def tok(buf, t):
    return buf[:, t * D:(t + 1) * D] if isinstance(t, int) else buf[:, bass.ds(t * D, D)]


def tail_stats(c, e, s, t, p, first, src=None):
    src = c.x if src is None else src
    if not first:
        held(e, s["xn_ready"], t - 1, s["gate_dve"])
    e.bn_stats(c.stats[:, p, 0:6], tok(src, t)).then_inc(s["stat"], 1)
    held(e, s["stat"], t + 1, s["gate_dve"])
    e.bn_aggr(c.stats[:, p, 6:8], c.stats[:, p, 0:6]).then_inc(s["aggr"], 1)


def tail_dve(c, e, s, t, p, first, y, layer, ready=None, count=None):
    held(e, ready or s["y_ready"], t + 1 if count is None else count, s["gate_dve"])
    xt = tok(c.x, t)
    e.scalar_tensor_tensor(out=xt, in0=y, scalar=c.tg[:, layer:layer + 1], in1=xt,
                           op0=ALU.mult, op1=ALU.add).then_inc(s["y_free"], 1)
    held(e, s["y_free"], t + 1, s["gate_dve"])
    tail_stats(c, e, s, t, p, first)


def tail_pool(c, e, s, t, p, src=None, dst=None):
    src, dst = c.x if src is None else src, c.xn if dst is None else dst
    mean, var = c.stats[:, p, 6:7], c.stats[:, p, 7:8]
    e.wait_ge(s["aggr"], t + 1)
    e.tensor_tensor(var, var, c.eps, ALU.add).then_inc(s["eps_added"], 1)
    e.wait_ge(s["eps_added"], t + 1)
    e.tensor_tensor(var, var, c.neg_half, ALU.pow).then_inc(s["rstd"], 1)
    held(e, s["rstd"], t + 1, s["gate_pool"])
    xt, xn = tok(src, t), tok(dst, t)
    e.tensor_tensor(xn, xt, mean.broadcast_to([P, D]), ALU.subtract).then_inc(s["centred"], 1)
    held(e, s["centred"], t + 1, s["gate_pool"])
    e.tensor_tensor(xn, xn, var.broadcast_to([P, D]), ALU.mult).then_inc(s["xn_ready"], 1)


def tail_pool_all(c, pool, s, src=None, dst=None):
    with pool.Fori(0, T // 2) as i:
        for p in range(2):
            tail_pool(c, pool, s, 2 * i + p, p, src, dst)


def pairs(e, body):
    body(0, True)
    with e.Fori(1, T // 2) as i:
        body(i, False)


def transpose_xn(c):
    s = Sems(c, "turned")
    with c.nc.Block() as block:
        @block.tensor
        def _(pe):
            for n in range(KD * T):
                t, k = n // KD, n % KD
                mm = pe.transpose(c.banks[n // 4][:, n % 4 * P:n % 4 * P + P],
                                  c.xn[:, t * D + k * P:t * D + k * P + P], c.ident[:, :])
                if n % 4 == 3:
                    mm.then_inc(s["turned"], 1)

        def evacuate(e, j, copy):
            e.wait_ge(s["turned"], j + 1)
            copy(c.xnT[:, :, 2 * j * P:2 * (j + 1) * P].rearrange("p k (t n) -> p t k n", t=2),
                 c.banks[j][:, :].rearrange("p (t k n) -> p t k n", t=2, k=KD))

        @block.scalar
        def _(act):
            for j in range(0, T // 2, 2):
                evacuate(act, j, act.copy)

        @block.vector
        def _(dve):
            for j in range(1, T // 2, 2):
                evacuate(dve, j, dve.tensor_copy)
    s.close()


def norm_and_turn(c, src, dst, update=None, scale=None, shift=None, names="", others=None):
    s = Sems(c, "y_free stat aggr rooted inverted xn_ready turned evac gate_dve " + names)
    with c.nc.Block() as block:
        if others:
            others(block, s)

        @block.vector
        def _(dve):
            def stats(t):
                if update:
                    dve.wait_ge(s["y_free"], t + 1)
                dve.bn_stats(c.stats[:, t, 0:6], tok(src, t)).then_inc(s["stat"], 1)

            for t in range(T):
                if update:
                    update(dve, s, t)
                    if t >= 1:
                        stats(t - 1)
                else:
                    stats(t)
            if update:
                stats(T - 1)
            for t in range(T):
                dve.wait_ge(s["stat"], t + 1)
                dve.bn_aggr(c.stats[:, t, 6:8], c.stats[:, t, 0:6]).then_inc(s["aggr"], 1)
            dve.wait_ge(s["rooted"], 1)
            dve.reciprocal(c.stats[:, :, 7], c.stats[:, :, 7]).then_inc(s["inverted"], 1)
            dve.wait_ge(s["inverted"], 1)
            for t in range(T):
                dve.tensor_scalar(tok(dst, t), tok(src, t), c.stats[:, t, 6:7], c.stats[:, t, 7:8],
                                  ALU.subtract, ALU.mult).then_inc(s["xn_ready"], 1)

        @block.scalar
        def _(act):
            act.wait_ge(s["aggr"], T)
            act.activation(c.stats[:, :, 7], c.stats[:, :, 7], ACT.Sqrt, bias=c.eps).then_inc(s["rooted"], 1)
            for j in range(T // 2):
                act.wait_ge(s["turned"], j + 1)
                of = c.banks[j][:, :].rearrange("p (t k n) -> p t k n", t=2, k=KD)
                to = c.xnT[:, :, 2 * j * P:2 * (j + 1) * P].rearrange("p k (t n) -> p t k n", t=2)
                if scale is None:
                    act.activation(to, of, ACT.Copy)
                else:
                    for k in range(KD):
                        act.activation(to[:, :, k, :], of[:, :, k, :], ACT.Identity, bias=shift[k], scale=scale[k])

        @block.tensor
        def _(pe):
            for j in range(T // 2):
                pe.wait_ge(s["xn_ready"], 2 * j + 2)
                for q in range(4):
                    t, k = 2 * j + q // KD, q % KD
                    mm = pe.transpose(c.banks[j][:, q * P:(q + 1) * P], dst[:, t * D + k * P:t * D + (k + 1) * P], c.ident[:, :])
                mm.then_inc(s["turned"], 1)
    s.close()


def phase_setup(c):
    d = c.dram
    s = Sems(c, "x_loaded gates_loaded loaded set")
    with c.nc.Block() as block:
        @block.sync
        def _(sp):
            sp.dma_start(c.x[:, :].rearrange("p (t d) -> p t d", d=D),
                         d["x"].rearrange("(t p) d -> p t d", p=P)).then_inc(s["x_loaded"], 16)
            sp.dma_start(c.ident[:, :], d["ident"]).then_inc(s["loaded"], 16)
            sp.dma_start(c.tg[:, :], d["gates"]).then_inc(s["gates_loaded"], 16)
            sp.dma_start(c.ctxT[:, :, :], rows(d["ctxT"], KD)).then_inc(s["loaded"], 16)
            sp.dma_start(c.consts[:, :], d["consts"]).then_inc(s["loaded"], 16)
            sp.dma_start(c.vrows[:, :], d["vrows"]).then_inc(s["loaded"], 16)
            load_l0x(c, sp)

        @block.gpsimd
        def _(pool):
            pool.memset(c.ones[:, :], 1.0)
            pool.memset(c.eps, LN_EPS)
            pool.memset(c.eps6, 1e-6)
            pool.memset(c.unround, -ROUND)
            pool.memset(c.neg_half, -0.5).then_inc(s["set"], 1)
            pool.wait_ge(s["set"], 1)
            pool.wait_ge(s["loaded"], 64)
            for k in range(KD):
                for b in range(B):
                    pool.tensor_copy(c.ctxR[:, k, b, :].rearrange("p (r m) -> p r m", r=4),
                                     c.ctxT[:, k, b * M + P:(b + 1) * M].unsqueeze(1).broadcast_to([P, 4, ML]))

        @block.scalar
        def _(act):
            act.wait_ge(s["gates_loaded"], 16)
            act.activation(c.tg[:, :], c.tg[:, :], ACT.Tanh)

        @block.vector
        def _(dve):
            dve.wait_ge(s["x_loaded"], 16)
    s.close()
    norm_and_turn(c, c.x, c.xn)



class Heads:

    def __init__(self, H, DH, NK, HG, QB, masked=False):
        self.H, self.DH, self.NK, self.HG, self.QB, self.masked = H, DH, NK, HG, QB, masked
        self.NL = NK - P
        self.GL = H // HG
        self.C = H * DH
        self.CT = self.C // P
        self.groups = [list(range(h, min(h + 3, H))) for h in range(0, H, 3)]
        self.G = len(self.groups)
        self.R = 3 if self.G % 3 == 0 else 2
        turned = list(range(H + self.GL))
        self.batches = [turned[i:i + 4] for i in range(0, len(turned), 4)]
        self.NB = len(self.batches)

    def part(self, which):
        numbered = list(enumerate(self.groups))
        return numbered if which is None else numbered[:self.R] if which == 0 else numbered[self.R:]

    def rows_of(self, n):
        return P if n < self.H else self.HG * self.NL

    def q_of(self, h):
        return list(range(KD)) if self.H == 1 else [h * self.DH // P]


ATT = " last_ready q_ready q_evac scores_ready masked_ max_ready exped turned p_evac o_ready recips osb_ready o_turned ot_evac"
TURN, YB, OB = (3, 4), 5, (6, 7)


class AttentionMemory:

    def __init__(self, c, ctx, a, tag, borrowed=()):
        had = dict(borrowed)

        def of(name, shape):
            return had[name] if name in had else c.sb(ctx, name + tag, shape)

        self.q = of("q", [P, 2, a.QB, P])
        self.p = of("p", [P, 2, a.H, a.NK])
        self.pt = of("pt", [P, a.H + a.GL, P])
        self.pl = of("pl", [P, 2, a.H * a.NL])
        self.nmax = of("nmax", [P, 2, a.H])
        self.sum = of("sum", [P, 2, a.H])
        self.rsum = of("rsum", [P, 2, a.H])
        self.osb = of("osb", [P, a.C])
        self.ot = of("ot", [P, a.CT, P])


class Parts:

    def __init__(self, keys, values, left, mask, stage, q_pe, q_act, project, finish_dve, finish_pool):
        self.keys, self.values, self.left, self.mask = keys, values, left, mask
        self.stage, self.q_pe, self.q_act = stage, q_pe, q_act
        self.project, self.finish_dve, self.finish_pool = project, finish_dve, finish_pool


def att_scores(c, pe, s, a, m, i, t, p, first, keys, part=None):
    for g, hs in a.part(part):
        n = a.G * t + g
        slot = p * a.G + g
        if g == 0:
            held(pe, s["q_ready"], t + 1, s["gate_pe"])
        if not (first and slot < a.R):
            held(pe, s["masked_"] if a.masked else s["exped"], n + 1 - a.R, s["gate_pe"])
        for j, h in enumerate(hs):
            ks = a.q_of(h)
            for kk, k in enumerate(ks):
                mm = pe.matmul(c.banks[slot % a.R][:, j * a.NK:(j + 1) * a.NK], m.q[:, p, k, :], keys(i, h, kk),
                               start=(kk == 0), stop=(kk == len(ks) - 1))
        mm.then_inc(s["scores_ready"], 1)


def att_max(c, dve, s, a, m, i, t, p, mask):
    for g, hs in enumerate(a.groups):
        n = a.G * t + g
        bank = c.banks[(p * a.G + g) % a.R]
        sc = bank[:, 0:len(hs) * a.NK].rearrange("p (h k) -> p h k", k=a.NK)
        held(dve, s["scores_ready"], n + 1, s["gate_dve"])
        if a.masked:
            to = m.p[:, p, hs[0]:hs[-1] + 1, :]
            dve.tensor_tensor(to, sc, mask(i).unsqueeze(1).broadcast_to([P, len(hs), a.NK]),
                              ALU.add).then_inc(s["masked_"], 1)
            dve.wait_ge(s["masked_"], n + 1)
            sc = to
        dve.tensor_reduce(m.nmax[:, p, hs[0]:hs[-1] + 1], sc, AX.X, ALU.max, negate=True).then_inc(s["max_ready"], 1)


def att_exp(c, act, s, a, m, t, p, part=None):
    for g, hs in a.part(part):
        n = a.G * t + g
        bank = c.banks[(p * a.G + g) % a.R]
        act.wait_ge(s["max_ready"], n + 1)
        for j, h in enumerate(hs):
            src = m.p[:, p, h, :] if a.masked else bank[:, j * a.NK:(j + 1) * a.NK]
            ins = act.activation(m.p[:, p, h, :], src, ACT.Exp, bias=m.nmax[:, p, h:h + 1],
                                 accum_out=m.sum[:, p, h:h + 1])
        ins.then_inc(s["exped"], 1)


def att_turn(c, pe, s, a, m, t, p):
    for j, batch in enumerate(a.batches):
        if j == 0:
            held(pe, s["exped"], a.G * (t + 1), s["gate_pe"])
        if j >= 2:
            held(pe, s["p_evac"], a.NB * t + j - 1, s["gate_pe"])
        for q, u in enumerate(batch):
            g = u - a.H
            if u == a.H:
                held(pe, s["last_ready"], t + 1, s["gate_pe"])
            w = a.HG * a.NL
            src = m.p[:, p, u, 0:P] if u < a.H else m.pl[:, p, g * w:(g + 1) * w]
            mm = pe.transpose(c.banks[TURN[j % 2]][0:a.rows_of(u), q * P:(q + 1) * P], src, c.ident[:, :])
        mm.then_inc(s["turned"], 1)


def att_evacuate(c, act, s, a, m, t, p):
    for j, batch in enumerate(a.batches):
        bank = c.banks[TURN[j % 2]]
        act.wait_ge(s["turned"], a.NB * t + j + 1)
        full = [u for u in batch if u < a.H]
        part = [u for u in batch if u >= a.H]
        if full:
            ins = act.activation(m.pt[:, full[0]:full[-1] + 1, :], bank[:, 0:len(full) * P], ACT.Copy)
        if part:
            r = a.rows_of(part[0])
            ins = act.activation(m.pt[0:r, part[0]:part[-1] + 1, :], bank[0:r, len(full) * P:len(batch) * P], ACT.Copy)
        ins.then_inc(s["p_evac"], 1)


def att_values(c, pe, s, a, m, i, t, p, vals, left):
    held(pe, s["p_evac"], a.NB * (t + 1), s["gate_pe"])
    w = a.HG * a.DH
    started = set()
    for g in range(a.GL):
        b = g * w // 512
        pe.matmul(c.banks[OB[b]][:, g * w % 512:g * w % 512 + w], m.pt[0:a.HG * a.NL, a.H + g, :], left(i, g),
                  start=(b not in started), stop=False, skip_group_check=True)
        started.add(b)
    for h in range(a.H):
        o = h * a.DH
        mm = pe.matmul(c.banks[OB[o // 512]][:, o % 512:o % 512 + a.DH], m.pt[:, h, :], vals(i, h),
                       start=False, stop=True, skip_group_check=True)
    mm.then_inc(s["o_ready"], 1)


def att_normalise(c, dve, s, a, m, t, p):
    dve.wait_ge(s["exped"], a.G * (t + 1))
    dve.reciprocal(m.rsum[:, p, :], m.sum[:, p, :]).then_inc(s["recips"], 1)
    held(dve, s["recips"], t + 1, s["gate_dve"])
    held(dve, s["o_ready"], t + 1, s["gate_dve"])
    nb = -(-a.C // 512)
    hb, w = a.H // nb, a.C // nb
    for b in range(nb):
        ins = dve.tensor_tensor(m.osb[:, b * w:(b + 1) * w].rearrange("p (h d) -> p h d", d=a.DH),
                                c.banks[OB[b]][:, 0:w].rearrange("p (h d) -> p h d", d=a.DH),
                                m.rsum[:, p, b * hb:(b + 1) * hb].unsqueeze(2).broadcast_to([P, hb, a.DH]),
                                ALU.mult)
    ins.then_inc(s["osb_ready"], 1)


def att_turn_out(c, pe, s, a, m, t):
    held(pe, s["osb_ready"], t + 1, s["gate_pe"])
    for k in range(a.CT):
        mm = pe.transpose(c.banks[OB[k // 4]][:, k % 4 * P:(k % 4 + 1) * P], m.osb[:, k * P:(k + 1) * P], c.ident[:, :])
    mm.then_inc(s["o_turned"], 1)


def att_project(c, pe, s, a, m, i, t, w_out, b_out):
    held(pe, s["ot_evac"], t + 1, s["gate_pe"])
    for k in range(a.CT):
        mm = pe.matmul(c.banks[YB][:, 0:D], m.ot[:, k, :], w_out(i, k), start=(k == 0),
                       stop=(k == a.CT - 1 and b_out is None))
    if b_out is not None:
        mm = pe.matmul(c.banks[YB][:, 0:D], c.ones[0:1, :], b_out, start=False, stop=True)
    mm.then_inc(s["y_ready"], 1)


def att_finish_pe(c, pe, s, a, m, i, t, w_out, b_out):
    att_turn_out(c, pe, s, a, m, t)
    att_project(c, pe, s, a, m, i, t, w_out, b_out)


def att_finish_act(c, act, s, a, m, t):
    act.wait_ge(s["o_turned"], t + 1)
    for b in range(-(-a.CT // 4)):
        n = min(4, a.CT - 4 * b)
        ins = act.activation(m.ot[:, 4 * b:4 * b + n, :], c.banks[OB[b]][:, 0:n * P], ACT.Copy)
    ins.then_inc(s["ot_evac"], 1)


def every_tile(e, body):
    for p in range(2):
        body(0, p, True, False)
    with e.Fori(1, T // 2 - 1) as i:
        for p in range(2):
            body(i, p, False, False)
    for p in range(2):
        body(T // 2 - 1, p, False, p == 1)


def at(i, size, o, n):
    return slice(i // (T // 4) * size + o, i // (T // 4) * size + o + n) if isinstance(i, int) else bass.ds(i // (T // 4) * size + o, n)


def attention(c, block, s, a, m, h):
    @block.tensor
    def _(pe):
        if h.q_pe:
            h.q_pe(pe, 0)
        att_scores(c, pe, s, a, m, 0, 0, 0, True, h.keys)
        if h.q_pe:
            h.q_pe(pe, 1)

        def tile(i, p, first, last):
            t = 2 * i + p
            ahead = (c, pe, s, a, m, i if p == 0 else i + 1, t + 1, 1 - p, first and p == 0, h.keys)
            behind = not (first and p == 0)
            if behind and h.project:
                att_turn_out(c, pe, s, a, m, t - 1)
            if not last:
                att_scores(*ahead, 0)
            if behind:
                if h.project:
                    att_project(c, pe, s, a, m, i, t - 1, *h.project)
                else:
                    held(pe, s["osb_ready"], t, s["gate_pe"])
            att_turn(c, pe, s, a, m, t, p)
            if not last:
                att_scores(*ahead, 1)
            att_values(c, pe, s, a, m, i, t, p, h.values, h.left)
            if h.q_pe and not (isinstance(i, int) and t + 2 >= T):
                h.q_pe(pe, t + 2)
        every_tile(pe, tile)
        if h.project:
            att_finish_pe(c, pe, s, a, m, T // 2 - 1, T - 1, *h.project)

    @block.scalar
    def _(act):
        if h.q_act:
            h.q_act(act, 0, 0)
        att_exp(c, act, s, a, m, 0, 0)
        if h.q_act:
            h.q_act(act, 1, 1)

        def tile(i, p, first, last):
            t = 2 * i + p
            if not (first and p == 0) and h.project:
                att_finish_act(c, act, s, a, m, t - 1)
            if not last:
                att_exp(c, act, s, a, m, t + 1, 1 - p, 0)
            att_evacuate(c, act, s, a, m, t, p)
            if not last:
                att_exp(c, act, s, a, m, t + 1, 1 - p, 1)
            if h.q_act and not (isinstance(i, int) and t + 2 >= T):
                h.q_act(act, t + 2, p)
        every_tile(act, tile)
        if h.project:
            att_finish_act(c, act, s, a, m, T - 1)

    @block.vector
    def _(dve):
        att_max(c, dve, s, a, m, 0, 0, 0, h.mask)

        def tile(i, p, first, last):
            t = 2 * i + p
            if not last:
                att_max(c, dve, s, a, m, i if p == 0 else i + 1, t + 1, 1 - p, h.mask)
            if not (first and p == 0):
                h.finish_dve(dve, t - 1, 1 - p, first)
            att_normalise(c, dve, s, a, m, t, p)
        every_tile(dve, tile)
        h.finish_dve(dve, T - 1, 1, False)

    @block.gpsimd
    def _(pool):
        if h.stage:
            for t in range(2):
                h.stage(pool, t, t, True)

        def last_keys(t, p):
            held(pool, s["exped"], a.G * (t + 1), s["gate_pool"])
            pool.tensor_copy(m.pl[:, p, :].rearrange("p (h k) -> p h k", k=a.NL),
                             m.p[:, p, :, P:a.NK]).then_inc(s["last_ready"], 1)

        last_keys(0, 0)

        def tile(i, p, first, last):
            t = 2 * i + p
            if h.stage and not (isinstance(i, int) and t + 2 >= T):
                h.stage(pool, t + 2, p, False)
            if not (first and p == 0):
                h.finish_pool(pool, t - 1, 1 - p)
            if not last:
                last_keys(t + 1, 1 - p)
        every_tile(pool, tile)
        h.finish_pool(pool, T - 1, 1)


def stage_tile(c, s, a, m, src):
    def stage(pool, t, p, first):
        if not first:
            held(pool, s["scores_ready"], a.G * (t - 1), s["gate_pool"])
        sl = src[:, :, t * P:(t + 1) * P] if isinstance(t, int) else src[:, :, bass.ds(t * P, P)]
        pool.tensor_copy(m.q[:, p, :, :], sl).then_inc(s["q_ready"], 1)
    return stage



L0X = Heads(H=16, DH=16, NK=M, HG=4, QB=KD)


def load_l0x(c, sp):
    d, w = c.dram, c.wa
    c.load_a(sp, w[:, 0:512].rearrange("p (k n) -> p k n", k=KD), rows(d["L0_xattn_Wq"], KD))
    c.load_a(sp, w[:, 512:1536].rearrange("p (k n) -> p k n", k=2 * KD), rows(d["L0_xattn_Wkv"], 2 * KD))
    c.load_a(sp, w[:, 1536:2048].rearrange("p (k n) -> p k n", k=KD), rows(d["L0_WvT"], KD))
    c.load_a(sp, w[:, 2048:2560].rearrange("p (k n) -> p k n", k=KD), rows(d["L0_WprojT"], KD))


def layer0_attention(c, load_next):
    with ExitStack() as ctx:
        a = L0X
        w = c.wa
        w_nat = [w[:, 0:512].rearrange("p (m n) -> p m n", m=KD), w[:, 512:1024].rearrange("p (m n) -> p m n", m=KD)]
        wv = w[:, 1536:2048].rearrange("p (k n) -> p k n", k=KD)
        wo = w[:, 2048:2560].rearrange("p (k n) -> p k n", k=KD)
        kb = c.sb(ctx, "l0_keys", [P, B * 16 * M])
        vm = c.sb(ctx, "l0_values", [P, B * D])
        vl = c.sb(ctx, "l0_values_last", [P, B * 4 * 64])
        with ExitStack() as prep:
            layer0_prepare(c, prep, w_nat, wv, kb, vm, vl)
        m = AttentionMemory(c, ctx, a, "_l0")
        s = Sems(c, ATT + TAIL)
        with c.nc.Block() as block:
            @block.sync
            def _(sp):
                load_next(c, sp)

            def finish(dve, t, p, first):
                tail_dve(c, dve, s, t, p, first, c.banks[YB][:, 0:D], 0)

            attention(c, block, s, a, m, Parts(
                q_pe=None, q_act=None, keys=lambda i, h, kk: kb[:, at(i, 16 * M, h * M, M)],
                values=lambda i, h: vm[:, at(i, D, h * 16, 16)], left=lambda i, g: vl[0:104, at(i, D, g * 64, 64)], mask=None, stage=stage_tile(c, s, a, m, c.xnT),
                project=(lambda i, k: wo[:, k, :], c.vrow("L0_xattn_bproj")), finish_dve=finish,
                finish_pool=lambda pool, t, p: tail_pool(c, pool, s, t, p)))
        s.close()


def layer0_prepare(c, ctx, w_nat, wv, kb, vm, vl):
    wc = c.sb(ctx, "centred_weights", [P, 2, KD, D])
    bc = c.sb(ctx, "centred_biases", [P, 4])
    qc = c.sb(ctx, "centred_q", [P, 2, KD, CH])
    sq = c.sb(ctx, "squares", [P, 2, KD, CH])
    kn = c.sb(ctx, "normed_k", [P, KD, B * M])
    s = Sems(c, "weights_ready job evac squared inverted scaled normed blocks values_done")
    chunks = [(1, c.ctxT[:, :, :], B * M, kn[:, :, :])]
    chunks += [(0, c.xnT[:, :, n * CH:(n + 1) * CH], CH, c.xnT[:, :, n * CH:(n + 1) * CH]) for n in range(NC)]
    jobs = [("centre", 0), ("centre", 1), ("bias", 0)]
    for n in range(len(chunks) + 1):
        if n < len(chunks):
            jobs += [("project", n, 0), ("project", n, 1)]
        if n >= 1:
            jobs += [("average", n - 1, 0), ("average", n - 1, 1)]
    jobs += [("values", 0), ("values", 1), ("last", 0), ("last", 1)]
    at = {j: n for n, j in enumerate(jobs)}
    bank = {j: c.banks[n % 8] for n, j in enumerate(jobs)}
    with c.nc.Block() as block:
        @block.tensor
        def _(pe):
            pe.wait_ge(c.wa_loaded, c.wa_count)
            for n, job in enumerate(jobs):
                if n >= 8:
                    pe.wait_ge(s["evac"], n - 7)
                out = bank[job]
                if job[0] == "centre":
                    for cb in range(KD):
                        for mb in range(KD):
                            mm = pe.matmul(out[:, cb * D + mb * P:cb * D + (mb + 1) * P],
                                           w_nat[job[1]][:, mb, cb * P:(cb + 1) * P], c.const("centre16"),
                                           start=True, stop=True)
                elif job[0] == "bias":
                    for j, name in enumerate(("bq0", "bq1", "bk0", "bk1")):
                        mm = pe.matmul(out[:, j:j + 1], c.const("centre16"), c.const(name), start=True, stop=True)
                elif job[0] == "project":
                    kind, src, width, _dst = chunks[job[1]]
                    if job[2] == 0 and job[1] == 0:
                        pe.wait_ge(s["evac"], 3)
                    for k in range(KD):
                        mm = pe.matmul(out[:, 0:width], wc[:, kind, k, job[2] * P:(job[2] + 1) * P], src[:, k, :],
                                       start=(k == 0), stop=(k == KD - 1))
                elif job[0] == "average":
                    width = chunks[job[1]][2]
                    pe.wait_ge(s["squared"], job[1] + 1)
                    mm = pe.matmul(out[:, 0:width], c.const("average16"), sq[:, job[1] % 2, job[2], 0:width],
                                   start=True, stop=True)
                else:
                    b = job[1]
                    r = P if job[0] == "values" else 104
                    for k in range(KD):
                        lhs = c.ctxT[:, k, b * M:b * M + P] if r == P else c.ctxR[:, k, b, :]
                        pe.matmul(out[0:r, 0:D], lhs, wv[:, k, :], start=(k == 0), stop=False)
                    mm = pe.matmul(out[0:r, 0:D], c.ones[0:1, 0:r], c.vrow("bv"), start=False, stop=True)
                mm.then_inc(s["job"], 1)

        @block.scalar
        def _(act):
            for n, job in enumerate(jobs):
                act.wait_ge(s["job"], n + 1)
                src = bank[job]
                if job[0] == "centre":
                    act.activation(wc[:, job[1], :, :], src[:, :], ACT.Copy).then_inc(s["evac"], 1)
                elif job[0] == "bias":
                    act.activation(bc[:, :], src[:, 0:4], ACT.Copy).then_inc(s["evac"], 1)
                    act.wait_ge(s["evac"], n + 1)
                elif job[0] == "project":
                    kind, _src, width, _dst = chunks[job[1]]
                    if job[2] == 0 and job[1] >= 2:
                        act.wait_ge(s["scaled"], job[1] - 1)
                    act.activation(qc[:, job[1] % 2, job[2], 0:width], src[:, 0:width], ACT.Identity,
                                   bias=bc[:, 2 * kind + job[2]:2 * kind + job[2] + 1]).then_inc(s["evac"], 1)
                elif job[0] == "average":
                    width = chunks[job[1]][2]
                    act.activation(sq[:, job[1] % 2, job[2], 0:width], src[:, 0:width], ACT.Sqrt,
                                   bias=c.eps).then_inc(s["evac"], 1)
                elif job[0] == "values":
                    b = job[1]
                    act.activation(vm[:, b * D:(b + 1) * D], src[:, 0:D], ACT.Copy).then_inc(s["evac"], 1)
                else:
                    b = job[1]
                    act.activation(vl[0:104, b * D:(b + 1) * D], src[0:104, 0:D], ACT.Copy).then_inc(s["evac"], 1)

        @block.vector
        def _(dve):
            def squares(n):
                width = chunks[n][2]
                dve.wait_ge(s["evac"], at[("project", n, 1)] + 1)
                if n >= 2:
                    dve.wait_ge(s["scaled"], n - 1)
                v = qc[:, n % 2, :, 0:width]
                dve.tensor_tensor(sq[:, n % 2, :, 0:width], v, v, ALU.mult).then_inc(s["squared"], 1)

            def norm(n):
                kind, _src, width, dst = chunks[n]
                gamma, beta = (("kgam", "kbet") if kind else ("qgam", "qbet"))
                dve.wait_ge(s["evac"], at[("average", n, 1)] + 1)
                v, r = qc[:, n % 2, :, 0:width], sq[:, n % 2, :, 0:width]
                dve.reciprocal(r, r).then_inc(s["inverted"], 1)
                dve.wait_ge(s["inverted"], n + 1)
                dve.scalar_tensor_tensor(out=v, in0=v, scalar=c.const(gamma), in1=sq[:, n % 2, :, 0:width],
                                         op0=ALU.mult, op1=ALU.mult).then_inc(s["normed"], 1)
                dve.wait_ge(s["normed"], n + 1)
                dve.tensor_scalar(dst, v, c.const(beta), None, ALU.add).then_inc(s["scaled"], 1)

            for n in range(len(chunks) + 1):
                if n < len(chunks):
                    squares(n)
                if n >= 1:
                    norm(n - 1)
            dve.wait_ge(s["scaled"], len(chunks))
            kbv = kb[:, :].rearrange("p (b h k) -> p b h k", b=B, h=16)
            for h in range(16):
                dve.tensor_scalar(kbv[:, :, h, :], kn[:, h // 8, :].rearrange("p (b k) -> p b k", b=B),
                                  c.const("heads16")[:, h % 8:h % 8 + 1], None, ALU.mult).then_inc(s["blocks"], 1)
            for b in range(B):
                dve.wait_ge(s["evac"], at[("last", b)] + 1)
                v = vl[0:104, b * D:(b + 1) * D].rearrange("p (g n) -> p g n", g=4)
                dve.tensor_tensor(v, v, c.const("left16")[0:104, :].unsqueeze(1).broadcast_to([104, 4, 64]),
                                  ALU.mult).then_inc(s["values_done"], 1)
    s.close()



def route(c, block, s, logits, n_experts, comb, work, floor, best_one=None, next_one=None):
    E = n_experts
    shape = [P, T, E]

    def view(n):
        return work[:, n * T * E:(n + 1) * T * E].rearrange("p (t e) -> p t e", e=E)

    def each(n):
        return work[:, 5 * T * E + n * T:5 * T * E + (n + 1) * T]

    def spread(v):
        return v.unsqueeze(2).broadcast_to(shape)

    L, first, second, score, ex = (view(n) for n in range(5))
    best, most, den, rest = (each(n) for n in range(4))
    order = c.const("falling")[:, 0:E].unsqueeze(1).broadcast_to(shape)
    cb = comb[:, 0:T * E].rearrange("p (t e) -> p t e", e=E)

    def on_vector(dve):
        steps = [0]

        def step(ins):
            steps[0] += 1
            ins.then_inc(s["routed"], 1)
            dve.wait_ge(s["routed"], steps[0])

        step(dve.tensor_copy(L, logits))
        for chosen in (first, second):
            step(dve.tensor_reduce(most, L, AX.X, ALU.max))
            if chosen is first:
                step(dve.tensor_copy(best, most))
                step(dve.tensor_tensor(ex, L, spread(best), ALU.subtract))
            step(dve.tensor_tensor(score, L, spread(most), ALU.is_equal))
            step(dve.tensor_tensor(score, score, order, ALU.mult))
            step(dve.tensor_reduce(most, score, AX.X, ALU.max))
            step(dve.tensor_tensor(chosen, score, spread(most), ALU.is_equal))
            if chosen is first:
                step(dve.scalar_tensor_tensor(out=L, in0=first, scalar=-3e38, in1=L, op0=ALU.mult, op1=ALU.add))
        if best_one is not None:
            step(dve.tensor_copy(best_one, first))
            step(dve.tensor_copy(next_one, second))
        step(dve.tensor_tensor(first, first, second, ALU.add))
        dve.sem_inc(s["shifted"], 1)
        dve.wait_ge(s["exponentials"], 1)
        if floor:
            step(dve.tensor_reduce(rest, ex, AX.X, ALU.add))
        step(dve.tensor_tensor(first, first, ex, ALU.mult))
        step(dve.tensor_reduce(den, first, AX.X, ALU.add))
        if floor:
            step(dve.scalar_tensor_tensor(out=den, in0=rest, scalar=1e-9, in1=den, op0=ALU.mult, op1=ALU.add))
        step(dve.reciprocal(den, den))
        step(dve.tensor_tensor(cb, first, spread(den), ALU.mult))
        dve.sem_inc(s["comb_ready"], 1)

    def on_scalar(act):
        act.wait_ge(s["shifted"], 1)
        act.activation(ex, ex, ACT.Exp).then_inc(s["exponentials"], 1)

    return on_vector, on_scalar


ROUTE = " logits_ready routed shifted exponentials comb_ready"


def router_logits(c, pe, s, weights, E, bank):
    for t in range(T):
        for k in range(KD):
            mm = pe.matmul(bank[:, t * E:(t + 1) * E], c.xnT[:, k, t * P:(t + 1) * P], weights[:, k, :],
                           start=(k == 0), stop=(k == KD - 1), skip_group_check=True)
    mm.then_inc(s["logits_ready"], 1)


MLP = " gate_pe gate_act gate_dve gate_up_ready silu_done product h_ready downed y_read"
GATE, UP, WEIGH, DOWN = (0, 1), (2, 3), (4, 5), (6, 7)


def mlp_gate_pe(c, pe, s, n, p, rhs, gate, up, weigh=None):
    held(pe, s["h_ready"], n + 1, s["gate_pe"])
    for w, bank in ((gate, GATE), (up, UP)):
        for k in range(KD):
            mm = pe.matmul(c.banks[bank[p]][:, :], w(k), rhs(k), start=(k == 0), stop=(k == KD - 1))
    if weigh:
        mm = pe.matmul(c.banks[WEIGH[p]][:, :], *weigh, start=True, stop=True)
    mm.then_inc(s["gate_up_ready"], 1)


def mlp_down_pe(c, pe, s, n, hT, wd, banks, first, last):
    held(pe, s["h_ready"], n + 3, s["gate_pe"])
    for tt in range(CH // P):
        mm = pe.matmul(c.banks[banks[tt // 2]][:, tt % 2 * D:(tt % 2 + 1) * D], hT[:, tt * P:(tt + 1) * P], wd,
                       start=first and tt % 2 == 0, stop=last, skip_group_check=True)
    mm.then_inc(s["downed"], 1)


def mlp_act(c, act, s, n, p, sg):
    held(act, s["h_ready"], n + 1, s["gate_act"])
    act.wait_ge(s["gate_up_ready"], n + 1)
    act.activation(sg[:, p, :], c.banks[GATE[p]][:, :], ACT.Silu).then_inc(s["silu_done"], 1)


def mlp_dve(c, dve, s, n, p, sg, hT, weighed):
    held(dve, s["downed"], n + 1, s["gate_dve"])
    dve.wait_ge(s["silu_done"], n + 1)
    ins = dve.tensor_tensor(hT[:, p, :], sg[:, p, :], c.banks[UP[p]][:, :], ALU.mult)
    if weighed is not None:
        ins.then_inc(s["product"], 1)
        dve.wait_ge(s["product"], weighed + 1)
        ins = dve.tensor_tensor(hT[:, p, :], hT[:, p, :], c.banks[WEIGH[p]][:, :], ALU.mult)
    ins.then_inc(s["h_ready"], 1)


def chunks(e, body):
    with e.Fori(0, NC) as i:
        body(i)


N_R, MID_R, N_S, MID_S = 16, 64, 2, 128
L0F_BLOCKS = (N_R * MID_R + N_S * MID_S) // P
L0F_ROUTED = N_R * MID_R // P


def load_l0f(c, sp):
    d, w, n = c.dram, c.wb, L0F_BLOCKS * P
    c.load_b(sp, w[:, 0:2 * n].rearrange("p (k n) -> p k n", k=KD), rows(d["L0_gates"], KD))
    c.load_b(sp, w[:, 2 * n:4 * n].rearrange("p (k n) -> p k n", k=KD), rows(d["L0_ups"], KD))
    c.load_b(sp, w[:, 4 * n:6 * n].rearrange("p (k n) -> p k n", k=L0F_BLOCKS), rows(d["L0_downs"], L0F_BLOCKS))
    c.load_b(sp, w[:, 6 * n:6 * n + 2 * N_R].rearrange("p (k n) -> p k n", k=KD), rows(d["L0_ffn_router_w"], KD))


def layer0_experts(c, load_next):
    n = L0F_BLOCKS * P
    wg = c.wb[:, 0:2 * n].rearrange("p (k n) -> p k n", k=KD)
    wu = c.wb[:, 2 * n:4 * n].rearrange("p (k n) -> p k n", k=KD)
    wd = c.wb[:, 4 * n:6 * n].rearrange("p (k n) -> p k n", k=L0F_BLOCKS)
    wr = c.wb[:, 6 * n:6 * n + 2 * N_R].rearrange("p (k n) -> p k n", k=KD)
    with ExitStack() as ctx:
        comb = c.sb(ctx, "comb0", [P, T * N_R])
        combT = c.sb(ctx, "comb0_feat", [N_R, B * S])
        work = c.sb(ctx, "route0_work", [P, 5 * T * N_R + 4 * T])
        sg = c.sb(ctx, "silu0", [P, 2, CH])
        hT = c.sb(ctx, "hidden0", [P, 2, CH])
        s = Sems(c, "comb_turned" + ROUTE)
        with c.nc.Block() as block:
            on_vector, on_scalar = route(c, block, s, c.banks[0][:, 0:T * N_R].rearrange("p (t e) -> p t e", e=N_R),
                                         N_R, comb, work, True)

            @block.tensor
            def _(pe):
                pe.wait_ge(c.wb_loaded, c.wb_count)
                router_logits(c, pe, s, wr, N_R, c.banks[0])
                pe.wait_ge(s["comb_ready"], 1)
                for t in range(T):
                    mm = pe.transpose(c.banks[1 + t // 4][0:N_R, t % 4 * P:(t % 4 + 1) * P],
                                      comb[:, t * N_R:(t + 1) * N_R], c.ident[:, :])
                mm.then_inc(s["comb_turned"], 1)

            @block.vector
            def _(dve):
                dve.wait_ge(s["logits_ready"], 1)
                on_vector(dve)
                dve.wait_ge(s["comb_turned"], 1)
                for n4 in range(4):
                    dve.tensor_copy(combT[:, n4 * CH:(n4 + 1) * CH], c.banks[1 + n4][0:N_R, :])

            @block.scalar
            def _(act):
                on_scalar(act)
        s.close()

        s = Sems(c, MLP + TAIL.replace(' gate_pe', '').replace(' gate_act', '').replace(' gate_dve', ''))
        NB = L0F_BLOCKS
        with c.nc.Block() as block:
            @block.sync
            def _(sp):
                load_next(c, sp)

            @block.tensor
            def _(pe):
                pe.sem_inc(s["downed"], 2)

                def chunk(i):
                    for m in range(NB):
                        mlp_gate_pe(c, pe, s, i * NB + m, m % 2, lambda k: c.xnT[:, k, bass.ds(i * CH, CH)],
                                    lambda k: wg[:, k, m * P:(m + 1) * P], lambda k: wu[:, k, m * P:(m + 1) * P],
                                    (c.const("pairs16")[0:N_R, m * P:(m + 1) * P], combT[:, bass.ds(i * CH, CH)])
                                    if m < L0F_ROUTED else None)
                        if m == 1:
                            held(pe, s["y_read"], i * 4 + 1, s["gate_pe"])
                        if m >= 1:
                            mlp_down_pe(c, pe, s, i * NB + m - 1, hT[:, (m - 1) % 2, :], wd[:, m - 1, :], DOWN,
                                        m == 1, False)
                    mlp_down_pe(c, pe, s, i * NB + NB - 1, hT[:, (NB - 1) % 2, :], wd[:, NB - 1, :], DOWN, False, True)
                chunks(pe, chunk)

            @block.scalar
            def _(act):
                def chunk(i):
                    for m in range(NB):
                        mlp_act(c, act, s, i * NB + m, m % 2, sg)
                chunks(act, chunk)

            @block.vector
            def _(dve):
                dve.sem_inc(s["h_ready"], 2)
                dve.sem_inc(s["y_read"], 1)
                def chunk(i):
                    for m in range(NB):
                        mlp_dve(c, dve, s, i * NB + m, m % 2, sg, hT, i * L0F_ROUTED + m if m < L0F_ROUTED else None)
                    held(dve, s["downed"], (i + 1) * NB + 2, s["gate_dve"])
                    for tt in range(4):
                        t = 4 * i + tt
                        y = c.banks[DOWN[tt // 2]][:, tt % 2 * D:(tt % 2 + 1) * D]
                        xt = tok(c.x, t)
                        dve.scalar_tensor_tensor(out=xt, in0=y, scalar=c.tg[:, 1:2], in1=xt,
                                                 op0=ALU.mult, op1=ALU.add).then_inc(s["y_read"], 1)
                    for tt in range(4):
                        t = 4 * i + tt
                        held(dve, s["y_read"], 4 * (i + 1) + 1, s["gate_dve"])
                        held(dve, s["xn_ready"], t + 1, s["gate_dve"])
                        dve.bn_stats(c.stats[:, tt % 2, 0:6], tok(c.x, t)).then_inc(s["stat"], 1)
                        held(dve, s["stat"], t + 1, s["gate_dve"])
                        dve.bn_aggr(c.stats[:, tt % 2, 6:8], c.stats[:, tt % 2, 0:6]).then_inc(s["aggr"], 1)
                chunks(dve, chunk)

            @block.gpsimd
            def _(pool):
                pool.sem_inc(s["xn_ready"], 2)
                tail_pool_all(c, pool, s)
        s.close()



ITERS = 3
GRU = 3 * D


def load_l1x(c, sp):
    d, w = c.dram, c.wa
    at = 0
    for src, n in ((d["L1_xattn_Wq"], D), (d["L1_WkT"], D), (d["L1_WvT"], D), (d["L1_wihT"], GRU), (d["L1_whhT"], GRU)):
        c.load_a(sp, w[:, at:at + KD * n].rearrange("p (k n) -> p k n", k=KD), rows(src, KD))
        at += KD * n


def layer1_slots(c, load_next):
    def part(at, n):
        return c.wa[:, at:at + KD * n].rearrange("p (k n) -> p k n", k=KD)

    wq, wk, wv, wih, whh = part(0, D), part(512, D), part(1024, D), part(1536, GRU), part(3072, GRU)
    with ExitStack() as ctx:
        mq = c.sb(ctx, "slot_keys", [P, KD, B * M])
        vw = c.sb(ctx, "slot_values", [P, B, 2, GRU])
        gb = c.sb(ctx, "gate_biases", [P, 6])
        with ExitStack() as prep:
            layer1_prepare(c, prep, wq, wk, wv, wih, mq, vw, gb)
        sq = c.xn[:, :].rearrange("p (c k n) -> p c k n", c=NC, k=KD)
        rbc = c.sb(ctx, "slot_rstd", [P, NC, CH])
        ex = c.sb(ctx, "slot_scores", [P, 2, B * S])
        nm = c.sb(ctx, "slot_max", [P, B, 2])
        sm = c.sb(ctx, "slot_sum", [P, B, 2])
        rs = c.sb(ctx, "slot_rsum", [P, B, 2])
        rsb = c.sb(ctx, "slot_rsum_wide", [P, B, 2, P])
        rd = c.sb(ctx, "slot_rden", [P, 2, CH])
        at = c.sb(ctx, "slot_attn", [P, 2, 2, CH])
        r_sb = c.sb(ctx, "gate_r", [P, KD, CH])
        z_sb = c.sb(ctx, "gate_z", [P, KD, CH])
        n_in = c.sb(ctx, "gate_n_in", [P, KD, CH])
        n_sb = c.sb(ctx, "gate_n", [P, KD, CH])
        slots = c.xnT
        s = Sems(c, "sq_ready ms_ready root_done inverted scores_done e_done max_done exp_done rsum_done wide_done "
                    "d_ready d_read rd_done attn_ready r_ready hn_ready z_ready xin_ready r_done z_done hn_read "
                    "xin_read n_done diff scaled_diff slots_done gate_pe gate_act gate_dve")
        SC, MS, DN = (4, 5), 6, 7
        rows_of = (P, ML)
        with c.nc.Block() as block:
            @block.sync
            def _(sp):
                load_next(c, sp)

            @block.tensor
            def _(pe):
                def sl(k, ch):
                    return slots[:, k, ch * CH:(ch + 1) * CH]

                def colsum(it, ch):
                    b, n = ch // 2, it * NC + ch
                    held(pe, s["wide_done"], (it * B + b + 1) * 2, s["gate_pe"])
                    held(pe, s["d_read"], n + 1, s["gate_pe"])
                    for j, r in enumerate(rows_of):
                        mm = pe.matmul(c.banks[DN][:, :], rsb[0:r, b, j, :], ex[0:r, j, ch * CH:(ch + 1) * CH],
                                       start=(j == 0), stop=(j == 1))
                    mm.then_inc(s["d_ready"], 1)

                def gates(it, ch):
                    b, n = ch // 2, it * NC + ch
                    held(pe, s["attn_ready"], 2 * n + 2, s["gate_pe"])
                    for m in range(KD):
                        g = 2 * n + m
                        for bank, at_col, from_attn, from_slots, free, ready in (
                                (0, 0, 1, 1, s["r_done"], s["r_ready"]), (1, 2, 0, 1, s["hn_read"], s["hn_ready"]),
                                (2, 1, 1, 1, s["z_done"], s["z_ready"]), (3, 2, 1, 0, s["xin_read"], s["xin_ready"])):
                            held(pe, free, g + 1, s["gate_pe"])
                            cols = slice(at_col * D + m * P, at_col * D + (m + 1) * P)
                            ops = [(whh[:, k, cols], sl(k, ch)) for k in range(KD)] if from_slots else []
                            if from_attn:
                                ops += [(vw[0:r, b, j, cols], at[0:r, ch % 2, j, :]) for j, r in enumerate(rows_of)]
                            for q, (lhs, rhs) in enumerate(ops):
                                mm = pe.matmul(c.banks[bank][:, :], lhs, rhs, start=(q == 0), stop=(q == len(ops) - 1))
                            mm.then_inc(ready, 1)

                with pe.Fori(0, ITERS) as it:
                    for ch in range(NC):
                        b, n = ch // 2, it * NC + ch
                        held(pe, s["sq_ready"], n + 1, s["gate_pe"])
                        held(pe, s["root_done"], n + 1, s["gate_pe"])
                        for k in range(KD):
                            mm = pe.matmul(c.banks[MS][:, :], c.const("mean256"), sq[:, ch, k, :], start=(k == 0), stop=(k == KD - 1))
                        mm.then_inc(s["ms_ready"], 1)
                        held(pe, s["e_done"], 2 * n + 2, s["gate_pe"])
                        for j, r in enumerate(rows_of):
                            for k in range(KD):
                                mm = pe.matmul(c.banks[SC[j]][0:r, :], mq[:, k, b * M + j * P:b * M + j * P + r], sl(k, ch),
                                               start=(k == 0), stop=(k == KD - 1))
                        mm.then_inc(s["scores_done"], 1)
                    colsum(it, 0)
                    for ch in range(NC):
                        if ch + 1 < NC:
                            colsum(it, ch + 1)
                        gates(it, ch)

            @block.scalar
            def _(act):
                act.sem_inc(s["root_done"], 1)
                act.sem_inc(s["r_done"], 1)
                act.sem_inc(s["z_done"], 1)
                with act.Fori(0, ITERS) as it:
                    for ch in range(NC):
                        n = it * NC + ch
                        act.wait_ge(s["ms_ready"], n + 1)
                        act.activation(rbc[:, ch, :], c.banks[MS][:, :], ACT.Sqrt, bias=c.eps6).then_inc(s["root_done"], 1)
                    for b in range(B):
                        act.wait_ge(s["max_done"], 2 * (it * B + b) + 2)
                        for j, r in enumerate(rows_of):
                            v = ex[0:r, j, b * S:(b + 1) * S]
                            ins = act.activation(v, v, ACT.Exp, bias=nm[0:r, b, j:j + 1], accum_out=sm[0:r, b, j:j + 1])
                        ins.then_inc(s["exp_done"], 1)
                    for ch in range(NC):
                        for m in range(KD):
                            g = 2 * (it * NC + ch) + m
                            act.wait_ge(s["r_ready"], g + 1)
                            act.activation(r_sb[:, m, :], c.banks[0][:, :], ACT.Sigmoid, bias=gb[:, m:m + 1]).then_inc(s["r_done"], 1)
                            held(act, s["scaled_diff"], g + 1, s["gate_act"])
                            act.wait_ge(s["z_ready"], g + 1)
                            act.activation(z_sb[:, m, :], c.banks[2][:, :], ACT.Sigmoid, bias=gb[:, 2 + m:3 + m]).then_inc(s["z_done"], 1)
                            act.wait_ge(s["xin_read"], g + 2)
                            act.activation(n_sb[:, m, :], n_in[:, m, :], ACT.Tanh, bias=c.const("bih")[:, 4 + m:5 + m]).then_inc(s["n_done"], 1)

            @block.vector
            def _(dve):
                dve.sem_inc(s["e_done"], 2)
                dve.sem_inc(s["d_read"], 1)
                dve.sem_inc(s["hn_read"], 1)
                dve.sem_inc(s["xin_read"], 1)
                dve.sem_inc(s["slots_done"], 1)
                dve.sem_inc(s["scaled_diff"], 2)

                def attn(it, ch):
                    b, n = ch // 2, it * NC + ch
                    held(dve, s["d_ready"], n + 1, s["gate_dve"])
                    v = rd[:, ch % 2, :]
                    dve.tensor_scalar(v, c.banks[DN][:, :], c.eps6, None, ALU.add).then_inc(s["d_read"], 1)
                    dve.wait_ge(s["d_read"], n + 2)
                    dve.reciprocal(v, v).then_inc(s["rd_done"], 1)
                    dve.wait_ge(s["rd_done"], n + 1)
                    for j, r in enumerate(rows_of):
                        dve.scalar_tensor_tensor(out=at[0:r, ch % 2, j, :], in0=ex[0:r, j, ch * CH:(ch + 1) * CH],
                                                 scalar=rs[0:r, b, j:j + 1], in1=rd[0:r, ch % 2, :],
                                                 op0=ALU.mult, op1=ALU.mult).then_inc(s["attn_ready"], 1)

                def gru(it, ch):
                    n = it * NC + ch
                    for m in range(KD):
                        g = 2 * n + m
                        held(dve, s["r_done"], g + 2, s["gate_dve"])
                        held(dve, s["hn_ready"], g + 1, s["gate_dve"])
                        v = n_in[:, m, :]
                        dve.scalar_tensor_tensor(out=v, in0=c.banks[1][:, :], scalar=c.const("bhh")[:, 4 + m:5 + m],
                                                 in1=r_sb[:, m, :], op0=ALU.add, op1=ALU.mult).then_inc(s["hn_read"], 1)
                        held(dve, s["hn_read"], g + 2, s["gate_dve"])
                        held(dve, s["xin_ready"], g + 1, s["gate_dve"])
                        dve.tensor_tensor(v, v, c.banks[3][:, :], ALU.add).then_inc(s["xin_read"], 1)
                    for m in range(KD):
                        g = 2 * n + m
                        h, v = slots[:, m, ch * CH:(ch + 1) * CH], n_in[:, m, :]
                        held(dve, s["n_done"], g + 1, s["gate_dve"])
                        dve.tensor_tensor(v, h, n_sb[:, m, :], ALU.subtract).then_inc(s["diff"], 1)
                        held(dve, s["diff"], g + 1, s["gate_dve"])
                        dve.tensor_tensor(v, v, z_sb[:, m, :], ALU.mult).then_inc(s["scaled_diff"], 1)
                        dve.wait_ge(s["scaled_diff"], g + 3)
                        dve.tensor_tensor(h, v, n_sb[:, m, :], ALU.add).then_inc(s["slots_done"], 1)

                with dve.Fori(0, ITERS) as it:
                    held(dve, s["slots_done"], it * (NC * KD) + 1, s["gate_dve"])
                    for ch in range(NC):
                        v = slots[:, :, ch * CH:(ch + 1) * CH]
                        dve.tensor_tensor(sq[:, ch, :, :], v, v, ALU.mult).then_inc(s["sq_ready"], 1)
                    for ch in range(NC):
                        n = it * NC + ch
                        held(dve, s["root_done"], n + 2, s["gate_dve"])
                        dve.reciprocal(rbc[:, ch, :], rbc[:, ch, :]).then_inc(s["inverted"], 1)
                        held(dve, s["inverted"], n + 1, s["gate_dve"])
                        held(dve, s["scores_done"], n + 1, s["gate_dve"])
                        for j, r in enumerate(rows_of):
                            dve.tensor_tensor(ex[0:r, j, ch * CH:(ch + 1) * CH], c.banks[SC[j]][0:r, :], rbc[0:r, ch, :],
                                              ALU.mult).then_inc(s["e_done"], 1)
                        if ch % 2:
                            b = ch // 2
                            held(dve, s["e_done"], 2 * n + 4, s["gate_dve"])
                            for j, r in enumerate(rows_of):
                                dve.tensor_reduce(nm[0:r, b, j:j + 1], ex[0:r, j, b * S:(b + 1) * S], AX.X, ALU.max,
                                                  negate=True).then_inc(s["max_done"], 1)
                    for b in range(B):
                        held(dve, s["exp_done"], it * B + b + 1, s["gate_dve"])
                        for j, r in enumerate(rows_of):
                            dve.reciprocal(rs[0:r, b, j:j + 1], sm[0:r, b, j:j + 1]).then_inc(s["rsum_done"], 1)
                        held(dve, s["rsum_done"], 2 * (it * B + b) + 2, s["gate_dve"])
                        for j, r in enumerate(rows_of):
                            dve.tensor_scalar(rsb[0:r, b, j, :], c.ones[0:r, :], rs[0:r, b, j:j + 1], None,
                                              ALU.mult).then_inc(s["wide_done"], 1)
                    attn(it, 0)
                    for ch in range(NC):
                        if ch + 1 < NC:
                            attn(it, ch + 1)
                        gru(it, ch)
        s.close()

    def turn_back(block, s):
        @block.tensor
        def _(pe):
            for t in range(T):
                if t >= 8:
                    pe.wait_ge(s["y_free"], t - 7)
                for k in range(KD):
                    mm = pe.transpose(c.banks[t % 8][:, k * P:(k + 1) * P], slots[:, k, t * P:(t + 1) * P], c.ident[:, :])
                mm.then_inc(s["y_ready"], 1)

    def residual(dve, s, t):
        dve.wait_ge(s["y_ready"], t + 1)
        dve.scalar_tensor_tensor(out=tok(c.x, t), in0=c.banks[t % 8][:, 0:D], scalar=c.tg[:, 2:3], in1=tok(c.x, t),
                                 op0=ALU.mult, op1=ALU.add).then_inc(s["y_free"], 1)

    norm_and_turn(c, c.x, c.xn, residual, names="y_ready", others=turn_back)


def layer1_prepare(c, ctx, wq, wk, wv, wih, mq, vw, gb):
    W = B * M
    sq = c.sb(ctx, "ctx_squares", [P, KD, W])
    r = c.sb(ctx, "ctx_rstd", [P, W])
    pn = c.sb(ctx, "ctx_normed", [P, KD, W])
    kT = c.sb(ctx, "slot_k", [P, KD, W])
    vT = c.sb(ctx, "slot_v", [P, KD, W])
    w16 = c.sb(ctx, "slot_w_sixteenth", [P, KD])
    s = Sems(c, "step job evac rooted")
    with c.nc.Block() as block:
        @block.tensor
        def _(pe):
            pe.wait_ge(c.wa_loaded, c.wa_count)
            pe.wait_ge(s["step"], 1)
            for k in range(KD):
                mm = pe.matmul(c.banks[0][:, 0:W], c.const("mean256"), sq[:, k, :], start=(k == 0), stop=(k == KD - 1))
            mm.then_inc(s["job"], 1)
            pe.wait_ge(s["step"], 4)
            for n, w in enumerate((wk, wk, wv, wv)):
                for k in range(KD):
                    mm = pe.matmul(c.banks[1 + n][:, 0:W], w[:, k, n % 2 * P:(n % 2 + 1) * P], pn[:, k, :],
                                   start=(k == 0), stop=(k == KD - 1))
                mm.then_inc(s["job"], 1)
            pe.wait_ge(s["evac"], 2)
            for m in range(KD):
                for k in range(KD):
                    mm = pe.matmul(c.banks[5 + m][:, 0:W], wq[:, k, m * P:(m + 1) * P], kT[:, k, :],
                                   start=(k == 0), stop=(k == KD - 1))
                mm.then_inc(s["job"], 1)
            pe.wait_ge(s["evac"], 6)
            for n in range(8):
                b, j, half = n // 4, n // 2 % 2, n % 2
                rr = (P, ML)[j]
                if n >= 6:
                    pe.wait_ge(s["evac"], n + 1)
                for k in range(KD):
                    mm = pe.matmul(c.banks[n % 6][0:rr, 0:384], vT[:, k, b * M + j * P:b * M + j * P + rr],
                                   wih[:, k, half * 384:(half + 1) * 384], start=(k == 0), stop=(k == KD - 1))
                mm.then_inc(s["job"], 1)

        @block.scalar
        def _(act):
            act.wait_ge(s["job"], 1)
            act.activation(r[:, :], c.banks[0][:, 0:W], ACT.Sqrt, bias=c.eps6).then_inc(s["rooted"], 1)
            for n in range(4):
                act.wait_ge(s["job"], 2 + n)
                act.activation((kT if n < 2 else vT)[:, n % 2, :], c.banks[1 + n][:, 0:W], ACT.Copy).then_inc(s["evac"], 1)
            for m in range(KD):
                act.wait_ge(s["job"], 6 + m)
                act.activation(mq[:, m, :], c.banks[5 + m][:, 0:W], ACT.Copy, scale=w16[:, m:m + 1]).then_inc(s["evac"], 1)
            for n in range(8):
                b, j, half = n // 4, n // 2 % 2, n % 2
                rr = (P, ML)[j]
                act.wait_ge(s["job"], 8 + n)
                act.activation(vw[0:rr, b, j, half * 384:(half + 1) * 384], c.banks[n % 6][0:rr, 0:384], ACT.Copy).then_inc(s["evac"], 1)

        @block.vector
        def _(dve):
            dve.tensor_scalar(w16[:, :], c.const("slotw"), float(D) ** -0.5, None, ALU.mult)
            dve.tensor_tensor(sq[:, :, :], c.ctxT[:, :, :], c.ctxT[:, :, :], ALU.mult).then_inc(s["step"], 1)
            dve.wait_ge(s["rooted"], 1)
            dve.reciprocal(r[:, :], r[:, :]).then_inc(s["step"], 1)
            dve.wait_ge(s["step"], 2)
            for k in range(KD):
                dve.scalar_tensor_tensor(out=pn[:, k, :], in0=c.ctxT[:, k, :], scalar=c.const("inw")[:, k:k + 1], in1=r[:, :],
                                         op0=ALU.mult, op1=ALU.mult).then_inc(s["step"], 1)
            dve.tensor_tensor(gb[:, :], c.const("bih"), c.const("bhh"), ALU.add)
    s.close()



N_E, INTER = 8, 1024
EB = INTER // P
EXPERT = 2 * KD * INTER + EB * D
SG = 256
SLOTS = (2 * B * S - N_E) // SG + N_E


def load_l1f(c, sp):
    d, w = c.dram, c.wb
    c.load_b(sp, w[:, 0:512].rearrange("p (k n) -> p k n", k=KD), rows(d["L1_attnT"], KD))
    c.load_b(sp, w[:, 512:512 + KD * N_E].rearrange("p (k n) -> p k n", k=KD), rows(d["L1_gateT"], KD))


def layer1_experts(c, load_next):
    wa = c.wb[:, 0:512].rearrange("p (k n) -> p k n", k=KD)
    wr = c.wb[:, 512:512 + KD * N_E].rearrange("p (k n) -> p k n", k=KD)

    def free(block, n):
        return c.wb[:, block * 1024:block * 1024 + n]

    sorted_x, sorted_y = c.sorted_x, c.sorted_y
    with ExitStack() as ctx:
        t_tok = c.sb(ctx, "normed_again", [P, T * D])
        wexp = c.sb(ctx, "expert_weights", [P, 2, EXPERT])
        comb = c.sb(ctx, "comb1", [P, T * N_E])
        work = c.sb(ctx, "route1_work", [P, 5 * T * N_E + 4 * T])
        sg = free(1, 1024).rearrange("p (b n) -> p b n", b=4)
        hT = free(2, 1024).rearrange("p (b n) -> p b n", b=4)
        one_hot = c.sb(ctx, "choices", [P, 2, T * N_E])
        w12 = c.sb(ctx, "choice_weights", [P, 2, T])
        at12 = c.sb(ctx, "choice_rows", [P, 2, T], U32)
        erow = c.sb(ctx, "expert_rows", [P, SLOTS], U32)
        zero = free(6, D)
        xs = free(3, 1024).rearrange("p (b n) -> p b n", b=2)
        xsT = free(4, 1024).rearrange("p (b k n) -> p b k n", b=2, k=KD)
        ysb = free(5, 1024).rearrange("p (b n) -> p b n", b=2)

        def gather_expert(pool, q):
            pool.indirect_dma_start(wexp[:, q % 2, :], None, c.dram["L1_experts"],
                                    bass.IndirectOffsetOnAxis(ap=erow[:, q:q + 1], axis=0)).then_inc(c.we_loaded[q % 2], 16)

        def zeros(block, s):
            @block.gpsimd
            def _(pool):
                pool.memset(zero[:, :], 0.0).then_inc(s["zero_set"], 1)

            @block.sync
            def _(sp):
                sp.wait_ge(s["zero_set"], 1)
                sp.dma_start(sorted_x.rearrange("(a p) d -> p a d", p=P),
                             zero[:, :].unsqueeze(1).broadcast_to([P, SLOTS * SG // P, D])).then_inc(c.zero_stored, 16)

        norm_and_turn(c, c.xn, t_tok, None, [c.const("ln1g")[:, k:k + 1] for k in range(KD)],
                      [c.const("ln1b")[:, k:k + 1] for k in range(KD)], "zero_set", zeros)

        def products(block, s):
            @block.tensor
            def _(pe):
                pe.wait_ge(c.wb_loaded, c.wb_count)
                for t in range(T):
                    if t >= 8:
                        pe.wait_ge(s["y_free"], t - 7)
                    for k in range(KD):
                        mm = pe.matmul(c.banks[t % 8][:, 0:D], c.xnT[:, k, t * P:(t + 1) * P], wa[:, k, :],
                                       start=(k == 0), stop=(k == KD - 1))
                    mm.then_inc(s["y_ready"], 1)

        def add(dve, s, t):
            dve.wait_ge(s["y_ready"], t + 1)
            dve.tensor_tensor(tok(c.xn, t), tok(c.xn, t), c.banks[t % 8][:, 0:D], ALU.add).then_inc(s["y_free"], 1)

        norm_and_turn(c, c.xn, t_tok, add, [c.const("ln2g")[:, k:k + 1] for k in range(KD)],
                      [c.const("ln2b")[:, k:k + 1] for k in range(KD)], "y_ready", products)

        s = Sems(c, "step counted scattered" + ROUTE)
        tot = c.sb(ctx, "tile_counts", [P, T * N_E])
        run = c.sb(ctx, "rows_before", [P, T, N_E])
        ex = c.sb(ctx, "expert_counts", [P, 4, N_E])
        cmp = c.sb(ctx, "slot_ends", [P, SLOTS, N_E])
        fl = c.sb(ctx, "rows_float", [P, 2, T])
        es = c.sb(ctx, "slot_experts", [P, SLOTS])
        best_one, next_one = (one_hot[:, j, :].rearrange("p (t e) -> p t e", e=N_E) for j in range(2))
        with c.nc.Block() as block:
            on_vector, on_scalar = route(c, block, s, c.banks[0][:, 0:T * N_E].rearrange("p (t e) -> p t e", e=N_E),
                                         N_E, comb, work, False, best_one, next_one)

            @block.tensor
            def _(pe):
                router_logits(c, pe, s, wr, N_E, c.banks[0])
                pe.wait_ge(s["comb_ready"], 1)
                for bank, w in ((1, c.const("before")), (2, c.ones[:, :])):
                    for j in range(2):
                        mm = pe.matmul(c.banks[bank][:, 0:T * N_E], w, one_hot[:, j, :], start=(j == 0), stop=(j == 1))
                mm.then_inc(s["counted"], 1)

            @block.vector
            def _(dve):
                dve.wait_ge(s["logits_ready"], 1)
                on_vector(dve)
                steps = [0]

                def step(ins):
                    steps[0] += 1
                    ins.then_inc(s["step"], 1)
                    dve.wait_ge(s["step"], steps[0])

                cb = comb[:, :].rearrange("p (t e) -> p t e", e=N_E)
                pick = work[:, 0:T * N_E].rearrange("p (t e) -> p t e", e=N_E)
                for j, one in enumerate((best_one, next_one)):
                    step(dve.tensor_tensor(pick, cb, one, ALU.mult))
                    step(dve.tensor_reduce(w12[:, j, :], pick, AX.X, ALU.add))
                dve.wait_ge(s["counted"], 1)
                step(dve.tensor_copy(tot[:, :], c.banks[2][:, 0:T * N_E]))
                step(dve.memset(run[:, 0, :], 0.0))
                for t in range(1, T):
                    step(dve.tensor_tensor(run[:, t, :], run[:, t - 1, :], tot[:, (t - 1) * N_E:t * N_E], ALU.add))
                count, slots, ends, first = (ex[:, n, :] for n in range(4))
                step(dve.tensor_tensor(count, run[:, T - 1, :], tot[:, (T - 1) * N_E:T * N_E], ALU.add))
                step(dve.tensor_scalar(slots, count, 1.0 / SG, 0.5 - 1 / (2.0 * SG), ALU.mult, ALU.add))
                step(dve.tensor_scalar(slots, slots, ROUND, -ROUND, ALU.add, ALU.add))
                step(dve.tensor_tensor_scan(ends, c.ones[:, 0:N_E], slots, 0.0, ALU.mult, ALU.add))
                step(dve.tensor_tensor(first, ends, slots, ALU.subtract))
                step(dve.tensor_scalar(first, first, float(SG), None, ALU.mult))
                step(dve.tensor_tensor(run[:, :, :], run[:, :, :], first.unsqueeze(1).broadcast_to([P, T, N_E]), ALU.add))
                step(dve.tensor_tensor(run[:, :, :], run[:, :, :],
                                       c.banks[1][:, 0:T * N_E].rearrange("p (t e) -> p t e", e=N_E), ALU.add))
                for j, one in enumerate((best_one, next_one)):
                    step(dve.tensor_tensor(pick, run[:, :, :], one, ALU.mult))
                    step(dve.tensor_reduce(fl[:, j, :], pick, AX.X, ALU.add))
                step(dve.tensor_copy(at12[:, :, :], fl[:, :, :]))
                dve.sem_inc(s["scattered"], 1)
                step(dve.tensor_tensor(cmp[:, :, :], ends.unsqueeze(1).broadcast_to([P, SLOTS, N_E]),
                                       c.const("counting")[:, 0:SLOTS].unsqueeze(2).broadcast_to([P, SLOTS, N_E]), ALU.is_le))
                step(dve.tensor_reduce(es[:, :], cmp[:, :, :], AX.X, ALU.add))
                step(dve.tensor_scalar(es[:, :], es[:, :], N_E - 1.0, float(P), ALU.min, ALU.mult))
                step(dve.tensor_scalar(es[:, :], es[:, :], c.const("places")[:, 0:1], None, ALU.add))
                step(dve.tensor_copy(erow[:, :], es[:, :]))

            @block.scalar
            def _(act):
                on_scalar(act)
        s.close()

        s = Sems(c, "scattered")
        with c.nc.Block() as block:
            @block.gpsimd
            def _(pool):
                for q in range(2):
                    gather_expert(pool, q)
                pool.wait_ge(c.zero_stored, 16)
                for j in range(2):
                    for t in range(T):
                        pool.indirect_dma_start(sorted_x, bass.IndirectOffsetOnAxis(ap=at12[:, j, t:t + 1], axis=0),
                                                t_tok[:, t * D:(t + 1) * D], None).then_inc(s["scattered"], 16)
                pool.wait_ge(s["scattered"], 16 * 2 * T)
        s.close()

        s = Sems(c, "x_loaded0 x_loaded1 x_turned xT_ready y_ready y_evac y_stored0 y_stored1 gate_up_ready silu_done h_ready "
                    "downed gate_pe gate_act gate_dve")
        x_loaded, y_stored = (s["x_loaded0"], s["x_loaded1"]), (s["y_stored0"], s["y_stored1"])
        TB_, YB_ = 4, (5, 6)

        def every_slot(e, body):
            with e.Fori(0, SLOTS // 2) as i:
                for p in range(2):
                    body(i, p)
            if SLOTS % 2:
                body(SLOTS // 2, 0)

        def slot_of(ap, q):
            v = ap.rearrange("(q j p) d -> q p j d", j=SG // P, p=P)
            return v[q] if isinstance(q, int) else v[bass.ds(q, 1)].rearrange("q p j d -> (q p) j d")

        def turn(pe, i, p):
            held(pe, x_loaded[p], 16 * (i + 1), s["gate_pe"])
            for j in range(SG // P):
                for k in range(KD):
                    mm = pe.transpose(c.banks[TB_][:, k * SG + j * P:k * SG + (j + 1) * P],
                                      xs[:, p, j * D + k * P:j * D + (k + 1) * P], c.ident[:, :])
            mm.then_inc(s["x_turned"], 1)

        with c.nc.Block() as block:
            @block.sync
            def _(sp):
                load_next(c, sp)

                def load(q, p):
                    sp.dma_start(xs[:, p, :].rearrange("p (j d) -> p j d", d=D), slot_of(sorted_x, q)).then_inc(x_loaded[p], 16)

                def store(q, p):
                    sp.wait_ge(s["y_evac"], q + 3)
                    sp.dma_start(slot_of(sorted_y, q), ysb[:, p, :].rearrange("p (j d) -> p j d", d=D)).then_inc(y_stored[p], 16)

                load(0, 0)
                load(1, 1)
                with sp.Fori(0, (SLOTS - 2) // 2) as i:
                    for p in range(2):
                        q = 2 * i + p
                        sp.wait_ge(s["x_turned"], q + 1)
                        load(q + 2, p)
                        store(q, p)
                for q in range((SLOTS - 2) // 2 * 2, SLOTS):
                    if q + 2 < SLOTS:
                        sp.wait_ge(s["x_turned"], q + 1)
                        load(q + 2, q % 2)
                    store(q, q % 2)
                for p in range(2):
                    sp.wait_ge(y_stored[p], 16 * ((SLOTS + 1 - p) // 2 + 1))

            @block.gpsimd
            def _(pool):
                for q in range(2, SLOTS):
                    pool.wait_ge(s["downed"], (q - 1) * EB + 4)
                    gather_expert(pool, q)

            @block.tensor
            def _(pe):
                turn(pe, 0, 0)
                pe.sem_inc(s["downed"], 4)

                def slot(i, p):
                    q = 2 * i + p
                    w = wexp[:, p, :]
                    held(pe, c.we_loaded[p], 16 * (i + 1), s["gate_pe"])
                    held(pe, s["xT_ready"], q + 1, s["gate_pe"])
                    for m in range(EB + 1):
                        if m < EB:
                            held(pe, s["h_ready"], q * EB + m + 1, s["gate_pe"])
                            for j in range(2):
                                for k in range(KD):
                                    o = (j * KD + k) * INTER + m * P
                                    mm = pe.matmul(c.banks[m % 4][:, j * SG:(j + 1) * SG], w[:, o:o + P], xsT[:, p, k, :],
                                                   start=(k == 0), stop=(k == KD - 1), skip_group_check=True)
                            mm.then_inc(s["gate_up_ready"], 1)
                        if m == 4 and not (isinstance(i, int) and q == SLOTS - 1):
                            turn(pe, i if p == 0 else i + 1, 1 - p)
                        if m == 1:
                            held(pe, s["y_evac"], q + 1, s["gate_pe"])
                        if m >= 1:
                            held(pe, s["h_ready"], q * EB + m + 4, s["gate_pe"])
                            o = 2 * KD * INTER + (m - 1) * D
                            for j in range(SG // P):
                                mm = pe.matmul(c.banks[YB_[p]][:, j * D:(j + 1) * D], hT[:, (m - 1) % 4, j * P:(j + 1) * P],
                                               w[:, o:o + D], start=(m == 1 and j == 0), stop=(m == EB), skip_group_check=True)
                            mm.then_inc(s["downed"], 1)
                every_slot(pe, slot)

            @block.scalar
            def _(act):
                def xT(i, p):
                    act.wait_ge(s["x_turned"], 2 * i + p + 1)
                    for k in range(KD):
                        ins = act.activation(xsT[:, p, k, :], c.banks[TB_][:, k * SG:(k + 1) * SG], ACT.Identity,
                                             bias=c.const("ln2b")[:, k:k + 1], scale=c.const("ln2g")[:, k:k + 1])
                    ins.then_inc(s["xT_ready"], 1)

                xT(0, 0)

                def slot(i, p):
                    for m in range(EB):
                        n = (2 * i + p) * EB + m
                        held(act, s["h_ready"], n + 1, s["gate_act"])
                        act.wait_ge(s["gate_up_ready"], n + 1)
                        act.activation(sg[:, m % 4, :], c.banks[m % 4][:, 0:SG], ACT.Silu).then_inc(s["silu_done"], 1)
                        if m == 4 and not (isinstance(i, int) and 2 * i + p == SLOTS - 1):
                            xT(i if p == 0 else i + 1, 1 - p)
                every_slot(act, slot)

            @block.vector
            def _(dve):
                dve.sem_inc(s["h_ready"], 4)
                dve.sem_inc(s["y_evac"], 2)
                for p in range(2):
                    dve.sem_inc(y_stored[p], 16)

                def slot(i, p):
                    q = 2 * i + p
                    for m in range(EB):
                        n = q * EB + m
                        held(dve, s["downed"], n + 1, s["gate_dve"])
                        dve.wait_ge(s["silu_done"], n + 1)
                        dve.tensor_tensor(hT[:, m % 4, :], sg[:, m % 4, :], c.banks[m % 4][:, SG:2 * SG], ALU.mult).then_inc(s["h_ready"], 1)
                    held(dve, s["downed"], (q + 1) * EB + 4, s["gate_dve"])
                    held(dve, y_stored[p], 16 * (i + 1), s["gate_dve"])
                    dve.tensor_copy(ysb[:, p, :], c.banks[YB_[p]][:, :]).then_inc(s["y_evac"], 1)
                every_slot(dve, slot)
        s.close()

        yg = wexp[:, :, :].rearrange("p e n -> p (e n)")[:, 0:2 * T * D].rearrange("p (t j d) -> p t j d", t=T, j=2)

        def fetch(block, s):
            @block.gpsimd
            def _(pool):
                for t in range(T):
                    for j in range(2):
                        pool.indirect_dma_start(yg[:, t, j, :], None, sorted_y,
                                                bass.IndirectOffsetOnAxis(ap=at12[:, j, t:t + 1], axis=0)
                                                ).then_inc(s[f"rows{t // 2}"], 16)

        def add_rows(dve, s, t):
            ht = tok(c.xn, t)
            if t % 2 == 0:
                dve.wait_ge(s[f"rows{t // 2}"], 16 * 4)
            for j in range(2):
                dve.scalar_tensor_tensor(out=ht, in0=yg[:, t, j, :], scalar=w12[:, j, t:t + 1], in1=ht,
                                         op0=ALU.mult, op1=ALU.add).then_inc(s["weighed"], 1)
                dve.wait_ge(s["weighed"], 2 * t + j + 1)
            dve.scalar_tensor_tensor(out=tok(c.x, t), in0=ht, scalar=c.tg[:, 3:4], in1=tok(c.x, t),
                                     op0=ALU.mult, op1=ALU.add).then_inc(s["y_free"], 1)

        norm_and_turn(c, c.x, c.xn, add_rows, names="weighed " + " ".join(f"rows{n}" for n in range(T // 2)), others=fetch)



L2X = Heads(H=16, DH=64, NK=M, HG=4, QB=8, masked=True)
FLT_MAX = 3.4028234663852886e38


def load_l2x(c, sp):
    d, w = c.dram, c.wa
    for n, (src, k) in enumerate(((d["L2_WqT"], KD), (d["L2_WkT"], KD), (d["L2_WvT"], KD), (d["L2_WoutT"], 8))):
        c.load_a(sp, w[:, n * 2048:(n + 1) * 2048].rearrange("p (k n) -> p k n", k=k), rows(src, k))


def layer2_attention(c, load_next):
    a = L2X
    W, C = B * M, 16 * 64
    wq, wk, wv = (c.wa[:, n * 2048:(n + 1) * 2048].rearrange("p (k n) -> p k n", k=KD) for n in range(3))
    wo = c.wa[:, 6144:8192].rearrange("p (k n) -> p k n", k=8)
    with ExitStack() as ctx:
        kb = c.sb(ctx, "l2_keys", [P, B * 16 * M])
        vm = c.sb(ctx, "l2_values", [P, B * C])
        vl = c.sb(ctx, "l2_values_last", [P, B * C])
        mb = c.wb[:, 7168:7168 + W]
        with ExitStack() as prep:
            m01 = c.sb(prep, "mask_ones", [P, W])
            mu8 = c.sb(prep, "mask_bytes", [P, W], U8)
            ctxm = c.sb(prep, "ctx_masked", [P, KD, W])
            s = Sems(c, "mask_loaded step job k_evac v_evac done")
            with c.nc.Block() as block:
                @block.sync
                def _(sp):
                    sp.dma_start(mu8[:, :], c.dram["mask"]).then_inc(s["mask_loaded"], 16)

                @block.tensor
                def _(pe):
                    pe.wait_ge(c.wa_loaded, c.wa_count)
                    for n in range(8):
                        b, half = n // 2 % 2, n % 2
                        r = P if n < 4 else 104
                        for k in range(KD):
                            lhs = c.ctxT[:, k, b * M:b * M + P] if n < 4 else c.ctxR[:, k, b, :]
                            mm = pe.matmul(c.banks[n][0:r, :], lhs, wv[:, k, half * 512:(half + 1) * 512],
                                           start=(k == 0), stop=(k == KD - 1))
                        mm.then_inc(s["job"], 1)
                    pe.wait_ge(s["step"], 4)
                    for n in range(8):
                        pe.wait_ge(s["v_evac"], n + 1)
                        for k in range(KD):
                            mm = pe.matmul(c.banks[n][:, 0:W], wk[:, k, n * P:(n + 1) * P], ctxm[:, k, :],
                                           start=(k == 0), stop=(k == KD - 1))
                        mm.then_inc(s["job"], 1)

                @block.scalar
                def _(act):
                    for n in range(8):
                        b, half = n // 2 % 2, n % 2
                        r, to = (P, vm) if n < 4 else (104, vl)
                        act.wait_ge(s["job"], n + 1)
                        act.activation(to[0:r, b * C + half * 512:b * C + (half + 1) * 512], c.banks[n][0:r, :],
                                       ACT.Copy).then_inc(s["v_evac"], 1)

                @block.vector
                def _(dve):
                    dve.wait_ge(s["mask_loaded"], 16)
                    dve.tensor_copy(m01[:, :], mu8[:, :]).then_inc(s["step"], 1)
                    dve.wait_ge(s["step"], 1)
                    dve.tensor_scalar(mb[:, :], m01[:, :], -1.0, FLT_MAX, ALU.add, ALU.mult).then_inc(s["step"], 1)
                    for k in range(KD):
                        dve.tensor_tensor(ctxm[:, k, :], c.ctxT[:, k, :], m01[:, :], ALU.mult).then_inc(s["step"], 1)
                    kbv = kb[:, :].rearrange("p (b h k) -> p b h k", b=B, h=16)
                    for h in range(16):
                        dve.wait_ge(s["job"], 8 + h // 2 + 1)
                        dve.tensor_scalar(kbv[:, :, h, :], c.banks[h // 2][:, 0:W].rearrange("p (b k) -> p b k", b=B),
                                          c.const("heads64")[:, h % 2:h % 2 + 1], None, ALU.mult).then_inc(s["k_evac"], 1)
                    dve.wait_ge(s["v_evac"], 8)
                    for b in range(B):
                        v = vl[0:104, b * C:(b + 1) * C].rearrange("p (g n) -> p g n", g=4)
                        dve.tensor_tensor(v, v, c.const("left64")[0:104, :].unsqueeze(1).broadcast_to([104, 4, 256]),
                                          ALU.mult).then_inc(s["done"], 1)
            s.close()

        m = AttentionMemory(c, ctx, a, "_l2", {
            "osb": c.wb[:, 4096:5120], "ot": c.wb[:, 5120:6144].rearrange("p (k n) -> p k n", k=8),
            "pl": c.wb[:, 6144:6144 + 2 * a.H * a.NL].rearrange("p (i n) -> p i n", i=2)})
        s = Sems(c, "q_projected" + ATT + TAIL)
        with c.nc.Block() as block:
            @block.sync
            def _(sp):
                load_next(c, sp)

            def q_pe(pe, t):
                cols = slice(t * P, (t + 1) * P) if isinstance(t, int) else bass.ds(t * P, P)
                if isinstance(t, int) and t == 1:
                    pe.wait_ge(s["q_ready"], 1)
                for n in range(8):
                    for k in range(KD):
                        mm = pe.matmul(c.banks[TURN[n // 4]][:, n % 4 * P:(n % 4 + 1) * P], wq[:, k, n * P:(n + 1) * P],
                                       c.xnT[:, k, cols], start=(k == 0), stop=(k == KD - 1), skip_group_check=True)
                mm.then_inc(s["q_projected"], 1)

            def q_act(act, t, p):
                act.wait_ge(s["q_projected"], t + 1)
                for b in range(2):
                    ins = act.activation(m.q[:, p, 4 * b:4 * b + 4, :], c.banks[TURN[b]][:, :], ACT.Copy)
                ins.then_inc(s["q_ready"], 1)

            attention(c, block, s, a, m, Parts(
                q_pe=q_pe, q_act=q_act, stage=None, mask=lambda i: mb[:, at(i, M, 0, M)],
                keys=lambda i, h, kk: kb[:, at(i, 16 * M, h * M, M)],
                values=lambda i, h: vm[:, at(i, C, h * 64, 64)],
                left=lambda i, g: vl[0:104, at(i, C, g * 256, 256)],
                project=(lambda i, k: wo[:, k, :], c.vrow("L2_xattn_b_out")),
                finish_dve=lambda dve, t, p, first: tail_dve(c, dve, s, t, p, first, c.banks[YB][:, 0:D], 4),
                finish_pool=lambda pool, t, p: tail_pool(c, pool, s, t, p)))
        s.close()



GATES, NQ, NKV, RH, RD = 4, 256, 128, 8, 64
RC = RH * RD
PAIRS = B * GATES
R_W = 2 * RC + 4 * RC + 4 * D
L2F = Heads(H=RH, DH=RD, NK=NKV + 1, HG=RH, QB=RC // P)
PICKED = -3.0e38


def load_l2f(c, sp):
    sp.dma_start(c.wb[:, 0:R_W], c.dram["L2_gates"][0]).then_inc(c.wr_loaded[0], 16)


def layer2_routed(c, load_next):
    a = L2F
    NR, ST_ = 2 * PAIRS, S // P
    with ExitStack() as ctx:
        pos = c.sb(ctx, "place_rows", [NR, S], F32R)
        posT = c.sb(ctx, "place_tok", [P, ST_, NR])
        sigT = c.sb(ctx, "sigmoid_tok", [P, ST_, NR])
        wr = c.sb(ctx, "routing_weights", [P, KD, 2, NR])
        with ExitStack() as prep:
            sig = c.sb(prep, "sigmoid_rows", [NR, S])
            lg = c.sb(prep, "logit_rows", [NR, S])
            early = c.sb(prep, "chosen_128", [NR, S])
            one = c.sb(prep, "row_ones", [NR, S])
            best = c.sb(prep, "best8", [NR, 8])
            s = Sems(c, "w_loaded logits evac best_ready replaced step rows_ready rows_turned turned_evac gate_dve")
            with c.nc.Block() as block:
                @block.sync
                def _(sp):
                    sp.dma_start(wr[:, :, :, :], c.dram["L2_routing"].rearrange("(k p) b n -> p k b n", p=P)).then_inc(s["w_loaded"], 16)

                @block.tensor
                def _(pe):
                    pe.wait_ge(s["w_loaded"], 16)
                    for half in range(2):
                        for n in range(2 * KD):
                            b, k = n // KD, n % KD
                            at = b * S + half * CH
                            mm = pe.matmul(c.banks[half][0:NR, :], wr[:, k, b, :], c.xnT[:, k, at:at + CH],
                                           start=(n == 0), stop=(n == 2 * KD - 1))
                        mm.then_inc(s["logits"], 1)
                    pe.wait_ge(s["rows_ready"], 2)
                    for n, src in enumerate((pos[:, :].bitcast(F32), sig)):
                        for t in range(ST_):
                            mm = pe.transpose(c.banks[2 + n][:, t * NR:(t + 1) * NR], src[:, t * P:(t + 1) * P], c.ident[0:NR, 0:NR])
                        mm.then_inc(s["rows_turned"], 1)

                @block.scalar
                def _(act):
                    for half in range(2):
                        act.wait_ge(s["logits"], half + 1)
                        act.activation(lg[:, half * CH:(half + 1) * CH], c.banks[half][0:NR, :], ACT.Copy).then_inc(s["evac"], 1)
                    act.activation(sig[:, 0:CH], c.banks[0][0:NR, :], ACT.Sigmoid)
                    act.activation(sig[:, CH:S], c.banks[1][0:NR, :], ACT.Sigmoid).then_inc(s["rows_ready"], 1)
                    act.wait_ge(s["rows_turned"], 2)
                    act.activation(posT[:, :, :], c.banks[2][:, 0:ST_ * NR], ACT.Copy)
                    act.activation(sigT[:, :, :], c.banks[3][:, 0:ST_ * NR], ACT.Copy).then_inc(s["turned_evac"], 1)

                @block.vector
                def _(dve):
                    dve.memset(one[:, :], 1.0)
                    dve.wait_ge(s["evac"], 2)
                    for stage in range(2):
                        with dve.Fori(0, NKV // 8) as i:
                            n = stage * (NKV // 8) + i
                            dve.max(best[:, :], lg[:, :]).then_inc(s["best_ready"], 1)
                            held(dve, s["best_ready"], n + 1, s["gate_dve"])
                            dve.match_replace(lg[:, :], best[:, :], lg[:, :], PICKED).then_inc(s["replaced"], 1)
                            held(dve, s["replaced"], n + 1, s["gate_dve"])
                        if stage == 0:
                            dve.tensor_scalar(early[:, :], lg[:, :], PICKED, None, ALU.is_equal).then_inc(s["step"], 1)
                    dve.wait_ge(s["step"], 1)
                    dve.tensor_scalar(lg[:, :], lg[:, :], PICKED, c.const("query_rows")[0:NR, :], ALU.is_equal, ALU.mult).then_inc(s["step"], 1)
                    dve.wait_ge(s["step"], 2)
                    dve.scalar_tensor_tensor(out=lg[:, :], in0=early[:, :], scalar=c.const("key_rows")[0:NR, :], in1=lg[:, :],
                                             op0=ALU.mult, op1=ALU.add).then_inc(s["step"], 1)
                    dve.wait_ge(s["step"], 3)
                    dve.tensor_tensor_scan(early[:, :], one[:, :], lg[:, :], 0.0, ALU.mult, ALU.add).then_inc(s["step"], 1)
                    dve.wait_ge(s["step"], 4)
                    dve.tensor_tensor(early[:, :], early[:, :], lg[:, :], ALU.mult).then_inc(s["step"], 1)
                    dve.wait_ge(s["step"], 5)
                    dve.tensor_scalar(pos[:, :], early[:, :], -1.0, None, ALU.add).then_inc(s["rows_ready"], 1)
            s.close()

        kb = c.sb(ctx, "l3_keys", [P, RH, NKV + 1])
        vm = c.sb(ctx, "l3_values", [P, RC])
        vl = c.sb(ctx, "l3_null_values", [RH, 2, RC])
        nk = c.sb(ctx, "null_keys", [P, PAIRS // B * 4])
        nv = c.sb(ctx, "null_values", [RH, GATES * RC])
        sel = c.sb(ctx, "chosen", [P, ST_, NQ + NKV], F32R)
        xhl = c.sb(ctx, "xn_halves", [P, 2, ST_ * D], F32R)
        back = c.sb(ctx, "chosen_back", [P, 2, S], F32R)
        posb = c.wa[:, 0:S]
        xq = c.sb(ctx, "chosen_queries", [P, KD, NQ])
        xk = c.sb(ctx, "chosen_keys", [P, KD, NKV])
        scores = c.sb(ctx, "chosen_scores", [P, 2, 3])
        osc = c.sb(ctx, "gate_out", [P, 2, D])
        osh = c.sb(ctx, "gate_out_halves", [P, 2, 2, D], F32R)
        pick = c.sb(ctx, "row_pick", [NR, 2, P], F32R)
        cnt = c.sb(ctx, "counts", [P, 4 * T])
        msk = c.sb(ctx, "picked_tok", [P, B, ST_, GATES])
        nul = c.sb(ctx, "null_wide", [P, D])
        m = AttentionMemory(c, ctx, a, "_r", {
            "q": c.wa[:, S:2 * S].rearrange("p (i k n) -> p i k n", i=2, k=4),
            "p": c.wa[:, 2 * S:2 * S + 2 * RH * L2F.NK].rearrange("p (i h n) -> p i h n", i=2, h=RH),
            "pt": c.wa[:, 4608:4608 + (RH + 1) * P].rearrange("p (h n) -> p h n", n=P),
            "osb": c.wa[:, 6144:6656], "ot": c.wa[:, 6656:7168].rearrange("p (k n) -> p k n", k=4)})
        acc = c.xnT[:, :, :].rearrange("p k n -> p (k n)")
        s = Sems(c, "nulls_loaded sel_ready gathered x_evac qkv_done kv_evac keys_ready wide_ready pos_evac back_ready scattered "
                    "summed scored high_ready finished pick_ready halved" + ATT + TAIL)

        def weights(i):
            w = c.wb[:, i % 2 * R_W:(i % 2 + 1) * R_W]
            return (w[:, 0:2 * RC].rearrange("p (k n) -> p k n", k=KD), w[:, 2 * RC:6 * RC].rearrange("p (k n) -> p k n", k=KD),
                    w[:, 6 * RC:6 * RC + 4 * D].rearrange("p (k n) -> p k n", k=4))

        def row(i):
            return i // GATES * 2 * GATES + i % GATES

        with c.nc.Block() as block:
            @block.sync
            def _(sp):
                sp.dma_start(nk[:, :], c.dram["L2_null_k"]).then_inc(s["nulls_loaded"], 16)
                sp.dma_start(nv[:, :], c.dram["L2_null_v"]).then_inc(s["nulls_loaded"], 16)
                sp.dma_start(nul[:, :], c.dram["L2_null_token"]).then_inc(s["nulls_loaded"], 16)
                for i in range(1, PAIRS):
                    if i >= 2:
                        sp.wait_ge(s["y_ready"], 2 * (i - 1))
                    sp.dma_start(c.wb[:, i % 2 * R_W:(i % 2 + 1) * R_W], c.dram["L2_gates"][i % GATES]).then_inc(c.wr_loaded[i % 2], 16)
                load_next(c, sp)

            @block.tensor
            def _(pe):
                def gather(i):
                    r = row(i)
                    pe.wait_ge(s["sel_ready"], i + 1)
                    for kd in range(KD):
                        for t in range(ST_):
                            at = t * D + kd * P
                            for half, src in enumerate((xhl[:, 0, at:at + P], xhl[:, 1, at:at + P])):
                                mm = pe.matmul(c.banks[TURN[kd]][:, 0:NQ + NKV], src, sel[:, t, :],
                                               start=(t == 0 and half == 0), stop=(t == ST_ - 1), skip_group_check=True)
                    for j, n in enumerate((r, r, r + GATES)):
                        for t in range(ST_):
                            mm = pe.matmul(c.banks[TURN[1]][:, NQ + NKV + j:NQ + NKV + j + 1], sel[:, t, j * P:(j + 1) * P].bitcast(F32),
                                           sigT[:, t, n:n + 1], start=(t == 0), stop=(t == ST_ - 1), skip_group_check=True)
                    mm.then_inc(s["gathered"], 1)

                def qkv(i):
                    wq, wkv, _ = weights(i)
                    pe.wait_ge(c.wr_loaded[i % 2], 16 * (i // 2 + 1))
                    pe.wait_ge(s["x_evac"], i + 1)
                    if i:
                        pe.wait_ge(s["exped"], a.G * 2 * i)
                    for n in range(4):
                        for k in range(KD):
                            pe.matmul(c.banks[0][:, n * P:(n + 1) * P], wkv[:, k, n * P:(n + 1) * P], xk[:, k, :],
                                      start=(k == 0), stop=(k == KD - 1), skip_group_check=True)
                    for k in range(KD):
                        mm = pe.matmul(c.banks[1][:, :], xk[:, k, :], wkv[:, k, RC:2 * RC], start=(k == 0), stop=(k == KD - 1))
                    mm.then_inc(s["qkv_done"], 1)
                    for n in range(4):
                        for k in range(KD):
                            mm = pe.matmul(c.banks[TURN[n // 2]][:, n % 2 * NQ:(n % 2 + 1) * NQ], wq[:, k, n * P:(n + 1) * P],
                                           xq[:, k, :], start=(k == 0), stop=(k == KD - 1), skip_group_check=True)
                    mm.then_inc(s["qkv_done"], 1)

                def scatter(i):
                    pe.wait_ge(s["pick_ready"], i + 1)
                    pe.wait_ge(s["q_ready"], min(2 * (i + 2), 2 * PAIRS))
                    pe.wait_ge(s["finished"], 2 * i + 2)
                    for half in range(2):
                        mm = pe.matmul(c.banks[(3, 5)[half]][:, :], pick[:, i % 2, :], pos[:, half * CH:(half + 1) * CH], start=True, stop=True)
                    mm.then_inc(s["wide_ready"], 1)
                    pe.wait_ge(s["back_ready"], i + 1)
                    for f in range(ST_ // 2):
                        if f >= 2:
                            pe.wait_ge(s["summed"], 4 * i + f - 1)
                        for u in range(2):
                            t = 2 * f + u
                            for j in range(2):
                                for half in range(2):
                                    mm = pe.matmul(c.banks[OB[1 - f % 2]][:, u * D:(u + 1) * D], back[:, j, t * P:(t + 1) * P],
                                                   osh[:, j, half, :], start=(j == 0 and half == 0), stop=(j == 1 and half == 1),
                                                   skip_group_check=True)
                        mm.then_inc(s["scattered"], 1)

                def finish(t):
                    att_finish_pe(c, pe, s, a, m, t // 2, t, lambda i, k: weights(i)[2][:, k, :], None)

                pe.wait_ge(s["nulls_loaded"], 48)
                gather(0)
                for i in range(PAIRS):
                    qkv(i)
                    if i:
                        finish(2 * i - 1)
                    pe.wait_ge(s["keys_ready"], i + 1)
                    pe.wait_ge(s["kv_evac"], i + 1)
                    for p in range(2):
                        t = 2 * i + p
                        att_scores(c, pe, s, a, m, i, t, p, i == 0, lambda i, h, kk: kb[:, h, :])
                        if p == 0 and i:
                            scatter(i - 1)
                            pe.wait_ge(s["summed"], 4 * i)
                        if p == 1:
                            if i + 1 < PAIRS:
                                gather(i + 1)
                            finish(t - 1)
                            if i + 1 < PAIRS:
                                pe.wait_ge(s["x_evac"], i + 2)
                        att_turn(c, pe, s, a, m, t, p)
                        att_values(c, pe, s, a, m, i, t, p, lambda i, h: vm[:, h * RD:(h + 1) * RD], lambda i, g: vl[:, i % 2, :])
                finish(T - 1)
                scatter(PAIRS - 1)

            @block.scalar
            def _(act):
                def places(i):
                    act.wait_ge(s["wide_ready"], i + 1)
                    act.activation(posb[:, 0:CH], c.banks[3][:, :], ACT.Copy)
                    act.activation(posb[:, CH:S], c.banks[5][:, :], ACT.Copy).then_inc(s["pos_evac"], 1)

                def tokens(i):
                    act.wait_ge(s["gathered"], i + 1)
                    if i >= 2:
                        act.wait_ge(s["finished"], 2 * (i - 1))
                    act.activation(scores[:, i % 2, :], c.banks[TURN[1]][:, NQ + NKV:NQ + NKV + 3], ACT.Copy)
                    for kd in range(KD):
                        act.activation(xq[:, kd, :], c.banks[TURN[kd]][:, 0:NQ], ACT.Copy)
                        ins = act.activation(xk[:, kd, :], c.banks[TURN[kd]][:, NQ:NQ + NKV], ACT.Copy)
                    ins.then_inc(s["x_evac"], 1)

                tokens(0)
                for i in range(PAIRS):
                    act.wait_ge(s["qkv_done"], 2 * i + 1)
                    act.wait_ge(s["x_evac"], i + 1)
                    act.activation(vm[:, :], c.banks[1][:, :], ACT.Copy, scale=scores[:, i % 2, 2:3]).then_inc(s["kv_evac"], 1)
                    act.wait_ge(s["qkv_done"], 2 * i + 2)
                    for p in range(2):
                        for n in range(2):
                            of = c.banks[TURN[n]][:, :].rearrange("p (n t q) -> p n t q", n=2, t=2)
                            ins = act.activation(m.q[:, p, 2 * n:2 * n + 2, :], of[:, :, p, :], ACT.Copy)
                        ins.then_inc(s["q_ready"], 1)
                    if i:
                        att_finish_act(c, act, s, a, m, 2 * i - 1)
                    for p in range(2):
                        t = 2 * i + p
                        if p == 0 and i:
                            places(i - 1)
                        att_exp(c, act, s, a, m, t, p)
                        if p == 1:
                            if i + 1 < PAIRS:
                                tokens(i + 1)
                            att_finish_act(c, act, s, a, m, t - 1)
                        att_evacuate(c, act, s, a, m, t, p)
                att_finish_act(c, act, s, a, m, T - 1)
                places(PAIRS - 1)

            @block.vector
            def _(dve):
                def choose(i):
                    r = row(i)
                    if i:
                        dve.wait_ge(s["gathered"], i)
                    if i % GATES == 0:
                        b = i // GATES
                        v = c.xn[:, b * ST_ * D:(b + 1) * ST_ * D]
                        dve.tensor_copy(xhl[:, 0, :], v).then_inc(s["halved"], 1)
                        dve.wait_ge(s["halved"], 2 * b + 1)
                        dve.tensor_tensor(xhl[:, 1, :], v, xhl[:, 0, :].bitcast(F32), ALU.subtract).then_inc(s["halved"], 1)
                    dve.tensor_tensor(vl[:, i % 2, :], nv[:, i % GATES * RC:(i % GATES + 1) * RC], c.const("diag8")[0:RH, :], ALU.mult)
                    if i >= 2:
                        dve.wait_ge(s["wide_ready"], i - 1)
                    dve.tensor_scalar(pick[:, i % 2, :], c.ones[0:NR, :], c.ident[0:NR, r:r + 1], None, ALU.mult).then_inc(s["pick_ready"], 1)
                    for t in range(ST_):
                        dve.tensor_scalar(sel[:, t, 0:NQ], c.const("counting"), posT[:, t, r:r + 1], None, ALU.is_equal)
                        ins = dve.tensor_scalar(sel[:, t, NQ:NQ + NKV], c.const("counting")[:, 0:NKV],
                                                posT[:, t, r + GATES:r + GATES + 1], None, ALU.is_equal)
                    ins.then_inc(s["sel_ready"], 1)

                def keys(i):
                    dve.wait_ge(s["qkv_done"], 2 * i + 1)
                    if i:
                        dve.wait_ge(s["scores_ready"], a.G * 2 * i)
                    for e in range(2):
                        scale = c.const("heads64")[:, e:e + 1]
                        dve.tensor_scalar(kb[:, e::2, 0:NKV], c.banks[0][:, :].rearrange("p (n k) -> p n k", n=4), scale, None, ALU.mult)
                        ins = dve.tensor_scalar(kb[:, e::2, NKV], nk[:, i % GATES * 4:(i % GATES + 1) * 4], scale, None, ALU.mult)
                    ins.then_inc(s["keys_ready"], 1)

                def send_back(i):
                    dve.wait_ge(s["pos_evac"], i + 1)
                    for j in range(2):
                        ins = dve.tensor_scalar(back[:, j, :], posb[:, :], c.const("places")[:, j:j + 1], None, ALU.is_equal)
                    ins.then_inc(s["back_ready"], 1)
                    for f in range(ST_ // 2):
                        dve.wait_ge(s["scattered"], 4 * i + f + 1)
                        at = (i // GATES * ST_ + 2 * f) * D
                        to = acc[:, at:at + 2 * D]
                        src = c.banks[OB[1 - f % 2]][:, :]
                        if i % GATES == 0:
                            dve.tensor_copy(to, src).then_inc(s["summed"], 1)
                        else:
                            if f == 0:
                                dve.wait_ge(s["summed"], 4 * i)
                            dve.tensor_tensor(to, to, src, ALU.add).then_inc(s["summed"], 1)

                def finish(t):
                    dve.wait_ge(s["y_ready"], t + 1)
                    if t >= 2:
                        dve.wait_ge(s["scattered"], 4 * (t // 2))
                    dve.tensor_scalar(osc[:, t % 2, :], c.banks[YB][:, 0:D], scores[:, t // 2 % 2, t % 2:t % 2 + 1], None,
                                      ALU.mult).then_inc(s["scored"], 1)
                    dve.wait_ge(s["scored"], t + 1)
                    dve.tensor_copy(osh[:, t % 2, 0, :], osc[:, t % 2, :]).then_inc(s["high_ready"], 1)
                    dve.wait_ge(s["high_ready"], t + 1)
                    dve.tensor_tensor(osh[:, t % 2, 1, :], osc[:, t % 2, :], osh[:, t % 2, 0, :].bitcast(F32),
                                      ALU.subtract).then_inc(s["finished"], 1)

                dve.wait_ge(s["nulls_loaded"], 48)
                choose(0)
                for i in range(PAIRS):
                    keys(i)
                    if i:
                        finish(2 * i - 1)
                    for p in range(2):
                        t = 2 * i + p
                        att_max(c, dve, s, a, m, i, t, p, None)
                        if p == 0:
                            if i:
                                send_back(i - 1)
                            if i + 1 < PAIRS:
                                choose(i + 1)
                        else:
                            finish(t - 1)
                        att_normalise(c, dve, s, a, m, t, p)
                finish(T - 1)
                send_back(PAIRS - 1)

            @block.gpsimd
            def _(pool):
                for t in range(T):
                    pool.wait_ge(s["exped"], a.G * (t + 1))
                    pool.tensor_copy(m.pl[:, t % 2, :].rearrange("p (h k) -> p h k", k=a.NL),
                                     m.p[:, t % 2, :, P:a.NK]).then_inc(s["last_ready"], 1)
        s.close()

        n_, inv, zero = cnt[:, 0:T], cnt[:, T:2 * T], cnt[:, 2 * T:3 * T]

        def mean(dve, s, t):
            if t == 0:
                for b in range(B):
                    dve.tensor_scalar(msk[:, b, :, :], posT[:, :, b * 2 * GATES:b * 2 * GATES + GATES], 0.0, None,
                                      ALU.is_ge).then_inc(s["step"], 1)
                dve.wait_ge(s["step"], 2)
                dve.tensor_reduce(n_, msk[:, :, :, :].rearrange("p b t g -> p (b t) g"), AX.X, ALU.add).then_inc(s["step"], 1)
                dve.wait_ge(s["step"], 3)
                dve.tensor_scalar(inv, n_, 1e-5, None, ALU.max).then_inc(s["step"], 1)
                dve.tensor_scalar(zero, n_, 0.0, None, ALU.is_equal).then_inc(s["step"], 1)
                dve.wait_ge(s["step"], 5)
                dve.reciprocal(inv, inv).then_inc(s["step"], 1)
                dve.wait_ge(s["step"], 6)
            y = tok(acc, t)
            dve.tensor_scalar(y, y, inv[:, t:t + 1], None, ALU.mult).then_inc(s["mean_done"], 1)
            dve.wait_ge(s["mean_done"], t + 1)
            dve.scalar_tensor_tensor(out=y, in0=nul[:, :], scalar=zero[:, t:t + 1], in1=y,
                                     op0=ALU.mult, op1=ALU.add).then_inc(s["null_added"], 1)
            dve.wait_ge(s["null_added"], t + 1)
            dve.scalar_tensor_tensor(out=tok(c.x, t), in0=y, scalar=c.tg[:, 5:6], in1=tok(c.x, t),
                                     op0=ALU.mult, op1=ALU.add).then_inc(s["y_free"], 1)

        norm_and_turn(c, c.x, c.xn, mean, names="step mean_done null_added")



L3X = Heads(H=1, DH=D, NK=M, HG=1, QB=KD)


def load_l3x(c, sp):
    v = c.dram["ctx_tok"].rearrange("(b m) d -> m b d", b=B)
    c.load_a(sp, c.wa[:, 7168:7680].rearrange("p (b d) -> p b d", b=B), v[0:P])
    c.load_a(sp, c.wa[0:ML, 7680:8192].rearrange("p (b d) -> p b d", b=B), v[P:M])


def layer3_attention(c, load_next):
    a = L3X
    vm, vl = c.wa[:, 7168:7680], c.wa[:, 7680:8192]
    with ExitStack() as ctx:
        kb = c.sb(ctx, "ctx_sixteenth", [P, KD, B * M])
        m = AttentionMemory(c, ctx, a, "_l3")
        s = Sems(c, "keys_scaled")
        with c.nc.Block() as block:
            @block.vector
            def _(dve):
                dve.tensor_scalar(kb[:, :, :], c.ctxT[:, :, :], float(D) ** -0.5, None, ALU.mult).then_inc(s["keys_scaled"], 1)

            @block.tensor
            def _(pe):
                pe.wait_ge(s["keys_scaled"], 1)
                pe.wait_ge(c.wa_loaded, c.wa_count)
        s.close()
        s = Sems(c, ATT + TAIL)
        with c.nc.Block() as block:
            @block.sync
            def _(sp):
                load_next(c, sp)

            attention(c, block, s, a, m, Parts(
                q_pe=None, q_act=None, stage=stage_tile(c, s, a, m, c.xnT), mask=None, project=None,
                keys=lambda i, h, kk: kb[:, kk, at(i, M, 0, M)],
                values=lambda i, h: vm[:, at(i, D, 0, D)],
                left=lambda i, g: vl[0:ML, at(i, D, 0, D)],
                finish_dve=lambda dve, t, p, first: tail_dve(c, dve, s, t, p, first, m.osb[:, :], 6, s["osb_ready"]),
                finish_pool=lambda pool, t, p: tail_pool(c, pool, s, t, p)))
        s.close()



INNER = 704
IB = -(-INNER // P)
IL = INNER - (IB - 1) * P
QMAX = 127.0


def block_rows(m):
    return P if m < IB - 1 else IL


def load_l3f(c, sp):
    w, n = c.wb, IB * D
    for j, src in enumerate((c.dram["L3_ffn_w_gate"], c.dram["L3_ffn_w_up"])):
        full = (IB - 1) * P
        c.load_b(sp, w[:, j * n:j * n + (IB - 1) * D].rearrange("p (k n) -> p k n", k=IB - 1), rows(src[0:full], IB - 1))
        c.load_b(sp, w[0:IL, j * n + (IB - 1) * D:(j + 1) * n], src[full:INNER])
    c.load_b(sp, w[:, 2 * n:2 * n + KD * INNER].rearrange("p (k n) -> p k n", k=KD), rows(c.dram["L3_ffn_w_down"], KD))


def layer3_quantised(c, _load_next):
    n_g = IB * D
    nat = [c.wb[:, 0:n_g].rearrange("p (k n) -> p k n", k=IB), c.wb[:, n_g:2 * n_g].rearrange("p (k n) -> p k n", k=IB),
           c.wb[:, 2 * n_g:2 * n_g + KD * INNER].rearrange("p (k n) -> p k n", k=KD)]
    hv = c.wa[:, :].rearrange("p (m n) -> p m n", n=B * S)
    hx = c.xn[:, :].rearrange("p (m n) -> p m n", n=B * S)

    def hidden(m, cols):
        return hv[0:block_rows(m), m, cols] if m < 4 else hx[0:block_rows(m), m - 4, cols]

    with ExitStack() as ctx:
        xi = c.sb(ctx, "x_whole", [P, KD, B * S], BF16)
        wgu = c.sb(ctx, "gate_up_whole", [P, 2, KD, INNER], BF16)
        wd = c.sb(ctx, "down_whole", [P, IB, D], BF16)
        most = c.sb(ctx, "row_most", [P, 16])
        ws = c.sb(ctx, "row_scales", [P, 16])
        winv = c.sb(ctx, "row_inverses", [P, 16])
        sc = c.sb(ctx, "scales", [P, 12])
        clip = c.sb(ctx, "clips", [P, 2])
        one = c.sb(ctx, "most_one", [1, 2])
        downs = c.sb(ctx, "down_scales_wide", [P, D])
        sx, ix, sh, ih, sig = sc[:, 0:1], sc[:, 1:2], sc[:, 2:3], sc[:, 3:4], sc[:, 4:6]

        with ExitStack() as prep:
            wi = [c.sb(prep, "gate_whole_rows", [P, IB, D], BF16), c.sb(prep, "up_whole_rows", [P, IB, D], BF16),
                  c.sb(prep, "down_whole_rows", [P, KD, INNER], BF16)]
            ib = c.sb(prep, "ident_whole", [P, P], BF16)
            dg = c.sb(prep, "down_diag", [P, KD, P])
            s = Sems(c, "clips_loaded sig_done zeroed ident_copied reduced scaled column_up row_most column_down x_scaled rounded "
                        "whole turned evac gate_dve diag down_wide")
            parts = [(0, P, 0, IB - 1), (0, IL, IB - 1, 1), (1, P, 0, IB - 1), (1, IL, IB - 1, 1), (2, P, 0, KD)]
            with c.nc.Block() as block:
                @block.sync
                def _(sp):
                    sp.dma_start(clip[:, :], c.dram["L3_clips"]).then_inc(s["clips_loaded"], 16)

                @block.gpsimd
                def _(pool):
                    pool.tensor_copy(ib[:, :], c.ident[:, :]).then_inc(s["ident_copied"], 1)

                @block.tensor
                def _(pe):
                    pe.wait_ge(s["reduced"], 1)
                    pe.transpose(c.banks[7][0:1, 0:P], most[:, 14:15], c.ident[:, :]).then_inc(s["column_up"], 1)
                    pe.wait_ge(s["row_most"], 1)
                    pe.matmul(c.banks[7][:, 256:257], c.ones[0:1, :], one[0:1, 0:1], start=True, stop=True).then_inc(s["column_down"], 1)
                    pe.wait_ge(s["diag"], KD)
                    for k in range(KD):
                        mm = pe.matmul(c.banks[6][:, k * P:(k + 1) * P], c.ones[:, :], dg[:, k, :], start=True, stop=True,
                                       skip_group_check=True)
                    mm.then_inc(s["down_wide"], 1)
                    pe.wait_ge(s["ident_copied"], 1)
                    for n in range(4):
                        j, k = n // KD, n % KD
                        pe.wait_ge(s["whole"], 2 * j + 2)
                        if n >= 2:
                            pe.wait_ge(s["evac"], 2 * (n - 1))
                        for m in range(IB):
                            r = block_rows(m)
                            mm = pe.matmul(c.banks[n % 2 * 2 + m // 4][:, m % 4 * P:m % 4 * P + r], wi[j][0:r, m, k * P:(k + 1) * P],
                                           ib[0:r, 0:r], start=True, stop=True, skip_group_check=True)
                        mm.then_inc(s["turned"], 1)
                    pe.wait_ge(s["whole"], 5)
                    for m in range(IB):
                        if m == 0:
                            pe.wait_ge(s["evac"], 8)
                        r = block_rows(m)
                        for k in range(KD):
                            mm = pe.matmul(c.banks[m // 2][0:r, m % 2 * D + k * P:m % 2 * D + (k + 1) * P], wi[2][:, k, m * P:m * P + r],
                                           ib[:, :], start=True, stop=True, skip_group_check=True)
                    mm.then_inc(s["turned"], 1)

                @block.scalar
                def _(act):
                    act.wait_ge(s["clips_loaded"], 16)
                    act.activation(sig, clip[:, :], ACT.Sigmoid).then_inc(s["sig_done"], 1)
                    for n, (j, r, m, k) in enumerate(parts):
                        act.wait_ge(s["rounded"], 2 * (n + 1))
                        act.activation(wi[j][0:r, m:m + k, :], nat[j][0:r, m:m + k, :], ACT.Identity, bias=c.unround[0:r, :]).then_inc(s["whole"], 1)
                    act.wait_ge(s["rounded"], 2 * len(parts) + 2 * 2)
                    for k in range(KD):
                        act.activation(xi[:, k, :], c.xnT[:, k, :], ACT.Identity, bias=c.unround)
                    for n in range(4):
                        act.wait_ge(s["turned"], n + 1)
                        to = wgu[:, n // KD, n % KD, :]
                        act.activation(to[:, 0:512], c.banks[n % 2 * 2][:, :], ACT.Copy).then_inc(s["evac"], 1)
                        act.activation(to[:, 512:INNER], c.banks[n % 2 * 2 + 1][:, 0:INNER - 512], ACT.Copy).then_inc(s["evac"], 1)
                    act.wait_ge(s["turned"], 5)
                    for m in range(IB):
                        r = block_rows(m)
                        act.activation(wd[0:r, m, :], c.banks[m // 2][0:r, m % 2 * D:(m % 2 + 1) * D], ACT.Copy)

                @block.vector
                def _(dve):
                    dve.memset(most[:, :], 1.0).then_inc(s["zeroed"], 1)
                    dve.wait_ge(s["zeroed"], 1)
                    dve.tensor_reduce(most[:, 14:15], c.xn[:, :], AX.X, ALU.max, apply_absolute_value=True).then_inc(s["reduced"], 1)
                    dve.wait_ge(c.wb_loaded, c.wb_count)
                    for j, r, m, k in parts:
                        ins = dve.tensor_reduce(most[0:r, 6 * j + m:6 * j + m + k], nat[j][0:r, m:m + k, :], AX.X, ALU.max,
                                                apply_absolute_value=True)
                        ins.then_inc(s["reduced"], 1)
                    dve.wait_ge(s["reduced"], 1 + len(parts))
                    dve.tensor_scalar(ws[:, :], most[:, :], 1.0 / QMAX, None, ALU.mult).then_inc(s["scaled"], 1)
                    dve.wait_ge(s["scaled"], 1)
                    dve.reciprocal(winv[:, :], ws[:, :]).then_inc(s["scaled"], 1)
                    for k in range(KD):
                        dve.tensor_scalar(dg[:, k, :], c.ident[:, :], ws[:, 12 + k:13 + k], None, ALU.mult).then_inc(s["diag"], 1)
                    dve.wait_ge(s["column_up"], 1)
                    dve.tensor_reduce(one[0:1, 0:1], c.banks[7][0:1, 0:P], AX.X, ALU.max).then_inc(s["row_most"], 1)
                    dve.wait_ge(s["scaled"], 2)
                    done = 0

                    def whole(v, inv):
                        nonlocal done
                        dve.tensor_scalar(v, v, inv, ROUND, ALU.mult, ALU.add).then_inc(s["rounded"], 1)
                        dve.wait_ge(s["rounded"], done + 1)
                        dve.tensor_scalar(v, v, ROUND + QMAX, ROUND - QMAX - 1.0, ALU.min, ALU.max).then_inc(s["rounded"], 1)
                        done += 2

                    for j, r, m, k in parts:
                        v = nat[j][0:r, m:m + k, :]
                        w = winv[0:r, 6 * j + m:6 * j + m + k].unsqueeze(2).broadcast_to(list(v.shape))
                        dve.tensor_tensor(v, v, w, ALU.mult).then_inc(s["x_scaled"], 1)
                        dve.wait_ge(s["x_scaled"], parts.index((j, r, m, k)) + 1)
                        whole(v, 1.0)
                    dve.wait_ge(s["column_down"], 1)
                    dve.wait_ge(s["sig_done"], 1)
                    n = len(parts)
                    dve.scalar_tensor_tensor(out=sx, in0=c.banks[7][:, 256:257], scalar=1.0 / QMAX, in1=sig[:, 0:1],
                                             op0=ALU.mult, op1=ALU.mult).then_inc(s["x_scaled"], 1)
                    dve.wait_ge(s["x_scaled"], n + 1)
                    dve.reciprocal(ix, sx).then_inc(s["x_scaled"], 1)
                    dve.wait_ge(s["x_scaled"], n + 2)
                    for k in range(KD):
                        whole(c.xnT[:, k, :], ix)
                    dve.tensor_scalar(ws[:, 0:12], ws[:, 0:12], sx, None, ALU.mult)
                    dve.wait_ge(s["down_wide"], 1)
                    dve.tensor_copy(downs[:, :], c.banks[6][:, 0:D])
            s.close()

        sg = c.sb(ctx, "silu3", [P, 3, CH])
        hm = c.sb(ctx, "hidden_most", [P, IB * NC])
        hi = c.sb(ctx, "hidden_whole", [P, 2, IB, CH], BF16)
        yb = c.sb(ctx, "scaled_out", [P, 2, D])
        s = Sems(c, "gate_up_ready silu_done h_ready zeroed most_ready column_up row_most column_down scaled gate_pe gate_act gate_dve")
        with c.nc.Block() as block:
            @block.tensor
            def _(pe):
                with pe.Fori(0, NC) as i:
                    for m in range(IB):
                        r, n = block_rows(m), i * IB + m
                        held(pe, s["h_ready"], n + 1, s["gate_pe"])
                        for j in range(2):
                            for k in range(KD):
                                mm = pe.matmul(c.banks[3 * j + m % 3][0:r, :], wgu[:, j, k, m * P:m * P + r],
                                               xi[:, k, bass.ds(i * CH, CH)], start=(k == 0), stop=(k == KD - 1))
                        mm.then_inc(s["gate_up_ready"], 1)
                pe.wait_ge(s["most_ready"], NC + 1)
                pe.transpose(c.banks[7][0:1, 0:P], most[:, 15:16], c.ident[:, :]).then_inc(s["column_up"], 1)
                pe.wait_ge(s["row_most"], 1)
                pe.matmul(c.banks[7][:, 256:257], c.ones[0:1, :], one[0:1, 1:2], start=True, stop=True).then_inc(s["column_down"], 1)

            @block.scalar
            def _(act):
                with act.Fori(0, NC) as i:
                    for m in range(IB):
                        r, n = block_rows(m), i * IB + m
                        held(act, s["h_ready"], n + 1, s["gate_act"])
                        act.wait_ge(s["gate_up_ready"], n + 1)
                        act.activation(sg[0:r, m % 3, :], c.banks[m % 3][0:r, :], ACT.Silu, scale=ws[0:r, m:m + 1]).then_inc(s["silu_done"], 1)

            @block.vector
            def _(dve):
                dve.memset(hm[:, :], 0.0).then_inc(s["zeroed"], 1)
                dve.wait_ge(s["zeroed"], 1)
                dve.sem_inc(s["h_ready"], 3)
                with dve.Fori(0, NC) as i:
                    for m in range(IB):
                        r, n = block_rows(m), i * IB + m
                        held(dve, s["silu_done"], n + 1, s["gate_dve"])
                        dve.scalar_tensor_tensor(out=hidden(m, bass.ds(i * CH, CH)), in0=c.banks[3 + m % 3][0:r, :],
                                                 scalar=ws[0:r, 6 + m:7 + m], in1=sg[0:r, m % 3, :],
                                                 op0=ALU.mult, op1=ALU.mult).then_inc(s["h_ready"], 1)
                    held(dve, s["h_ready"], (i + 1) * IB + 3, s["gate_dve"])
                    for v, at, r in ((hv[:, :, bass.ds(i * CH, CH)], 0, P), (hx[:, 0:1, bass.ds(i * CH, CH)], 4, P),
                                     (hx[0:IL, 1:2, bass.ds(i * CH, CH)], 5, IL)):
                        n = v.shape[1]
                        ins = dve.tensor_reduce(hm[0:r, bass.ds(i * IB + at, n)], v, AX.X, ALU.max, apply_absolute_value=True)
                    ins.then_inc(s["most_ready"], 1)
                dve.wait_ge(s["most_ready"], NC)
                dve.tensor_reduce(most[:, 15:16], hm[:, :], AX.X, ALU.max).then_inc(s["most_ready"], 1)
                dve.wait_ge(s["column_up"], 1)
                dve.tensor_reduce(one[0:1, 1:2], c.banks[7][0:1, 0:P], AX.X, ALU.max).then_inc(s["row_most"], 1)
                dve.wait_ge(s["column_down"], 1)
                dve.scalar_tensor_tensor(out=sh, in0=c.banks[7][:, 256:257], scalar=1.0 / QMAX, in1=sig[:, 1:2],
                                         op0=ALU.mult, op1=ALU.mult).then_inc(s["scaled"], 1)
                dve.wait_ge(s["scaled"], 1)
                dve.reciprocal(ih, sh).then_inc(s["scaled"], 1)
                dve.tensor_scalar(downs[:, :], downs[:, :], sh, c.tg[:, 7:8], ALU.mult, ALU.mult).then_inc(s["scaled"], 1)
        s.close()

        s = Sems(c, "clipped whole downed scaled_y stored x_done gate_pe gate_act gate_dve")
        with c.nc.Block() as block:
            @block.sync
            def _(sp):
                for i in range(NC):
                    sp.wait_ge(s["x_done"], 4 * (i + 1))
                    sp.dma_start(c.out[:, 4 * i:4 * i + 4, :], c.x[:, 4 * i * D:(4 * i + 4) * D].rearrange("p (t d) -> p t d", d=D)).then_inc(s["stored"], 16)
                sp.wait_ge(s["stored"], 16 * NC)

            def both(i):
                cols = slice(i * CH, (i + 1) * CH)
                return ((hv[:, :, cols], 0, 4), (hx[:, :, cols], 4, 6))

            @block.vector
            def _(dve):
                def whole(i):
                    for q, (v, lo, hi_) in enumerate(both(i)):
                        dve.tensor_scalar(v, v, ih, ROUND, ALU.mult, ALU.add).then_inc(s["clipped"], 1)
                        dve.wait_ge(s["clipped"], 4 * i + 2 * q + 1)
                        dve.tensor_scalar(v, v, ROUND + QMAX, ROUND - QMAX - 1.0, ALU.min, ALU.max).then_inc(s["clipped"], 1)

                whole(0)
                for i in range(NC):
                    if i + 1 < NC:
                        whole(i + 1)
                    for tt in range(4):
                        t = 4 * i + tt
                        dve.wait_ge(s["downed"], t + 1)
                        dve.tensor_tensor(yb[:, t % 2, :], c.banks[t % 8][:, 0:D], downs[:, :], ALU.mult).then_inc(s["scaled_y"], 1)
                        dve.wait_ge(s["scaled_y"], t + 1)
                        dve.tensor_tensor(tok(c.x, t), tok(c.x, t), yb[:, t % 2, :], ALU.add).then_inc(s["x_done"], 1)

            @block.scalar
            def _(act):
                for i in range(NC):
                    act.wait_ge(s["clipped"], 4 * (i + 1))
                    if i >= 2:
                        act.wait_ge(s["downed"], 4 * (i - 1))
                    for v, lo, hi_ in both(i):
                        act.activation(hi[:, i % 2, lo:hi_, :], v, ACT.Identity, bias=c.unround).then_inc(s["whole"], 1)

            @block.tensor
            def _(pe):
                for i in range(NC):
                    pe.wait_ge(s["whole"], 2 * (i + 1))
                    for tt in range(4):
                        t = 4 * i + tt
                        if t >= 8:
                            pe.wait_ge(s["scaled_y"], t - 7)
                        for m in range(IB):
                            r = block_rows(m)
                            mm = pe.matmul(c.banks[t % 8][:, 0:D], hi[0:r, i % 2, m, tt * P:(tt + 1) * P], wd[0:r, m, :],
                                           start=(m == 0), stop=(m == IB - 1))
                        mm.then_inc(s["downed"], 1)
        s.close()



def program(nc, dram, out):
    with ExitStack() as ctx:
        c = Core(nc, ctx, dram)
        c.sorted_x, c.sorted_y = (nc.dram_tensor(n, (SLOTS * SG, D), F32, kind="Internal").ap() for n in ("sorted_x", "sorted_y"))
        c.out = out.rearrange("b (t p) d -> p (b t) d", p=P)
        phase_setup(c)
        layers = [(layer0_attention, load_l0x), (layer0_experts, load_l0f), (layer1_slots, load_l1x), (layer1_experts, load_l1f),
                  (layer2_attention, load_l2x), (layer2_routed, load_l2f), (layer3_attention, load_l3x), (layer3_quantised, load_l3f)]
        for n, (layer, _load) in enumerate(layers):
            if layer in (layer0_experts, layer1_slots, layer2_routed, layer3_quantised):
                transpose_xn(c)
            layer(c, layers[n + 1][1] if n + 1 < len(layers) else None)


def col(v):
    return np.ascontiguousarray(v.reshape(-1, P).T)


def layouts(i):
    f = np.float32
    p = np.arange(P)
    consts = {
        "centre16": np.eye(P, dtype=f) - (p[:, None] // 16 == p[None, :] // 16).astype(f) / f(16),
        "average16": (p[:, None] // 16 == p[None, :] // 16).astype(f) / f(16),
        "heads16": (p[:, None] // 16 == np.arange(8)[None, :]).astype(f) * f(0.25),
        "heads64": (p[:, None] // 64 == np.arange(2)[None, :]).astype(f) * f(0.125),
        "left16": (p[:, None] // 26 == np.arange(64)[None, :] // 16).astype(f),
        "left64": (p[:, None] // 26 == np.arange(256)[None, :] // 64).astype(f),
        "mean256": np.full((P, P), 1 / 256, f),
        "ln1g": col(i["L1_ffn_ln1_g"]), "ln1b": col(i["L1_ffn_ln1_b"]),
        "ln2g": col(i["L1_ffn_ln2_g"]), "ln2b": col(i["L1_ffn_ln2_b"]),
        "slotw": col(i["L1_xattn_slot_norm_w"]), "inw": col(i["L1_xattn_input_norm_w"]),
        "bih": col(i["L1_xattn_gru_bih"]), "bhh": col(i["L1_xattn_gru_bhh"]),
        "counting": np.broadcast_to(np.arange(NQ, dtype=f), (P, NQ)),
        "places": np.stack([p, p + P], 1),
        "before": p[:, None] < p[None, :],
        "diag8": (p[:, None] == np.arange(RC)[None, :] // RD),
        "query_rows": (p[:, None] % 8 < 4), "key_rows": (p[:, None] % 8 >= 4),
        "falling": np.broadcast_to(32 - np.arange(16, dtype=f), (P, 16)),
        "pairs16": (p[:, None] == np.arange(N_R * MID_R)[None, :] // MID_R).astype(f),
        "bq0": col(i["L0_xattn_bq"])[:, 0:1], "bq1": col(i["L0_xattn_bq"])[:, 1:2],
        "bk0": col(i["L0_xattn_bkv"])[:, 0:1], "bk1": col(i["L0_xattn_bkv"])[:, 1:2],
        "qgam": np.tile(i["L0_xattn_q_gamma"], 8)[:, None], "qbet": np.tile(i["L0_xattn_q_beta"], 8)[:, None],
        "kgam": np.tile(i["L0_xattn_k_gamma"], 8)[:, None], "kbet": np.tile(i["L0_xattn_k_beta"], 8)[:, None],
    }
    vrows = {
        "bv": i["L0_xattn_bkv"][D:], "L0_xattn_bproj": i["L0_xattn_bproj"],
        "L2_xattn_b_out": i["L2_xattn_b_out"],
    }
    a = {
        "x": i["x"].reshape(B * S, D),
        "ctxT": i["ctx_1024"].transpose(2, 0, 1).reshape(D, B * M),
        "ctx_tok": i["ctx_1024"].reshape(B * M, D),
        "L3_ffn_w_gate": i["L3_ffn_w_gate"], "L3_ffn_w_up": i["L3_ffn_w_up"], "L3_ffn_w_down": i["L3_ffn_w_down"],
        "L3_clips": np.broadcast_to(np.stack([i["L3_ffn_clip_x"], i["L3_ffn_clip_down"]], 1), (P, 2)),
        "ident": np.eye(P, dtype=f),
        "gates": np.broadcast_to(np.stack([i["g_xattn"], i["g_ffn"]], 1).reshape(1, 8), (P, 8)),
        "L0_xattn_Wq": i["L0_xattn_Wq"], "L0_xattn_Wkv": i["L0_xattn_Wkv"],
        "L0_WvT": i["L0_xattn_Wkv"][D:].T, "L0_WprojT": i["L0_xattn_Wproj"].T,
    }
    wide = lambda r, sh: np.concatenate([r.transpose(1, 0, 2).reshape(D, -1), sh.transpose(1, 0, 2).reshape(D, -1)], 1)
    a["L0_gates"] = wide(i["L0_ffn_wg_r"], i["L0_ffn_wg_s"])
    a["L0_ups"] = wide(i["L0_ffn_wu_r"], i["L0_ffn_wu_s"])
    a["L0_downs"] = np.concatenate([i["L0_ffn_wd_r"].reshape(-1, D), i["L0_ffn_wd_s"].reshape(-1, D)], 0)
    a["L0_ffn_router_w"] = i["L0_ffn_router_w"]
    a["L1_xattn_Wq"] = i["L1_xattn_Wq"]
    a["L1_WkT"], a["L1_WvT"] = i["L1_xattn_Wk"].T, i["L1_xattn_Wv"].T
    a["L1_wihT"], a["L1_whhT"] = i["L1_xattn_gru_wih"].T, i["L1_xattn_gru_whh"].T
    a["L1_attnT"], a["L1_gateT"] = i["L1_ffn_attn_w"].T, i["L1_ffn_gate_w"].T
    side = lambda w: w.reshape(N_E, -1, P, w.shape[2]).transpose(0, 2, 1, 3).reshape(N_E, P, -1)
    a["L1_experts"] = np.concatenate([side(i["L1_ffn_gate_proj"].transpose(0, 2, 1)), side(i["L1_ffn_up_proj"].transpose(0, 2, 1)),
                                      side(i["L1_ffn_down_proj"].transpose(0, 2, 1))], 2).reshape(N_E * P, EXPERT)
    a["mask"] = np.broadcast_to(i["mask_BxS2_bf1"].view(np.uint8).reshape(1, B * M), (P, B * M))
    a["L2_WqT"], a["L2_WkT"], a["L2_WvT"] = i["L2_xattn_Wq"].T, i["L2_xattn_Wkv"][:1024].T, i["L2_xattn_Wkv"][1024:].T
    a["L2_WoutT"] = i["L2_xattn_Wout"].T
    rt = np.concatenate([i["L2_ffn_w_qr"], i["L2_ffn_w_kvr"]], 0).T
    none = np.zeros_like(rt)
    a["L2_routing"] = np.stack([np.concatenate([rt, none], 1), np.concatenate([none, rt], 1)], 1)
    side4 = lambda w: w.reshape(GATES, -1, P, w.shape[2]).transpose(0, 2, 1, 3).reshape(GATES, P, -1)
    a["L2_gates"] = np.concatenate([side4(i["L2_ffn_w_q"].transpose(0, 2, 1)), side4(i["L2_ffn_w_kv"].transpose(0, 2, 1)),
                                    side4(i["L2_ffn_w_out"].transpose(0, 2, 1))], 2)
    a["L2_null_k"] = i["L2_ffn_null_kv"][0].reshape(GATES * 4, P).T
    a["L2_null_v"] = np.broadcast_to(i["L2_ffn_null_kv"][1].reshape(1, GATES * RC), (RH, GATES * RC))
    a["L2_null_token"] = np.broadcast_to(i["L2_ffn_null_token"].reshape(1, D), (P, D))
    const_at, vrow_at, n = {}, {}, 0
    for k, v in consts.items():
        const_at[k] = (n, v.shape[1])
        n += v.shape[1]
    a["consts"] = np.concatenate([v.astype(f) for v in consts.values()], 1)
    n = 0
    for k, v in vrows.items():
        vrow_at[k] = (n, v.size)
        n += v.size
    a["vrows"] = np.concatenate([v.reshape(1, -1) for v in vrows.values()], 1)
    return {k: np.ascontiguousarray(v) for k, v in a.items()}, const_at, vrow_at


def kernel(**inputs):
    import concourse.bacc as bacc
    from concourse.bass_utils import run_bass_kernel_spmd

    arrays, const_at, vrow_at = layouts({k: np.asarray(v) for k, v in inputs.items()})
    nc = bacc.Bacc("TRN2", target_bir_lowering=False, num_devices=1)
    dram = {"const_at": const_at, "vrow_at": vrow_at}
    for name, v in arrays.items():
        dram[name] = nc.dram_tensor(f"in_{name}", v.shape, mybir.dt.from_np(v.dtype), kind="ExternalInput").ap()
    out = nc.dram_tensor("out_x", (B, S, D), F32, kind="ExternalOutput").ap()
    program(nc, dram, out)
    r = run_bass_kernel_spmd(nc, [{f"in_{k}": v for k, v in arrays.items()}], core_ids=[0])
    return r.results[0]["out_x"]
```
